# Optimizing a Trainium2 kernel written in Bass

```python
import numpy as np
import jax
import jax.numpy as jnp

def _softmax(x, axis=-1):
    return jax.nn.softmax(x, axis=axis)

def _gelu(x):
    return jax.nn.gelu(x, approximate=True)

def _silu(x):
    return jax.nn.silu(x)

def _sigmoid(x):
    return jax.nn.sigmoid(x)

def _layernorm(x, axis=-1, eps=1e-05):
    m = jnp.mean(x, axis=axis, keepdims=True)
    v = jnp.var(x, axis=axis, keepdims=True)
    return (x - m) / jnp.sqrt(v + eps)

def _scatter_add(tgt, idx, src, axis=0):
    return tgt.at[idx].add(src)

def _segment_sum(src, seg, n):
    return jax.ops.segment_sum(src, seg, n)
kernel_name = 'mk_seq_postln_d1_jaxref_r8_e3c83c'

def setup_inputs(seed: int=0):
    np.random.seed(seed)
    _w = jnp.asarray

    def _L0_attn_setup():
        import jax, jax.numpy as jnp
        import numpy as np
        from jax.scipy.linalg import solve_triangular
        H = 256
        NK = 16
        NV = 32
        DK = 128
        DV = 128
        KCONV = 4
        CHUNK = 64
        EPS = 1e-06
        KD = NK * DK
        VD = NV * DV
        CONV_DIM = 2 * KD + VD

        def _l2norm(x, eps=1e-06):
            return x * jax.lax.rsqrt(jnp.sum(x * x, axis=-1, keepdims=True) + eps)

        def _chunk_gated_delta_rule(q, k, v, g, beta):
            B, S, Hh, _ = q.shape
            q = _l2norm(q)
            k = _l2norm(k)
            q = q.transpose(0, 2, 1, 3).astype(jnp.float32) * DK ** (-0.5)
            k = k.transpose(0, 2, 1, 3).astype(jnp.float32)
            v = v.transpose(0, 2, 1, 3).astype(jnp.float32)
            g = g.transpose(0, 2, 1).astype(jnp.float32)
            beta = beta.transpose(0, 2, 1).astype(jnp.float32)
            N = S // CHUNK
            ch = lambda x: x.reshape(B, Hh, N, CHUNK, x.shape[-1])
            q, k, v = (ch(q), ch(k), ch(v))
            g = g.reshape(B, Hh, N, CHUNK)
            beta = beta.reshape(B, Hh, N, CHUNK)
            v_beta = v * beta[..., None]
            k_beta = k * beta[..., None]
            g = jnp.cumsum(g, axis=-1)
            dg = g[..., :, None] - g[..., None, :]
            decay = jnp.tril(jnp.exp(jnp.tril(dg)))
            M = -jnp.tril(jnp.einsum('bhnik,bhnjk->bhnij', k_beta, k) * decay, k=-1)
            eye = jnp.eye(CHUNK, dtype=jnp.float32)
            T = solve_triangular(eye - M, jnp.broadcast_to(eye, M.shape), lower=True)
            v_new = jnp.einsum('bhnij,bhnjd->bhnid', T, v_beta)
            k_cumdecay = jnp.einsum('bhnij,bhnjd->bhnid', T, k_beta * jnp.exp(g)[..., None])
            lower_incl = jnp.tril(jnp.ones((CHUNK, CHUNK), bool))

            def step(state, inp):
                q_i, k_i, v_i, kcd_i, g_i, dm_i = inp
                attn = jnp.where(lower_incl, jnp.einsum('bhik,bhjk->bhij', q_i, k_i) * dm_i, 0.0)
                v_prime = jnp.einsum('bhik,bhkv->bhiv', kcd_i, state)
                vn = v_i - v_prime
                inter = jnp.einsum('bhik,bhkv->bhiv', q_i * jnp.exp(g_i)[..., None], state)
                out = inter + jnp.einsum('bhij,bhjv->bhiv', attn, vn)
                g_last = g_i[..., -1]
                state = state * jnp.exp(g_last)[..., None, None] + jnp.einsum('bhck,bhcv->bhkv', k_i * jnp.exp(g_last[..., None] - g_i)[..., None], vn)
                return (state, out)
            xs = tuple((jnp.moveaxis(x, 2, 0) for x in (q, k, v_new, k_cumdecay, g, decay)))
            state0 = jnp.zeros((B, Hh, DK, DV), jnp.float32)
            _, outs = jax.lax.scan(step, state0, xs)
            out = jnp.moveaxis(outs, 0, 2).reshape(B, Hh, S, DV)
            return out.transpose(0, 2, 1, 3)
        key = jax.random.key(seed)
        ks = jax.random.split(key, 8)
        B, S = (2, 256)
        return {'hidden_states': jax.random.normal(ks[0], (B, S, H), jnp.float32), 'W_qkvz': jax.random.normal(ks[1], (H, 2 * KD + 2 * VD), jnp.float32) * 0.02, 'W_ba': jax.random.normal(ks[2], (H, 2 * NV), jnp.float32) * 0.02, 'conv_weight': jax.random.normal(ks[3], (CONV_DIM, KCONV), jnp.float32) * 0.1, 'A_log': jax.random.normal(ks[4], (NV,), jnp.float32) * 0.1, 'dt_bias': jax.random.normal(ks[5], (NV,), jnp.float32) * 0.1, 'norm_weight': jnp.ones((DV,), jnp.float32), 'W_out': jax.random.normal(ks[6], (VD, H), jnp.float32) * 0.02}
    _L0_attn_in = _L0_attn_setup()

    def _L0_ffn_setup():
        import jax, jax.numpy as jnp
        import numpy as np
        D_MODEL = 256
        D_EXPERT = 1024
        EPS = 1e-08

        def ternary_quant(w):
            scale = jnp.mean(jnp.abs(w)) + EPS
            q = jnp.clip(jnp.round(w / scale), -1.0, 1.0) * scale
            return w + jax.lax.stop_gradient(q - w)
        key = jax.random.key(seed)
        k_x, k_up, k_gate, k_down = jax.random.split(key, 4)
        std_in = 1.0 / np.sqrt(D_MODEL)
        std_exp = 1.0 / np.sqrt(D_EXPERT)
        return {'x': jax.random.normal(k_x, (4, 256, D_MODEL), dtype=jnp.float32), 'W_up': jax.random.normal(k_up, (D_EXPERT, D_MODEL), dtype=jnp.float32) * std_in, 'W_gate': jax.random.normal(k_gate, (D_EXPERT, D_MODEL), dtype=jnp.float32) * std_in, 'W_down': jax.random.normal(k_down, (D_MODEL, D_EXPERT), dtype=jnp.float32) * std_exp}
    _L0_ffn_in = _L0_ffn_setup()
    _d = {'L0_attn_hidden_states': _L0_attn_in['hidden_states'], 'L0_attn_W_qkvz': _L0_attn_in['W_qkvz'], 'L0_attn_W_ba': _L0_attn_in['W_ba'], 'L0_attn_conv_weight': _L0_attn_in['conv_weight'], 'L0_attn_A_log': _L0_attn_in['A_log'], 'L0_attn_dt_bias': _L0_attn_in['dt_bias'], 'L0_attn_norm_weight': _L0_attn_in['norm_weight'], 'L0_attn_W_out': _L0_attn_in['W_out'], 'L0_ffn_W_up': _L0_ffn_in['W_up'], 'L0_ffn_W_gate': _L0_ffn_in['W_gate'], 'L0_ffn_W_down': _L0_ffn_in['W_down']}
    _x0 = _d['L0_attn_hidden_states']
    _d['L0_attn_hidden_states'] = jax.random.normal(jax.random.fold_in(jax.random.key(seed), 1), (8, 512, 256), dtype=_x0.dtype)
    del _x0
    return _d

def reference(L0_attn_hidden_states, L0_attn_W_qkvz, L0_attn_W_ba, L0_attn_conv_weight, L0_attn_A_log, L0_attn_dt_bias, L0_attn_norm_weight, L0_attn_W_out, L0_ffn_W_up, L0_ffn_W_gate, L0_ffn_W_down):

    def _L0_attn_ref(hidden_states, W_qkvz, W_ba, conv_weight, A_log, dt_bias, norm_weight, W_out):
        import jax, jax.numpy as jnp
        import numpy as np
        from jax.scipy.linalg import solve_triangular
        H = 256
        NK = 16
        NV = 32
        DK = 128
        DV = 128
        KCONV = 4
        CHUNK = 64
        EPS = 1e-06
        KD = NK * DK
        VD = NV * DV
        CONV_DIM = 2 * KD + VD

        def _l2norm(x, eps=1e-06):
            return x * jax.lax.rsqrt(jnp.sum(x * x, axis=-1, keepdims=True) + eps)

        def _chunk_gated_delta_rule(q, k, v, g, beta):
            B, S, Hh, _ = q.shape
            q = _l2norm(q)
            k = _l2norm(k)
            q = q.transpose(0, 2, 1, 3).astype(jnp.float32) * DK ** (-0.5)
            k = k.transpose(0, 2, 1, 3).astype(jnp.float32)
            v = v.transpose(0, 2, 1, 3).astype(jnp.float32)
            g = g.transpose(0, 2, 1).astype(jnp.float32)
            beta = beta.transpose(0, 2, 1).astype(jnp.float32)
            N = S // CHUNK
            ch = lambda x: x.reshape(B, Hh, N, CHUNK, x.shape[-1])
            q, k, v = (ch(q), ch(k), ch(v))
            g = g.reshape(B, Hh, N, CHUNK)
            beta = beta.reshape(B, Hh, N, CHUNK)
            v_beta = v * beta[..., None]
            k_beta = k * beta[..., None]
            g = jnp.cumsum(g, axis=-1)
            dg = g[..., :, None] - g[..., None, :]
            decay = jnp.tril(jnp.exp(jnp.tril(dg)))
            M = -jnp.tril(jnp.einsum('bhnik,bhnjk->bhnij', k_beta, k) * decay, k=-1)
            eye = jnp.eye(CHUNK, dtype=jnp.float32)
            T = solve_triangular(eye - M, jnp.broadcast_to(eye, M.shape), lower=True)
            v_new = jnp.einsum('bhnij,bhnjd->bhnid', T, v_beta)
            k_cumdecay = jnp.einsum('bhnij,bhnjd->bhnid', T, k_beta * jnp.exp(g)[..., None])
            lower_incl = jnp.tril(jnp.ones((CHUNK, CHUNK), bool))

            def step(state, inp):
                q_i, k_i, v_i, kcd_i, g_i, dm_i = inp
                attn = jnp.where(lower_incl, jnp.einsum('bhik,bhjk->bhij', q_i, k_i) * dm_i, 0.0)
                v_prime = jnp.einsum('bhik,bhkv->bhiv', kcd_i, state)
                vn = v_i - v_prime
                inter = jnp.einsum('bhik,bhkv->bhiv', q_i * jnp.exp(g_i)[..., None], state)
                out = inter + jnp.einsum('bhij,bhjv->bhiv', attn, vn)
                g_last = g_i[..., -1]
                state = state * jnp.exp(g_last)[..., None, None] + jnp.einsum('bhck,bhcv->bhkv', k_i * jnp.exp(g_last[..., None] - g_i)[..., None], vn)
                return (state, out)
            xs = tuple((jnp.moveaxis(x, 2, 0) for x in (q, k, v_new, k_cumdecay, g, decay)))
            state0 = jnp.zeros((B, Hh, DK, DV), jnp.float32)
            _, outs = jax.lax.scan(step, state0, xs)
            out = jnp.moveaxis(outs, 0, 2).reshape(B, Hh, S, DV)
            return out.transpose(0, 2, 1, 3)
        B, S, _ = hidden_states.shape
        R = NV // NK
        qkvz = (hidden_states @ W_qkvz).reshape(B, S, NK, 2 * DK + 2 * R * DV)
        ba = (hidden_states @ W_ba).reshape(B, S, NK, 2 * R)
        q = qkvz[..., :DK]
        k = qkvz[..., DK:2 * DK]
        v = qkvz[..., 2 * DK:2 * DK + R * DV].reshape(B, S, NV, DV)
        z = qkvz[..., 2 * DK + R * DV:].reshape(B, S, NV, DV)
        b = ba[..., :R].reshape(B, S, NV)
        a = ba[..., R:].reshape(B, S, NV)
        mixed = jnp.concatenate([q.reshape(B, S, -1), k.reshape(B, S, -1), v.reshape(B, S, -1)], -1)
        xp = jnp.pad(mixed, ((0, 0), (KCONV - 1, 0), (0, 0)))
        conv = sum((xp[:, j:j + S, :] * conv_weight[:, j] for j in range(KCONV)))
        mixed = jax.nn.silu(conv)
        q = mixed[..., :KD].reshape(B, S, NK, DK)
        k = mixed[..., KD:2 * KD].reshape(B, S, NK, DK)
        v = mixed[..., 2 * KD:].reshape(B, S, NV, DV)
        beta = jax.nn.sigmoid(b)
        g = -jnp.exp(A_log) * jax.nn.softplus(a + dt_bias)
        q = jnp.repeat(q, R, axis=2)
        k = jnp.repeat(k, R, axis=2)
        core = _chunk_gated_delta_rule(q, k, v, g, beta)
        x = core * jax.nn.silu(z.astype(jnp.float32))
        x = x * jax.lax.rsqrt(jnp.mean(x * x, axis=-1, keepdims=True) + EPS) * norm_weight
        return x.reshape(B, S, VD) @ W_out

    def _L0_ffn_ref(x, W_up, W_gate, W_down):
        import jax, jax.numpy as jnp
        import numpy as np
        D_MODEL = 256
        D_EXPERT = 1024
        EPS = 1e-08

        def ternary_quant(w):
            scale = jnp.mean(jnp.abs(w)) + EPS
            q = jnp.clip(jnp.round(w / scale), -1.0, 1.0) * scale
            return w + jax.lax.stop_gradient(q - w)
        wu = ternary_quant(W_up)
        wg = ternary_quant(W_gate)
        wd = ternary_quant(W_down)
        up = jnp.einsum('bsd,ed->bse', x, wu)
        gate = jnp.einsum('bsd,ed->bse', x, wg)
        hidden = jax.nn.silu(up) * gate
        return jnp.einsum('bse,de->bsd', hidden, wd)
    x = L0_attn_hidden_states
    x = _layernorm(x + _L0_attn_ref(x, L0_attn_W_qkvz, L0_attn_W_ba, L0_attn_conv_weight, L0_attn_A_log, L0_attn_dt_bias, L0_attn_norm_weight, L0_attn_W_out), axis=-1)
    x = _layernorm(x + _L0_ffn_ref(x, L0_ffn_W_up, L0_ffn_W_gate, L0_ffn_W_down), axis=-1)
    return x

_drawn_inputs = setup_inputs


def setup_inputs(seed=0):
    import zlib

    import numpy as np

    out = dict(_drawn_inputs(seed))
    spreads = {'L0_attn_norm_weight': (1.0, 0.6)}
    factors = {'L0_attn_W_ba': 8.0, 'L0_attn_A_log': 31.233, 'L0_attn_dt_bias': 41.586}
    for name, (base, spread) in spreads.items():
        noise = np.random.default_rng([zlib.crc32(name.encode()), seed]).standard_normal(out[name].shape)
        drawn = base * np.exp(spread * noise) if base else spread * noise
        out[name] = jnp.asarray(drawn.astype(out[name].dtype))
    for name, factor in factors.items():
        out[name] = (out[name] * factor).astype(out[name].dtype)
    return out
```

```python
import numpy as np
import concourse.bass as bass
from concourse import mybir
from contextlib import ExitStack

B, S, H = 8, 512, 256
NK, R, D = 16, 2, 128
NV = NK * R
KT = H // 128
C = 128
NC = S // C
NB = B * NC
NU = NC * R
TAPS = 4
WCOL = 2 * D + 2 * R * D
ITS = NK * B
LEVELS = 6
E = 1024
ET = E // 128
ESC = 256.0
KINDS = 3
SMALL = NC * KINDS * R
EPS, LN_EPS, TERN_EPS = 1e-6, 1e-5, 1e-8

f32, f16, bf16, u16 = mybir.dt.float32, mybir.dt.float16, mybir.dt.bfloat16, mybir.dt.uint16
ALU, ACT, AX = mybir.AluOpType, mybir.ActivationFunctionType, mybir.AxisListType
ds = bass.ds


class Signal:

    def __init__(self, nc, ctx, name, per=1):
        self.sem, self.per = ctx.enter_context(nc.semaphore(name)), per

    def wait(self, engine, it, n):
        if isinstance(it, int) and it < 0:
            return
        engine.wait_ge(self.sem, it * self.per + n)


def build(nc, io):
    with ExitStack() as ctx:
        def sb(name, shape, dt=f32):
            return ctx.enter_context(nc.sbuf_tensor(name, shape, dt))
        m = {
            "yacc": sb("yacc", [128, NB, H]),
            "ident": sb("ident", [128, 128]),
        }
        with ExitStack() as attention:
            def sa(name, shape, dt=f32):
                return attention.enter_context(nc.sbuf_tensor(name, shape, dt))
            m["wout"] = sa("wout", [128, NV, H])
            m["vec"] = sa("vec", [128, ITS, SMALL])
            m["cw"] = sa("cw", [128, NK, 4 * TAPS])
            m["rows_dram"] = nc.dram_tensor("rows_scratch", (ITS, 2, 3, R, S), bf16, kind="Internal").ap()
            gates(nc, io, m)
            delta_rule(nc, io, m)
        feed_forward(nc, io, m)


def gates(nc, io, m):
    yacc, ident, wout, vec, cw, rows_dram = (m[k] for k in ("yacc", "ident", "wout", "vec", "cw", "rows_dram"))
    with ExitStack() as ctx:
        def sb(name, shape, dt=f32):
            return ctx.enter_context(nc.sbuf_tensor(name, shape, dt))

        def signal(name, per=1):
            return Signal(nc, ctx, name, per)
        wba = sb("wba", [128, KT, 2 * NV])
        xb = sb("gxb", [128, KT, S])
        nwt = sb("nwt", [128, 1])
        na = sb("na", [128, NV])
        dtb = sb("dtb", [128, NV])
        triu = sb("triu", [128, 128])
        ones = sb("ones", [128, 128])
        identb = sb("gidentb", [128, 128], bf16)
        ba = sb("ba", [128, NB, 2, NV])
        e = sb("ge", [128, NB, 2, NV])
        s = sb("gs", [128, NB, 2, NV])
        s2 = sb("gs2", [128, NB, 2, NV])
        p = sb("gp", [128, NB, 2, NV])
        sp_ = sb("gsoft", [128, NB, 2, NV])
        graw = sb("graw", [128, NB, NV])
        gs = sb("gcum", [128, NB, NV])
        gl = sb("glast", [128, NB, NV])
        hj = sb("ghj", [128, NB, NV])
        dl = sb("gdl", [128, NB, NV])
        r1 = sb("gr1", [128, NB, NV])
        parts = sb("parts", [128, NB, 2, 3, NV], bf16)
        rows = sb("rows", [3 * NV, 2, NB * C], bf16)
        pz = ctx.enter_context(nc.psum_tensor("pz", [128, 512], f32))
        pg = [ctx.enter_context(nc.psum_tensor(f"pg{i}", [128, 512], f32)) for i in range(4)]
        pt = [ctx.enter_context(nc.psum_tensor(f"pt{i}", [128, 1024], bf16)) for i in range(2)]

        consts_in, x_in = signal("g_consts_in", 16), signal("g_x_in", 16)
        made_ones, made_identb = signal("g_ones"), signal("g_identb")
        ba_mm, ba_out, x_ready, abs_ready, exp_a, exp_abs = (signal(f"g_{n}") for n in ("ba_mm", "ba_out", "x", "abs", "expa", "expabs"))
        graw_ready, cum_mm, cum_out, dl_ready, parts_ready = (signal(f"g_{n}") for n in ("graw", "cum_mm", "cum_out", "dl", "parts"))
        turn_mm, turn_out, rows_out, chain = signal("g_turn_mm"), signal("g_turn_out"), signal("g_rows_out", 16), signal("g_chain")
        NTURN = 2 * NB // 4
        block = ctx.enter_context(nc.Block())
        loads = [
            (wba[:, :, :], io["Wba"].rearrange("(k p) n -> p k n", p=128)),
            (dtb[:, :], io["dt_bias"].rearrange("(a n) -> a n", a=1).broadcast_to([128, NV])),
            (na[:, :], io["A_log"].rearrange("(a n) -> a n", a=1).broadcast_to([128, NV])),
            (nwt[:, :], io["norm_weight"].rearrange("(p a) -> p a", a=1)),
            (triu[:, :], io["triu"]),
            (ident[:, :], io["ident"]),
            (cw[:, :, :], io["convw"]),
            (wout[:, :, :], io["W_out"].rearrange("(h p) n -> p h n", p=128)),
            (yacc[:, 0:NB // 2, :], io["x_tok"].rearrange("(n p) h -> p n h", p=128)[:, 0:NB // 2, :]),
            (yacc[:, NB // 2:NB, :], io["x_tok"].rearrange("(n p) h -> p n h", p=128)[:, NB // 2:NB, :]),
        ]
        LOADED = 16 * len(loads)

        @block.sync
        def _(sp):
            for dst, src in loads:
                sp.dma_start(dst, src).then_inc(consts_in.sem, 16)
            sp.dma_start(xb[:, :, :], io["xT"][0].rearrange("k p n -> p k n")).then_inc(x_in.sem, 16)
            with sp.Fori(1, B) as b:
                ba_mm.wait(sp, b, 0)
                sp.dma_start(xb[:, :, :], io["xT"][ds(b, 1), :, :, :].rearrange("a k p n -> p (a k) n")).then_inc(x_in.sem, 16)
            sp.wait_ge(turn_out.sem, NTURN)
            dst = rows_dram.rearrange("(k b) w q h s -> w q k h b s", b=B)
            for w in range(2):
                for q in range(3):
                    for k in range(NK):
                        sp.dma_start(dst[w, q, k], rows[q * NV + k * R:q * NV + (k + 1) * R, w, :]
                                     .rearrange("h (b s) -> h b s", b=B)).then_inc(rows_out.sem, 16)
            sp.wait_ge(rows_out.sem, 6 * NK * 16)

        @block.tensor
        def _(pe):
            pe.wait_ge(consts_in.sem, LOADED)

            def project(b):
                x_in.wait(pe, b, 16)
                ba_out.wait(pe, b - 1, 1)
                for n in range(NC):
                    for k in range(KT):
                        last = nc.tensor.matmul(pz[:, n * 2 * NV:(n + 1) * 2 * NV], xb[:, k, n * C:(n + 1) * C],
                                                wba[:, k, :], start=(k == 0), stop=(k == KT - 1))
                last.then_inc(ba_mm.sem, 1)
            project(0)
            with pe.Fori(1, B) as b:
                project(b)
            pe.wait_ge(made_ones.sem, 1)
            pe.wait_ge(graw_ready.sem, 1)
            for h in range(2):
                rhs = graw[:, h * NB // 2:(h + 1) * NB // 2, :].rearrange("p b h -> p (b h)")
                nc.tensor.matmul(pg[h][:, :], triu[:, :], rhs, start=True, stop=True)
                nc.tensor.matmul(pg[2 + h][:, :], ones[:, :], rhs, start=True, stop=True).then_inc(cum_mm.sem, 1)
            pe.wait_ge(made_identb.sem, 1)
            for g in range(NTURN):
                w, n0 = g % 2, g // 2 * 4
                pe.wait_ge(parts_ready.sem, w + 1)
                if g >= 2:
                    pe.wait_ge(turn_out.sem, g - 1)
                for n in range(4):
                    last = nc.tensor.transpose(pt[g % 2][0:3 * NV, n * C:(n + 1) * C],
                                               parts[:, n0 + n, w, :, :].rearrange("p q h -> p (q h)"), identb[:, :])
                last.then_inc(turn_mm.sem, 1)

        @block.scalar
        def _(act):
            act.wait_ge(consts_in.sem, LOADED)
            nc.scalar.activation(na[:, :], na[:, :], ACT.Exp).then_inc(exp_a.sem, 1)
            act.wait_ge(x_ready.sem, 1)
            nc.scalar.activation(e[:, :, :, :], ba[:, :, :, :], ACT.Abs).then_inc(abs_ready.sem, 1)
            act.wait_ge(abs_ready.sem, 1)
            nc.scalar.activation(e[:, :, :, :], e[:, :, :, :], ACT.Exp, scale=-1.0).then_inc(exp_abs.sem, 1)
            act.wait_ge(cum_out.sem, 2)
            act.wait_ge(dl_ready.sem, 1)
            for kind, src in enumerate((gs, dl, gl)):
                for b in range(B):
                    for h in range(R):
                        o = vec[:, :, :].rearrange("p (k b) (n q h) -> p b q h n k", b=B, n=NC, q=KINDS)[:, b, kind, h]
                        i = src[:, :, :].rearrange("p (b n) (k h) -> p b h n k", b=B, h=R)[:, b, h]
                        nc.scalar.activation(o, i, ACT.Exp)
            for g in range(NTURN):
                w, n0 = g % 2, g // 2 * 4
                act.wait_ge(turn_mm.sem, g + 1)
                nc.scalar.activation(rows[:, w, n0 * C:(n0 + 4) * C], pt[g % 2][0:3 * NV, 0:4 * C],
                                     ACT.Copy).then_inc(turn_out.sem, 1)

        @block.vector
        def _(ve):
            links = [0]

            def link(ins):
                links[0] += 1
                ins.then_inc(chain.sem, 1)
                ve.wait_ge(chain.sem, links[0])
            nc.vector.memset(ones[:, :], 1.0).then_inc(made_ones.sem, 1)
            ve.wait_ge(consts_in.sem, LOADED)
            nc.vector.tensor_copy(identb[:, :], ident[:, :]).then_inc(made_identb.sem, 1)
            nc.vector.tensor_scalar(wout[:, :, :], wout[:, :, :], nwt[:, 0:1], None, ALU.mult)

            def take(b):
                ba_mm.wait(ve, b, 1)
                nc.vector.tensor_copy(ba[:, ds(b * NC, NC), :, :].rearrange("p n a h -> p (n a h)"),
                                      pz[:, 0:NC * 2 * NV]).then_inc(ba_out.sem, 1)
            take(0)
            with ve.Fori(1, B) as b:
                take(b)
            ve.wait_ge(ba_out.sem, B)
            bb, aa = ba[:, :, 0, :], ba[:, :, 1, :]
            nc.vector.tensor_scalar(bb, bb, -1.0, None, ALU.mult)
            nc.vector.tensor_tensor(aa, aa, dtb[:, None, :].broadcast_to([128, NB, NV]), ALU.add).then_inc(x_ready.sem, 1)
            ve.wait_ge(x_ready.sem, 1)
            ve.wait_ge(exp_abs.sem, 1)
            link(nc.vector.tensor_scalar(s[:, :, :, :], e[:, :, :, :], 2.0, None, ALU.add))
            link(nc.vector.reciprocal(s[:, :, :, :], s[:, :, :, :]))
            link(nc.vector.tensor_tensor(s[:, :, :, :], s[:, :, :, :], e[:, :, :, :], ALU.mult))
            link(nc.vector.tensor_tensor(s2[:, :, :, :], s[:, :, :, :], s[:, :, :, :], ALU.mult))
            link(nc.vector.tensor_scalar(p[:, :, :, :], s2[:, :, :, :], 1.0 / 15, None, ALU.mult))
            for k in (13, 11, 9, 7, 5, 3):
                link(nc.vector.scalar_tensor_tensor(out=p[:, :, :, :], in0=p[:, :, :, :], scalar=1.0 / k,
                                                    in1=s2[:, :, :, :], op0=ALU.add, op1=ALU.mult))
            link(nc.vector.scalar_tensor_tensor(out=p[:, :, :, :], in0=p[:, :, :, :], scalar=1.0,
                                                in1=s[:, :, :, :], op0=ALU.add, op1=ALU.mult))
            link(nc.vector.tensor_scalar(sp_[:, :, :, :], ba[:, :, :, :], 0.0, None, ALU.max))
            link(nc.vector.scalar_tensor_tensor(out=sp_[:, :, :, :], in0=p[:, :, :, :], scalar=2.0,
                                                in1=sp_[:, :, :, :], op0=ALU.mult, op1=ALU.add))
            ve.wait_ge(exp_a.sem, 1)
            nc.vector.scalar_tensor_tensor(out=graw[:, :, :], in0=sp_[:, :, 1, :], scalar=-1.0,
                                           in1=na[:, None, :].broadcast_to([128, NB, NV]),
                                           op0=ALU.mult, op1=ALU.mult).then_inc(graw_ready.sem, 1)
            for h in range(2):
                ve.wait_ge(cum_mm.sem, h + 1)
                n = slice(h * NB // 2, (h + 1) * NB // 2)
                nc.vector.tensor_copy(gs[:, n, :].rearrange("p b h -> p (b h)"), pg[h][:, :])
                nc.vector.tensor_copy(gl[:, n, :].rearrange("p b h -> p (b h)"), pg[2 + h][:, :]).then_inc(cum_out.sem, 1)
            ve.wait_ge(cum_out.sem, 2)
            link(nc.vector.scalar_tensor_tensor(out=hj[:, :, :], in0=sp_[:, :, 0, :], scalar=-1.0, in1=gs[:, :, :],
                                                op0=ALU.mult, op1=ALU.subtract))
            nc.vector.tensor_tensor(dl[:, :, :], hj[:, :, :], gl[:, :, :], ALU.add).then_inc(dl_ready.sem, 1)
            for w, src in enumerate((hj, gs)):
                link(nc.vector.tensor_copy(parts[:, :, w, 0, :], src[:, :, :]))
                link(nc.vector.tensor_tensor(r1[:, :, :], src[:, :, :], parts[:, :, w, 0, :], ALU.subtract))
                link(nc.vector.tensor_copy(parts[:, :, w, 1, :], r1[:, :, :]))
                link(nc.vector.tensor_tensor(r1[:, :, :], r1[:, :, :], parts[:, :, w, 1, :], ALU.subtract))
                nc.vector.tensor_copy(parts[:, :, w, 2, :], r1[:, :, :]).then_inc(parts_ready.sem, 1)
                if w == 0:
                    ve.wait_ge(parts_ready.sem, 1)


def delta_rule(nc, io, m):
    yacc, ident, wout, vec, cw, rows_dram = (m[k] for k in ("yacc", "ident", "wout", "vec", "cw", "rows_dram"))
    with ExitStack() as ctx:
        def sb(name, shape, dt=f32):
            return ctx.enter_context(nc.sbuf_tensor(name, shape, dt))

        def signal(name, per=1):
            return Signal(nc, ctx, name, per)
        ident16 = sb("ident16", [128, 128], f16)
        identb = sb("identb", [128, 128], bf16)
        ident_esc = sb("ident_esc", [128, 128])
        neg = sb("neg", [128, 4, 128], bf16)
        masks = sb("masks", [128, LEVELS, 128], u16)
        mask2 = sb("mask2", [128, 128], f16)
        expo_eps = sb("expo_eps", [128, 5, NC])
        wb = sb("wb", [128, KT, WCOL])
        xb = sb("xb", [128, KT, S])
        small = [sb(f"small{p}", [128, NC, KINDS, R]) for p in range(2)]
        cws = [sb(f"cws{p}", [128, 4 * TAPS]) for p in range(2)]
        lrow = [sb(f"lrow{p}", [6, R, NC, C], bf16) for p in range(2)]
        rrow = [sb(f"rrow{p}", [6, R, NC, C], bf16) for p in range(2)]
        conv = [sb(f"conv{c}", [128, S]) for c in range(4)]
        junk = sb("junk", [128, 4 * NC, C], bf16)
        ssq = sb("ssq", [128, 2, NC])
        ssqe = sb("ssqe", [128, 2, NC])
        rn = sb("rn", [128, 2, NC])
        tokn = [sb(f"tokn{c}", [128, NC, D]) for c in range(2)]
        kq = [sb(f"kq{p}", [128, NC, 2, C]) for p in range(2)]
        vt = [sb(f"vt{p}", [128, NC, R, D]) for p in range(2)]
        zs = [sb(f"zs{p}", [128, NC, R, D]) for p in range(2)]
        kw = [sb(f"kw{p}", [128, NC, R, D]) for p in range(2)]
        et = sb("et", [128, NU, C])
        a32 = sb("a32", [128, NU, C])
        an16 = sb("an16", [128, NU, C], f16)
        u16_ = sb("u16", [128, NU, C], f16)
        t16_ = sb("t16", [128, NU, C], f16)
        t32 = sb("t32", [128, NU, C])
        pl = [sb(f"pl{l}", [128, NU, C], f16) for l in range(LEVELS)]
        e16 = sb("e16", [128, NU, C], f16)
        u32 = [sb(f"u32{p}", [128, NU, C]) for p in range(2)]
        attn = [sb(f"attn{p}", [128, NU, C]) for p in range(2)]
        st = sb("st", [128, R, D])
        res = sb("res", [128, R, D])
        yb = sb("yb", [128, R, D])
        qe = sb("qe", [128, R, D])
        xo = sb("xo", [128, NC, R, D])
        rs = sb("rs", [128, NU])
        rse = sb("rse", [128, NU])
        rr = sb("rr", [128, NU])
        xt = sb("xt", [128, NU, C])
        pa = [ctx.enter_context(nc.psum_tensor(f"pa{i}", [128, 512], f32)) for i in range(4)]
        pb = [ctx.enter_context(nc.psum_tensor(f"pb{i}", [128, 512], f32)) for i in range(4)]

        def unit(n, h):
            return n * R + h

        def convolved(c):
            return 6 * (c // 2) + 5 + c % 2

        def four(bank):
            return bank[:, :].rearrange("p (n c) -> p n c", n=4)

        def group(t, g):
            return t[:, 4 * g:4 * g + 4, :]

        def per_head(x):
            return x[:, :, None, :].broadcast_to([128, 2, R, C])

        consts_in, made, preset = signal("consts_in", 16), signal("made"), signal("preset")
        w_in, x_in, small_ready = signal("w_in", 16), signal("x_in", 16), signal("small_ready")
        rows_in = [signal(f"rows_in{p}", 32) for p in range(2)]
        proj_mm, tap_first, tapped, silued, z_ready = signal("proj_mm", 6), signal("tap_first", 4), signal("tapped", 12), signal("silued", 4), signal("z_ready", 2)
        turn_mm, squares, eps_in, rnorm, normed = signal("turn_mm", 4), signal("squares", 2), signal("eps_in", 2), signal("rnorm", 2), signal("normed", 2)
        back_mm, kq_ready, vt_ready, kw_ready = signal("back_mm", 2), signal("kq_ready", 2), signal("vt_ready", 2), signal("kw_ready", 2)
        gram_mm, decay_mm, decay_ready, attn_ready, sys_ready, sys_diag, sys_neg = (
            signal(n, 2) for n in ("gram_mm", "decay_mm", "decay_ready", "attn_ready", "sys_ready", "sys_diag", "sys_neg"))
        u_first, t_first_mm, p_mm, p_ready, ut_mm = signal("u_first", 2), signal("t_first_mm", 2), signal("p_mm", 12), signal("p_ready", 12), signal("ut_mm", 12)
        u_ready = [signal(f"u_ready{g}", LEVELS) for g in range(2)]
        t_ready = [signal(f"t_ready{g}", LEVELS + 1) for g in range(2)]
        resid_mm, resid_ready, fix_mm, inv_ready = (signal(n, 2) for n in ("resid_mm", "resid_ready", "fix_mm", "inv_ready"))
        ks_mm, qs_mm, res_ready, y_mm, y_ready, upd_mm, intra_mm, qe_ready, st_ready, o_ready = (
            signal(*a) for a in (("ks_mm", 3), ("qs_mm", 3), ("res_ready", 4), ("y_mm", 4), ("y_ready", 4), ("upd_mm", 3),
                                 ("intra_mm", 4), ("qe_ready", 3), ("st_ready", 3), ("o_ready", 4)))
        gated, o_squares, o_eps, o_rnorm, o_normed, o_turn_mm, xt_ready, out_mm, added = (
            signal(n, 2) for n in ("gated", "o_squares", "o_eps", "o_rnorm", "o_normed", "o_turn_mm", "xt_ready", "out_mm", "added"))
        passed = [signal(f"passed{i}") for i in range(2)]
        block = ctx.enter_context(nc.Block())
        NCONST = 4
        MADE = 7

        @block.sync
        def _(sp):
            sp.dma_start(et[:, 0, :], io["neg"]).then_inc(consts_in.sem, 16)
            sp.dma_start(masks[:, :, :], io["masks"]).then_inc(consts_in.sem, 16)
            sp.dma_start(mask2[:, :], io["mask2"]).then_inc(consts_in.sem, 16)
            sp.dma_start(expo_eps[:, :, :], io["expo_eps"]).then_inc(consts_in.sem, 16)

            def load(a, p):
                proj_mm.wait(sp, a - 1, 6)
                sp.dma_start(wb[:, :, :], io["Wqkvz"].rearrange("(k p) (h n) -> h p k n", p=128, h=NK)[ds(a // B, 1)]
                             .rearrange("a p k n -> p (a k) n")).then_inc(w_in.sem, 16)
                sp.dma_start(xb[:, :, :], io["xT"][ds(a % B, 1)].rearrange("a k p n -> p (a k) n")).then_inc(x_in.sem, 16)
                decay_mm.wait(sp, a - 2, 2)
                sp.dma_start(lrow[p][3:6], rows_dram[ds(a, 1), 0].rearrange("a q h s -> (a q) h s")
                             .rearrange("q h (n c) -> q h n c", n=NC)).then_inc(rows_in[p].sem, 16)
                sp.dma_start(rrow[p][0:3], rows_dram[ds(a, 1), 1].rearrange("a q h s -> (a q) h s")
                             .rearrange("q h (n c) -> q h n c", n=NC)).then_inc(rows_in[p].sem, 16)
            made.wait(sp, 0, MADE)
            load(0, 0)
            load(1, 1)
            with sp.Fori(1, ITS // 2) as j:
                load(2 * j, 0)
                load(2 * j + 1, 1)

        ORDER = (("project", 0), ("chain", 0), ("project", 1), ("chain_in", 1), ("project", 2), ("chain", 1),
                 ("turn", 0), ("chain_in", 2), ("norm", 0), ("chain", 2), ("gram", 0), ("chain_in", 3), ("decay", 0),
                 ("chain", 3), ("first", 0), ("level", 0), ("tail", 0), ("level", 1), ("tail", 1), ("level", 2),
                 ("tail", 2), ("level", 3), ("tail", 3), ("level", 4), ("level", 5), ("refine", 0))

        def steps(engine, front, back):
            def step(a, p, has_front=True, has_back=True):
                for stage, n in ORDER:
                    if stage in front and has_front:
                        front[stage](a, p, n)
                    if stage in back and has_back:
                        back[stage](a - 1, 1 - p, n)
            step(0, 0, has_back=False)
            step(1, 1)
            with engine.Fori(1, ITS // 2) as j:
                step(2 * j, 0)
                step(2 * j + 1, 1)
            step(ITS, 0, has_front=False)

        @block.tensor
        def _(pe):
            made.wait(pe, 0, MADE)
            consts_in.wait(pe, 0, 16 * NCONST)

            def project(a, p, part):
                if part == 0:
                    w_in.wait(pe, a, 16)
                    x_in.wait(pe, a, 16)
                if part < 2:
                    for c in (2 * part, 2 * part + 1):
                        (resid_ready if c % 2 == 0 else inv_ready).wait(pe, a - 1, c // 2 + 1)
                        for k in range(KT):
                            last = nc.tensor.matmul(pa[c][:, :], wb[:, k, c * D:(c + 1) * D], xb[:, k, :],
                                                    start=(k == 0), stop=(k == KT - 1))
                        last.then_inc(proj_mm.sem, 1)
                else:
                    for g in range(2):
                        tapped.wait(pe, a, convolved(g))
                        for n in range(2):
                            for k in range(KT):
                                last = nc.tensor.matmul(pa[g][:, n * R * D:(n + 1) * R * D],
                                                        xb[:, k, (2 * g + n) * C:(2 * g + n + 1) * C],
                                                        wb[:, k, 4 * D:4 * D + R * D], start=(k == 0), stop=(k == KT - 1))
                        last.then_inc(proj_mm.sem, 1)

            def turn(a, p, _):
                for c in range(4):
                    silued.wait(pe, a, c + 1)
                    bank = pa[(c + 2) % 4]
                    if c < 2:
                        tapped.wait(pe, a, convolved(c + 2))
                    else:
                        z_ready.wait(pe, a, c - 1)
                    for n in range(NC):
                        last = nc.tensor.transpose(bank[:, n * C:(n + 1) * C], conv[c][:, n * C:(n + 1) * C], ident[:, :])
                    last.then_inc(turn_mm.sem, 1)

            def norm(a, p, _):
                for c in range(2):
                    normed.wait(pe, a, c + 1)
                    for n in range(NC):
                        last = nc.tensor.transpose(pa[c + 2][:, n * C:(n + 1) * C], tokn[c][:, n, :], ident[:, :])
                    last.then_inc(back_mm.sem, 1)

            def gram(a, p, _):
                kq_ready.wait(pe, a, 2)
                for g in range(2):
                    vt_ready.wait(pe, a, g + 1)
                    for n in range(2):
                        nn = 2 * g + n
                        last = nc.tensor.matmul(pa[g][:, n * 2 * C:(n + 1) * 2 * C], kq[p][:, nn, 0, :],
                                                kq[p][:, nn, :, :], start=True, stop=True)
                    last.then_inc(gram_mm.sem, 1)

            def decay(a, p, _):
                rows_in[p].wait(pe, a // 2, 32)
                for g in range(2):
                    kq_ready.wait(pe, a, g + 1)
                    nc.tensor.matmul(pa[2 + g][:, :], identb[:, :], neg[:, :, :].rearrange("p u c -> p (u c)"),
                                     start=True, stop=True)
                    for n in range(2):
                        for h in range(R):
                            u = n * R + h
                            last = nc.tensor.matmul(pa[2 + g][:, u * C:(u + 1) * C], lrow[p][:, h, 2 * g + n, :],
                                                    rrow[p][:, h, 2 * g + n, :], start=False, stop=True,
                                                    skip_group_check=True)
                    last.then_inc(decay_mm.sem, 1)

            def first(a, p, _):
                for g in range(2):
                    u_first.wait(pe, a, g + 1)
                    (attn_ready if g == 0 else decay_ready).wait(pe, a, 1)
                    sys_ready.wait(pe, a, 1)
                    for u in range(4):
                        last = nc.tensor.transpose(pa[2 * g][:, :].bitcast(f16)[:, u * C:(u + 1) * C],
                                                   u16_[:, 4 * g + u, :], ident16[:, :])
                    last.then_inc(t_first_mm.sem, 1)

            def level(a, p, l):
                for g in range(2):
                    t_ready[g].wait(pe, a, l + 1)
                    if l == 0 and g == 0:
                        attn_ready.wait(pe, a, 2)
                        sys_ready.wait(pe, a, 2)
                    if l == 0 and g == 1:
                        decay_ready.wait(pe, a, 2)
                    for u in range(4):
                        last = nc.tensor.matmul(pa[2 * g + 1][:, u * C:(u + 1) * C], an16[:, 4 * g + u, :],
                                                t16_[:, 4 * g + u, :], start=True, stop=True)
                    last.then_inc(p_mm.sem, 1)
                for g in range(2):
                    p_ready.wait(pe, a, 2 * l + g + 1)
                    if l:
                        u_ready[g].wait(pe, a, l)
                    for u in range(4):
                        nc.tensor.matmul(pa[2 * g][:, u * C:(u + 1) * C], pl[l][:, 4 * g + u, :], u16_[:, 4 * g + u, :],
                                         start=True, stop=True)
                    for u in range(4):
                        last = nc.tensor.matmul(pa[2 * g + 1][:, u * C:(u + 1) * C], u16_[:, 4 * g + u, :],
                                                pl[l][:, 4 * g + u, :], start=True, stop=True)
                    last.then_inc(ut_mm.sem, 1)

            def refine(a, p, _):
                for g in range(2):
                    t_ready[g].wait(pe, a, LEVELS + 1)
                    u_ready[g].wait(pe, a, LEVELS)
                    for u in range(4):
                        last = nc.tensor.matmul(pa[2 * g][:, u * C:(u + 1) * C], a32[:, 4 * g + u, :], t32[:, 4 * g + u, :],
                                                start=True, stop=True)
                    last.then_inc(resid_mm.sem, 1)
                for g in range(2):
                    resid_ready.wait(pe, a, g + 1)
                    for u in range(4):
                        last = nc.tensor.matmul(pa[2 * g + 1][:, u * C:(u + 1) * C], e16[:, 4 * g + u, :],
                                                u16_[:, 4 * g + u, :], start=True, stop=True)
                    last.then_inc(fix_mm.sem, 1)

            def chain_in(b, p, n):
                st_ready.wait(pe, b, n)
                y_ready.wait(pe, b, n)
                nc.tensor.matmul(pb[0][:, 0:R * D], kq[p][:, n, 0, :], st[:, :, :], start=True, stop=True)\
                    .then_inc(ks_mm.sem, 1)
                o_ready.wait(pe, b, n)
                nc.tensor.matmul(pb[1][:, 0:R * D], kq[p][:, n, 1, :], st[:, :, :], start=True, stop=True)\
                    .then_inc(qs_mm.sem, 1)

            def chain(b, p, n):
                res_ready.wait(pe, b, n + 1)
                if n == 0:
                    inv_ready.wait(pe, b, 2)
                    y_ready.wait(pe, b - 1, NC)
                for h in range(R):
                    last = nc.tensor.matmul(pb[0][:, h * D:(h + 1) * D], u32[p][:, unit(n, h), :], res[:, h, :],
                                            start=True, stop=True)
                last.then_inc(y_mm.sem, 1)
                y_ready.wait(pe, b, n + 1)
                if n < NC - 1:
                    if n == 0:
                        kw_ready.wait(pe, b, 2)
                    else:
                        st_ready.wait(pe, b, n)
                    for h in range(R):
                        last = nc.tensor.matmul(pb[2][:, h * D:(h + 1) * D], kw[p][:, n, h, :], yb[:, h, :],
                                                start=True, stop=True)
                    last.then_inc(upd_mm.sem, 1)
                if n == 0:
                    attn_ready.wait(pe, b, 2)
                    o_ready.wait(pe, b - 1, NC)
                else:
                    qe_ready.wait(pe, b, n)
                for h in range(R):
                    last = nc.tensor.matmul(pb[1][:, h * D:(h + 1) * D], attn[p][:, unit(n, h), :], yb[:, h, :],
                                            start=True, stop=True)
                last.then_inc(intra_mm.sem, 1)

            def tail(b, p, n):
                g = n // 2
                if n % 2 == 0:
                    o_normed.wait(pe, b, g + 1)
                    added.wait(pe, b if g else b - 1, 1 if g else 2)
                    for u in range(4):
                        last = nc.tensor.transpose(pb[3][:, u * C:(u + 1) * C],
                                                   xo[:, 2 * g + u // R, u % R, :], ident[:, :])
                    last.then_inc(o_turn_mm.sem, 1)
                else:
                    xt_ready.wait(pe, b, g + 1)
                    for i in range(2):
                        for h in range(R):
                            last = nc.tensor.matmul(pb[3][:, i * H:(i + 1) * H], xt[:, unit(2 * g + i, h), :],
                                                    wout[:, ds((b // B) * R + h, 1), :].rearrange("p a n -> p (a n)"),
                                                    start=(h == 0), stop=(h == R - 1))
                    last.then_inc(out_mm.sem, 1)
            steps(pe, {"project": project, "turn": turn, "norm": norm, "gram": gram, "decay": decay, "first": first,
                       "level": level, "refine": refine}, {"chain_in": chain_in, "chain": chain, "tail": tail})

        @block.scalar
        def _(act):
            made.wait(act, 0, MADE)

            def project(a, p, part):
                if part == 0:
                    small_ready.wait(act, a, 1)
                if part < 2:
                    for c in (2 * part, 2 * part + 1):
                        proj_mm.wait(act, a, c + 1)
                        turn_mm.wait(act, a - 1, c + 1)
                        nc.scalar.activation(conv[c][:, :], pa[c][:, :], ACT.Copy,
                                             scale=cws[p][:, c * TAPS + 3:c * TAPS + 4]).then_inc(tap_first.sem, 1)
                if part == 2:
                    for c in range(4):
                        tapped.wait(act, a, convolved(c))
                        nc.scalar.activation(conv[c][:, :], conv[c][:, :], ACT.Silu).then_inc(silued.sem, 1)
                    for g in range(2):
                        proj_mm.wait(act, a, 5 + g)
                        gated.wait(act, a - 2, 2)
                        nc.scalar.activation(zs[p][:, 2 * g:2 * g + 2, :, :].rearrange("p n h c -> p (n h c)"),
                                             pa[g][:, :], ACT.Silu).then_inc(z_ready.sem, 1)

            def turn(a, p, _):
                for c in range(2):
                    turn_mm.wait(act, a, c + 1)
                    for n in range(NC):
                        last = nc.scalar.activation(junk[:, c * NC + n, :], pa[c + 2][:, n * C:(n + 1) * C], ACT.Square,
                                                    scale=1.0 if c == 0 else float(D) ** 0.5, accum_out=ssq[:, c, n:n + 1])
                    last.then_inc(squares.sem, 1)
                for c in range(2):
                    turn_mm.wait(act, a, c + 3)
                    res_ready.wait(act, a - 2, NC)
                    nc.scalar.activation(vt[p][:, :, c, :], four(pa[c]), ACT.Copy).then_inc(vt_ready.sem, 1)

            def norm(a, p, _):
                for c in range(2):
                    back_mm.wait(act, a, c + 1)
                    qs_mm.wait(act, a - 2, 3)
                    nc.scalar.activation(kq[p][:, :, c, :], four(pa[c + 2]), ACT.Copy).then_inc(kq_ready.sem, 1)

            def decay(a, p, _):
                for g in range(2):
                    decay_mm.wait(act, a, g + 1)
                    attn_ready.wait(act, a - 1, 2)
                    sys_ready.wait(act, a - 1, 2)
                    nc.scalar.activation(group(et, g), four(pa[2 + g]), ACT.Exp).then_inc(decay_ready.sem, 1)

            def first(a, p, _):
                for g in range(2):
                    sys_diag.wait(act, a, g + 1)
                    nc.scalar.activation(group(an16, g), group(a32, g), ACT.Copy, scale=-1.0).then_inc(sys_neg.sem, 1)
                t_first_mm.wait(act, a, 2)
                nc.scalar.activation(group(t16_, 1), pa[2][:, :].bitcast(f16)[:, 0:512].rearrange("p (u c) -> p u c", u=4),
                                     ACT.Copy).then_inc(t_ready[1].sem, 1)

            def level(a, p, l):
                for g in range(2):
                    ut_mm.wait(act, a, 2 * l + g + 1)
                    nc.scalar.activation(group(u16_, g), four(pa[2 * g]), ACT.Copy).then_inc(u_ready[g].sem, 1)
                    if g == 1:
                        nc.scalar.activation(group(t16_ if l < LEVELS - 1 else t32, g), four(pa[2 * g + 1]), ACT.Copy)\
                            .then_inc(t_ready[g].sem, 1)

            def chain(b, p, n):
                y_mm.wait(act, b, n + 1)
                if n:
                    intra_mm.wait(act, b, n)
                else:
                    intra_mm.wait(act, b - 1, NC)
                nc.scalar.activation(yb[:, :, :], pb[0][:, 0:R * D].rearrange("p (h d) -> p h d", h=R), ACT.Copy)\
                    .then_inc(y_ready.sem, 1)

            def chain_in(b, p, n):
                qs_mm.wait(act, b, n)
                o_ready.wait(act, b, n)
                for h in range(R):
                    last = nc.scalar.activation(qe[:, h, :], pb[1][:, h * D:(h + 1) * D], ACT.Copy,
                                                scale=small[p][:, n, 0, h:h + 1])
                last.then_inc(qe_ready.sem, 1)

            def tail(b, p, n):
                g = n // 2
                if n % 2 == 0:
                    gated.wait(act, b, g + 1)
                    for u in range(4):
                        last = nc.scalar.activation(junk[:, 2 * NC + 4 * g + u, :], xo[:, 2 * g + u // R, u % R, :], ACT.Square,
                                                    scale=float(D) ** -0.5, accum_out=rs[:, 4 * g + u:4 * g + u + 1])
                    last.then_inc(o_squares.sem, 1)
                else:
                    o_turn_mm.wait(act, b, g + 1)
                    nc.scalar.activation(group(xt, g), four(pb[3]), ACT.Copy).then_inc(xt_ready.sem, 1)
            steps(act, {"project": project, "turn": turn, "norm": norm, "decay": decay, "first": first, "level": level},
                  {"chain": chain, "chain_in": chain_in, "tail": tail})

        @block.vector
        def _(ve):
            for q in range(2):
                nc.vector.memset(lrow[q][:, :, :, :], 1.0)
                nc.vector.memset(rrow[q][:, :, :, :], 1.0).then_inc(made.sem, 1)
            nc.vector.tensor_copy(ident16[:, :], ident[:, :]).then_inc(made.sem, 1)
            nc.vector.tensor_copy(identb[:, :], ident[:, :]).then_inc(made.sem, 1)
            nc.vector.tensor_scalar(ident_esc[:, :], ident[:, :], ESC, None, ALU.mult).then_inc(made.sem, 1)
            consts_in.wait(ve, 0, 16 * NCONST)
            nc.vector.tensor_copy(neg[:, :, :], et[:, 0:1, :].broadcast_to([128, 4, C])).then_inc(made.sem, 1)
            made.wait(ve, 0, MADE)
            consts_in.wait(ve, 0, 16 * NCONST)

            def project(a, p, part):
                if part == 0:
                    small_ready.wait(ve, a, 1)
                if part < 2:
                    for back in (1, 2, 3):
                        for c in (2 * part, 2 * part + 1):
                            if back == 1:
                                tap_first.wait(ve, a, c + 1)
                            else:
                                tapped.wait(ve, a, 6 * part + 2 * (back - 2) + (c % 2) + 1)
                            nc.vector.scalar_tensor_tensor(
                                out=conv[c][:, back:S], in0=pa[c][:, 0:S - back],
                                scalar=cws[p][:, c * TAPS + 3 - back:c * TAPS + 4 - back], in1=conv[c][:, back:S],
                                op0=ALU.mult, op1=ALU.add).then_inc(tapped.sem, 1)

            def turn(a, p, _):
                for c in range(2):
                    rnorm.wait(ve, a, c + 1)
                    if c == 0:
                        kw_ready.wait(ve, a - 1, 2)
                    nc.vector.tensor_tensor(tokn[c][:, :, :], four(pa[c + 2]),
                                            rn[:, c, :, None].broadcast_to([128, NC, C]), ALU.mult).then_inc(normed.sem, 1)

            def decay(a, p, _):
                for g in range(2):
                    decay_ready.wait(ve, a, g + 1)
                    gram_mm.wait(ve, a, g + 1)
                    grams = pa[g][:, :].rearrange("p (n w c) -> p n w c", n=2, w=2)
                    eg = group(et, g).rearrange("p (n h) c -> p n h c", h=R)
                    intra_mm.wait(ve, a - 2, NC)
                    nc.vector.tensor_tensor(group(a32, g).rearrange("p (n h) c -> p n h c", h=R), per_head(grams[:, :, 0, :]),
                                            eg, ALU.mult).then_inc(sys_ready.sem, 1)
                    nc.vector.tensor_tensor(group(attn[p], g).rearrange("p (n h) c -> p n h c", h=R),
                                            per_head(grams[:, :, 1, :]), eg, ALU.mult).then_inc(attn_ready.sem, 1)

            def first(a, p, _):
                for g in range(2):
                    sys_neg.wait(ve, a, g + 1)
                    nc.vector.tensor_tensor(group(u16_, g), group(an16, g),
                                            mask2[:, None, :].broadcast_to([128, 4, C]), ALU.mult).then_inc(u_first.sem, 1)
                t_first_mm.wait(ve, a, 1)
                nc.vector.tensor_copy(group(t16_, 0), pa[0][:, :].bitcast(f16)[:, 0:512].rearrange("p (u c) -> p u c", u=4))\
                    .then_inc(t_ready[0].sem, 1)

            preset.wait(ve, 0, LEVELS)

            def level(a, p, l):
                for g in range(2):
                    p_mm.wait(ve, a, 2 * l + g + 1)
                    ve.sem_inc(passed[0].sem, 1)
                    nc.vector.copy_predicated(group(pl[l], g), masks[:, l:l + 1, :].broadcast_to([128, 4, C]),
                                              four(pa[2 * g + 1])).then_inc(p_ready.sem, 1)
                ut_mm.wait(ve, a, 2 * l + 1)
                nc.vector.tensor_copy(group(t16_ if l < LEVELS - 1 else t32, 0), four(pa[1])).then_inc(t_ready[0].sem, 1)

            def refine(a, p, _):
                for g in range(2):
                    resid_mm.wait(ve, a, g + 1)
                    nc.vector.scalar_tensor_tensor(out=group(e16, g), in0=four(pa[2 * g]), scalar=-ESC,
                                                   in1=ident_esc[:, None, :].broadcast_to([128, 4, C]),
                                                   op0=ALU.mult, op1=ALU.add).then_inc(resid_ready.sem, 1)
                for g in range(2):
                    fix_mm.wait(ve, a, g + 1)
                    y_mm.wait(ve, a - 2, NC)
                    nc.vector.scalar_tensor_tensor(out=group(u32[p], g), in0=four(pa[2 * g + 1]), scalar=1.0 / ESC,
                                                   in1=group(u16_, g), op0=ALU.mult, op1=ALU.add).then_inc(inv_ready.sem, 1)

            def residual(b, p, n):
                if n == 0:
                    vt_ready.wait(ve, b, 2)
                    y_mm.wait(ve, b - 1, NC)
                    nc.vector.tensor_scalar(res[:, :, :], vt[p][:, 0, :, :], -1.0, None, ALU.mult).then_inc(res_ready.sem, 1)
                    return
                ks_mm.wait(ve, b, n)
                for h in range(R):
                    last = nc.vector.scalar_tensor_tensor(out=res[:, h, :], in0=pb[0][:, h * D:(h + 1) * D],
                                                          scalar=small[p][:, n, 0, h:h + 1], in1=vt[p][:, n, h, :],
                                                          op0=ALU.mult, op1=ALU.subtract)
                last.then_inc(res_ready.sem, 1)

            def chain_in(b, p, n):
                residual(b, p, n)

            def chain(b, p, n):
                if n == 0:
                    residual(b, p, 0)
                if n < NC - 1:
                    upd_mm.wait(ve, b, n + 1)
                    if n == 0:
                        nc.vector.tensor_scalar(st[:, :, :].rearrange("p h d -> p (h d)"), pb[2][:, 0:R * D], -1.0, None,
                                                ALU.mult).then_inc(st_ready.sem, 1)
                    else:
                        st_ready.wait(ve, b, n)
                        for h in range(R):
                            last = nc.vector.scalar_tensor_tensor(out=st[:, h, :], in0=st[:, h, :],
                                                                  scalar=small[p][:, n, 2, h:h + 1],
                                                                  in1=pb[2][:, h * D:(h + 1) * D],
                                                                  op0=ALU.mult, op1=ALU.subtract)
                        last.then_inc(st_ready.sem, 1)
                intra_mm.wait(ve, b, n + 1)
                if n == 0:
                    o_turn_mm.wait(ve, b - 1, 2)
                    nc.vector.tensor_scalar(xo[:, 0, :, :].rearrange("p h d -> p (h d)"), pb[1][:, 0:R * D], -1.0, None,
                                            ALU.mult).then_inc(o_ready.sem, 1)
                else:
                    qe_ready.wait(ve, b, n)
                    nc.vector.tensor_tensor(xo[:, n, :, :], qe[:, :, :], pb[1][:, 0:R * D].rearrange("p (h d) -> p h d", h=R),
                                            ALU.subtract).then_inc(o_ready.sem, 1)

            def tail(b, p, n):
                g = n // 2
                if n % 2 == 0:
                    o_rnorm.wait(ve, b, g + 1)
                    o_squares.wait(ve, b, g + 1)
                    x = xo[:, 2 * g:2 * g + 2, :, :].rearrange("p n h d -> p (n h) d")
                    nc.vector.tensor_tensor(x, x, rr[:, 4 * g:4 * g + 4, None].broadcast_to([128, 4, D]), ALU.mult)\
                        .then_inc(o_normed.sem, 1)
                else:
                    out_mm.wait(ve, b, g + 1)
                    y = yacc[:, ds((b % B) * NC + 2 * g, 2), :]
                    added.wait(ve, b - 1, 2)
                    nc.vector.tensor_tensor(y, y, pb[3][:, :].rearrange("p (n h) -> p n h", n=2), ALU.add)\
                        .then_inc(added.sem, 1)
            steps(ve, {"project": project, "turn": turn, "decay": decay, "first": first, "level": level, "refine": refine},
                  {"chain": chain, "chain_in": chain_in, "tail": tail})

        @block.gpsimd
        def _(pool):
            made.wait(pool, 0, 1)
            for q in range(LEVELS):
                nc.gpsimd.tensor_copy(pl[q][:, :, :], ident[:, None, :].broadcast_to([128, NU, C])).then_inc(preset.sem, 1)
            nc.gpsimd.memset(junk[:, 0, :], 0.0).then_inc(made.sem, 1)
            consts_in.wait(pool, 0, 16 * NCONST)

            def project(a, p, part):
                if part == 0:
                    consts_in.wait(pool, 0, 16 * NCONST)
                    qe_ready.wait(pool, a - 2, 3)
                    st_ready.wait(pool, a - 2, 3)
                    res_ready.wait(pool, a - 2, NC)
                    nc.gpsimd.tensor_copy(cws[p][:, :], cw[:, ds(a // B, 1), :].rearrange("p a n -> p (a n)"))
                    nc.gpsimd.tensor_copy(small[p][:, :, :, :].rearrange("p n q h -> p (n q h)"),
                                          vec[:, ds(a, 1), :].rearrange("p a n -> p (a n)")).then_inc(small_ready.sem, 1)

            def turn(a, p, _):
                for c in range(2):
                    squares.wait(pool, a, c + 1)
                    nc.gpsimd.tensor_tensor(ssqe[:, c, :], ssq[:, c, :], expo_eps[:, 1 + c, :], ALU.add)\
                        .then_inc(eps_in.sem, 1)
                    eps_in.wait(pool, a, c + 1)
                    nc.gpsimd.tensor_tensor(rn[:, c, :], ssqe[:, c, :], expo_eps[:, 0, :], ALU.pow).then_inc(rnorm.sem, 1)

            def norm(a, p, _):
                normed.wait(pool, a, 1)
                upd_mm.wait(pool, a - 2, 3)
                small_ready.wait(pool, a, 1)
                for h in range(R):
                    nc.gpsimd.tensor_tensor(kw[p][:, :, h, :], tokn[0][:, :, :],
                                            small[p][:, :, 1, h:h + 1].broadcast_to([128, NC, D]), ALU.mult)\
                        .then_inc(kw_ready.sem, 1)

            def first(a, p, _):
                for g in range(2):
                    sys_ready.wait(pool, a, g + 1)
                    pool.sem_inc(passed[1].sem, 1)
                    nc.gpsimd.affine_select(out=group(a32, g), in_=group(a32, g), compare_op=ALU.not_equal, fill=1.0,
                                            base=0, pattern=[[0, 4], [-1, C]], channel_multiplier=1).then_inc(sys_diag.sem, 1)

            def tail(b, p, n):
                g = n // 2
                x = xo[:, 2 * g:2 * g + 2, :, :]
                if n % 2 == 0:
                    z_ready.wait(pool, b, g + 1)
                    o_ready.wait(pool, b, 2 * g + 2)
                    nc.gpsimd.tensor_tensor(x, x, zs[p][:, 2 * g:2 * g + 2, :, :], ALU.mult).then_inc(gated.sem, 1)
                    o_squares.wait(pool, b, g + 1)
                    nc.gpsimd.tensor_tensor(rse[:, 4 * g:4 * g + 4], rs[:, 4 * g:4 * g + 4], expo_eps[:, 3, :], ALU.add)\
                        .then_inc(o_eps.sem, 1)
                    o_eps.wait(pool, b, g + 1)
                    nc.gpsimd.tensor_tensor(rr[:, 4 * g:4 * g + 4], rse[:, 4 * g:4 * g + 4], expo_eps[:, 0, :], ALU.pow)\
                        .then_inc(o_rnorm.sem, 1)
            steps(pool, {"project": project, "turn": turn, "norm": norm, "first": first}, {"tail": tail})


def feed_forward(nc, io, m):
    yacc, ident = m["yacc"], m["ident"]
    with ExitStack() as ctx:
        def sb(name, shape, dt=f32):
            return ctx.enter_context(nc.sbuf_tensor(name, shape, dt))

        def signal(name, per=1):
            return Signal(nc, ctx, name, per)
        wug = sb("wug", [128, 2, KT, E])
        wdn = sb("wdn", [128, ET, H])
        low = sb("low", [128, 2, KT, E])
        ones = sb("fones", [128, 128])
        expo_eps = sb("fexpo_eps", [128, 5, NC])
        asum = sb("asum", [128, 3])
        scale = sb("scale", [128, 3])
        half = sb("half", [128, 3])
        mhalfs = sb("mhalfs", [128, 3])
        sgd = sb("sgd", [128, 1])
        mean = sb("fmean", [128, 2, NC])
        meanm = sb("fmeanm", [128, 2, NC])
        var = sb("fvar", [128, 2, NC])
        vare = sb("fvare", [128, 2, NC])
        rstd = sb("frstd", [128, 2, NC])
        junk = sb("fjunk", [128, 2 * NC, H], bf16)
        xn = sb("fxn", [128, NC, H])
        xnT = sb("fxnT", [128, KT, S])
        up = sb("fup", [128, ET, S])
        hid = sb("fhid", [128, ET, S])
        yo = sb("fyo", [128, NC, H])
        ob = [sb(f"fob{i}", [128, NC, H]) for i in range(2)]
        pw = ctx.enter_context(nc.psum_tensor("pw", [128, 512], f32))
        pt = ctx.enter_context(nc.psum_tensor("fpt", [128, 512], f32))
        pu = [ctx.enter_context(nc.psum_tensor(f"pu{i}", [128, 512], f32)) for i in range(2)]
        pv = [ctx.enter_context(nc.psum_tensor(f"pv{i}", [128, 512], f32)) for i in range(2)]
        pd = [ctx.enter_context(nc.psum_tensor(f"pd{i}", [128, 512], f32)) for i in range(2)]
        w_in, made, sums, total_mm, chain, tern = (signal(f"f_{n}") for n in ("w_in", "made", "sums", "total_mm", "chain", "tern"))
        meaned, centred, vars_ready, eps_in, rstd_ready, normed = (signal(f"f_{n}", 2) for n in ("meaned", "centred", "vars", "eps", "rstd", "normed"))
        means = signal("f_means", 2)
        turn_mm, turned, up_mm, gate_mm, silued, hid_ready, down_mm, y_ready = (
            signal(*a) for a in (("f_turn_mm", 2), ("f_turned", 2), ("f_up_mm", ET), ("f_gate_mm", ET), ("f_silued", ET),
                                 ("f_hid", ET), ("f_down_mm", 2), ("f_y", 2)))
        stored = [signal(f"f_stored{p}", 16) for p in range(2)]
        block = ctx.enter_context(nc.Block())
        NTERN = 3

        @block.sync
        def _(sp):
            sp.dma_start(wug[:, 0, :, :], io["WupT"].rearrange("(k p) n -> p k n", p=128)).then_inc(w_in.sem, 16)
            sp.dma_start(wug[:, 1, :, :], io["WgateT"].rearrange("(k p) n -> p k n", p=128)).then_inc(w_in.sem, 16)
            sp.dma_start(wdn[:, :, :], io["WdownT"].rearrange("(k p) n -> p k n", p=128)).then_inc(w_in.sem, 16)
            sp.dma_start(expo_eps[:, :, :], io["expo_eps"]).then_inc(w_in.sem, 16)

            def store(i, p):
                normed.wait(sp, i, 2)
                sp.dma_start(io["out"].rearrange("(i n p) h -> i p n h", n=NC, p=128)[ds(i, 1)]
                             .rearrange("i p n h -> p (i n) h"), ob[p][:, :, :]).then_inc(stored[p].sem, 16)
            store(0, 0)
            store(1, 1)
            with sp.Fori(1, B // 2) as j:
                store(2 * j, 0)
                store(2 * j + 1, 1)
            for p in range(2):
                stored[p].wait(sp, B // 2 - 1, 16)

        def loop(engine, body):
            body(0, 0)
            body(1, 1)
            with engine.Fori(1, B // 2) as j:
                body(2 * j, 0)
                body(2 * j + 1, 1)

        @block.tensor
        def _(pe):
            made.wait(pe, 0, 1)
            sums.wait(pe, 0, 3)
            nc.tensor.matmul(pw[:, 0:3], ones[:, :], asum[:, :], start=True, stop=True).then_inc(total_mm.sem, 1)
            tern.wait(pe, 0, NTERN)

            def body(i, p):
                normed.wait(pe, i, 1)
                for k in range(KT):
                    if k == 0:
                        turned.wait(pe, i - 1, 2)
                    else:
                        turned.wait(pe, i, 1)
                    for n in range(NC):
                        last = nc.tensor.transpose(pt[:, n * C:(n + 1) * C], xn[:, n, k * 128:(k + 1) * 128], ident[:, :])
                    last.then_inc(turn_mm.sem, 1)
                turned.wait(pe, i, 2)
                for t in range(ET):
                    if t >= 2:
                        silued.wait(pe, i, t - 1)
                    else:
                        silued.wait(pe, i - 1, ET)
                    for k in range(KT):
                        last = nc.tensor.matmul(pu[t % 2][:, :], wug[:, 0, k, t * 128:(t + 1) * 128], xnT[:, k, :],
                                                start=(k == 0), stop=(k == KT - 1))
                    last.then_inc(up_mm.sem, 1)
                    if t >= 2:
                        hid_ready.wait(pe, i, t - 1)
                    else:
                        hid_ready.wait(pe, i - 1, ET)
                    for k in range(KT):
                        last = nc.tensor.matmul(pv[t % 2][:, :], wug[:, 1, k, t * 128:(t + 1) * 128], xnT[:, k, :],
                                                start=(k == 0), stop=(k == KT - 1))
                    last.then_inc(gate_mm.sem, 1)
                hid_ready.wait(pe, i, ET)
                for g in range(2):
                    y_ready.wait(pe, i - 1, g + 1)
                    for n in range(2):
                        for t in range(ET):
                            last = nc.tensor.matmul(pd[g][:, n * H:(n + 1) * H],
                                                    hid[:, t, (2 * g + n) * C:(2 * g + n + 1) * C], wdn[:, t, :],
                                                    start=(t == 0), stop=(t == ET - 1))
                    last.then_inc(down_mm.sem, 1)
            loop(pe, body)

        @block.scalar
        def _(act):
            def squares(i, which, src):
                centred.wait(act, i, which + 1)
                for n in range(NC):
                    last = nc.scalar.activation(junk[:, which * NC + n, :], src[:, n, :], ACT.Square, scale=float(H) ** -0.5,
                                                accum_out=var[:, which, n:n + 1])
                last.then_inc(vars_ready.sem, 1)
            tern.wait(act, 0, NTERN)

            def body(i, p):
                squares(i, 0, xn)
                for k in range(KT):
                    turn_mm.wait(act, i, k + 1)
                    nc.scalar.activation(xnT[:, k, :], pt[:, :], ACT.Copy).then_inc(turned.sem, 1)
                for t in range(ET):
                    up_mm.wait(act, i, t + 1)
                    hid_ready.wait(act, i - 1, ET)
                    nc.scalar.activation(up[:, t, :], pu[t % 2][:, :], ACT.Silu, scale=scale[:, 0:1]).then_inc(silued.sem, 1)
                squares(i, 1, yo)
            loop(act, body)

        @block.gpsimd
        def _(pool):
            w_in.wait(pool, 0, 64)

            def body(i, p):
                for w in range(2):
                    vars_ready.wait(pool, i, w + 1)
                    nc.gpsimd.tensor_tensor(vare[:, w, :], var[:, w, :], expo_eps[:, 4, :], ALU.add).then_inc(eps_in.sem, 1)
                    eps_in.wait(pool, i, w + 1)
                    nc.gpsimd.tensor_tensor(rstd[:, w, :], vare[:, w, :], expo_eps[:, 0, :], ALU.pow).then_inc(rstd_ready.sem, 1)
            loop(pool, body)

        @block.vector
        def _(ve):
            links = [0]

            def link(ins):
                links[0] += 1
                ins.then_inc(chain.sem, 1)
                ve.wait_ge(chain.sem, links[0])
            nc.vector.memset(ones[:, :], 1.0).then_inc(made.sem, 1)
            w_in.wait(ve, 0, 64)
            for q, w in enumerate((wug[:, 0], wug[:, 1], wdn[:, :, :])):
                nc.vector.tensor_reduce(asum[:, q:q + 1], w, AX.XY, ALU.add, apply_absolute_value=True).then_inc(sums.sem, 1)
            total_mm.wait(ve, 0, 1)
            link(nc.vector.tensor_scalar(scale[:, :], pw[:, 0:3], 1.0 / (E * H), TERN_EPS, ALU.mult, ALU.add))
            link(nc.vector.tensor_scalar(half[:, :], scale[:, :], 0.5, None, ALU.mult))
            link(nc.vector.tensor_scalar(mhalfs[:, :], scale[:, :], -0.5, None, ALU.mult))
            link(nc.vector.tensor_tensor(sgd[:, :], scale[:, 1:2], scale[:, 2:3], ALU.mult))
            for q, w in enumerate((wug[:, 0], wug[:, 1], wdn[:, :, :])):
                lo = low[:, 0, :, :] if q < 2 else low[:, 0, :, :].rearrange("p k n -> p (k n)").rearrange("p (t h) -> p t h", t=ET)
                link(nc.vector.tensor_scalar(lo, w, mhalfs[:, q:q + 1], None, ALU.is_lt))
                nc.vector.scalar_tensor_tensor(out=w, in0=w, scalar=half[:, q:q + 1], in1=lo, op0=ALU.is_gt,
                                               op1=ALU.subtract).then_inc(tern.sem, 1)
                tern.wait(ve, 0, q + 1)

            def norm(i, w, src, centre, dst):
                nc.vector.tensor_reduce(mean[:, w, :], src, AX.X, ALU.add).then_inc(meaned.sem, 1)
                meaned.wait(ve, i, w + 1)
                nc.vector.tensor_scalar(meanm[:, w, :], mean[:, w, :], 1.0 / H, None, ALU.mult).then_inc(means.sem, 1)
                means.wait(ve, i, w + 1)
                nc.vector.tensor_tensor(centre, src, meanm[:, w, :, None].broadcast_to([128, NC, H]), ALU.subtract)\
                    .then_inc(centred.sem, 1)
                rstd_ready.wait(ve, i, w + 1)
                vars_ready.wait(ve, i, w + 1)
                nc.vector.tensor_tensor(dst, centre, rstd[:, w, :, None].broadcast_to([128, NC, H]), ALU.mult)\
                    .then_inc(normed.sem, 1)

            def body(i, p):
                turn_mm.wait(ve, i - 1, 2)
                y_ready.wait(ve, i - 1, 2)
                norm(i, 0, yacc[:, ds(i * NC, NC), :], xn[:, :, :], xn[:, :, :])
                for t in range(ET):
                    gate_mm.wait(ve, i, t + 1)
                    silued.wait(ve, i, t + 1)
                    down_mm.wait(ve, i - 1, 2)
                    nc.vector.tensor_tensor(hid[:, t, :], up[:, t, :], pv[t % 2][:, :], ALU.mult).then_inc(hid_ready.sem, 1)
                normed.wait(ve, i, 1)
                for g in range(2):
                    down_mm.wait(ve, i, g + 1)
                    nc.vector.scalar_tensor_tensor(out=yo[:, 2 * g:2 * g + 2, :],
                                                   in0=pd[g][:, :].rearrange("p (n h) -> p n h", n=2), scalar=sgd[:, 0:1],
                                                   in1=xn[:, 2 * g:2 * g + 2, :], op0=ALU.mult, op1=ALU.add)\
                        .then_inc(y_ready.sem, 1)
                y_ready.wait(ve, i, 2)
                stored[p].wait(ve, i // 2 - 1, 16)
                norm(i, 1, yo[:, :, :], yo[:, :, :], ob[p][:, :, :])
            loop(ve, body)


def constants():
    i = np.arange(128)
    masks = np.zeros((128, LEVELS, 128), np.uint16)
    for l in range(LEVELS):
        s = 2 << l
        same = (i[:, None] // (2 * s)) == (i[None, :] // (2 * s))
        masks[:, l, :] = same & (i[:, None] % (2 * s) >= s) & (i[None, :] % (2 * s) < s)
    mask2 = -np.eye(128) + ((i[:, None] // 2 == i[None, :] // 2) & (i[:, None] < i[None, :]))
    neg = np.where(i[None, :] < i[:, None], -1e30, 0.0)
    return {
        "ident": np.eye(128, dtype=np.float32),
        "triu": (i[:, None] <= i[None, :]).astype(np.float32),
        "neg": neg.astype(np.float32),
        "masks": masks,
        "mask2": mask2.astype(np.float16),
        "expo_eps": np.broadcast_to(np.array([-0.5, EPS, EPS * D, EPS, LN_EPS], np.float32)[None, :, None], (128, 5, NC)),
    }


def kernel(L0_attn_hidden_states, L0_attn_W_qkvz, L0_attn_W_ba, L0_attn_conv_weight, L0_attn_A_log, L0_attn_dt_bias,
           L0_attn_norm_weight, L0_attn_W_out, L0_ffn_W_up, L0_ffn_W_gate, L0_ffn_W_down):
    import concourse.bacc as bacc
    from concourse.bass_utils import run_bass_kernel_spmd
    x = np.asarray(L0_attn_hidden_states)
    w = np.asarray(L0_attn_W_qkvz).reshape(H, NK, WCOL)
    w = np.concatenate([w[..., D:2 * D], w[..., 0:D], w[..., 2 * D:]], -1).reshape(H, NK * WCOL)
    wba = np.asarray(L0_attn_W_ba).reshape(H, NK, 2, R).transpose(0, 2, 1, 3).reshape(H, 2 * NV)
    cwt = np.asarray(L0_attn_conv_weight)
    q, k, v = cwt[:NK * D].reshape(NK, 1, D, TAPS), cwt[NK * D:2 * NK * D].reshape(NK, 1, D, TAPS), cwt[2 * NK * D:].reshape(NK, R, D, TAPS)
    cwt = np.concatenate([k, q, v], 1).transpose(2, 0, 1, 3).reshape(D, NK, 4 * TAPS)
    arrays = {
        "xT": x.transpose(0, 2, 1).reshape(B, KT, 128, S),
        "x_tok": x.reshape(B * S, H),
        "Wqkvz": w, "Wba": wba, "convw": cwt,
        "A_log": L0_attn_A_log, "dt_bias": L0_attn_dt_bias, "norm_weight": L0_attn_norm_weight, "W_out": L0_attn_W_out,
        "WupT": np.asarray(L0_ffn_W_up).T, "WgateT": np.asarray(L0_ffn_W_gate).T, "WdownT": np.asarray(L0_ffn_W_down).T,
    }
    arrays.update(constants())
    arrays = {f"in_{n}": np.ascontiguousarray(a) for n, a in arrays.items()}
    nc = bacc.Bacc("TRN2", target_bir_lowering=False, num_devices=1)
    io = {n[3:]: nc.dram_tensor(n, a.shape, mybir.dt.from_np(a.dtype), kind="ExternalInput").ap() for n, a in arrays.items()}
    io["out"] = nc.dram_tensor("out", (B * S, H), f32, kind="ExternalOutput").ap()
    build(nc, io)
    r = run_bass_kernel_spmd(nc, [arrays], core_ids=[0])
    return r.results[0]["out"].reshape(B, S, H)
```

```python
import numpy as np
import concourse.bass as bass
from concourse import mybir
from contextlib import ExitStack

B, S, H = 8, 512, 256
NK, R, D = 16, 2, 128
NV = NK * R
KT = H // 128
C = 128
NC = S // C
NB = B * NC
NU = NC * R
TAPS = 4
WCOL = 2 * D + 2 * R * D
ITS = NK * B
LEVELS = 6
E = 1024
ET = E // 128
ESC = 256.0
KINDS = 3
SMALL = NC * KINDS * R
EPS, LN_EPS, TERN_EPS = 1e-6, 1e-5, 1e-8

f32, f16, bf16, u16 = mybir.dt.float32, mybir.dt.float16, mybir.dt.bfloat16, mybir.dt.uint16
ALU, ACT, AX = mybir.AluOpType, mybir.ActivationFunctionType, mybir.AxisListType
ds = bass.ds


class Signal:

    def __init__(self, nc, ctx, name, per=1):
        self.sem, self.per = ctx.enter_context(nc.semaphore(name)), per

    def wait(self, engine, it, n):
        if isinstance(it, int) and it < 0:
            return
        engine.wait_ge(self.sem, it * self.per + n)


def build(nc, io):
    with ExitStack() as ctx:
        def sb(name, shape, dt=f32):
            return ctx.enter_context(nc.sbuf_tensor(name, shape, dt))
        m = {
            "yacc": sb("yacc", [128, NB, H]),
            "ident": sb("ident", [128, 128]),
        }
        with ExitStack() as attention:
            def sa(name, shape, dt=f32):
                return attention.enter_context(nc.sbuf_tensor(name, shape, dt))
            m["wout"] = sa("wout", [128, NV, H])
            m["vec"] = sa("vec", [128, ITS, SMALL])
            m["cw"] = sa("cw", [128, NK, 4 * TAPS])
            m["rows_dram"] = nc.dram_tensor("rows_scratch", (ITS, 2, 3, R, S), bf16, kind="Internal").ap()
            gates(nc, io, m)
            delta_rule(nc, io, m)
        feed_forward(nc, io, m)


def gates(nc, io, m):
    yacc, ident, wout, vec, cw, rows_dram = (m[k] for k in ("yacc", "ident", "wout", "vec", "cw", "rows_dram"))
    with ExitStack() as ctx:
        def sb(name, shape, dt=f32):
            return ctx.enter_context(nc.sbuf_tensor(name, shape, dt))

        def signal(name, per=1):
            return Signal(nc, ctx, name, per)
        wba = sb("wba", [128, KT, 2 * NV])
        xb = sb("gxb", [128, KT, S])
        nwt = sb("nwt", [128, 1])
        na = sb("na", [128, NV])
        dtb = sb("dtb", [128, NV])
        triu = sb("triu", [128, 128])
        ones = sb("ones", [128, 128])
        identb = sb("gidentb", [128, 128], bf16)
        ba = sb("ba", [128, NB, 2, NV])
        e = sb("ge", [128, NB, 2, NV])
        s = sb("gs", [128, NB, 2, NV])
        s2 = sb("gs2", [128, NB, 2, NV])
        p = sb("gp", [128, NB, 2, NV])
        sp_ = sb("gsoft", [128, NB, 2, NV])
        graw = sb("graw", [128, NB, NV])
        gs = sb("gcum", [128, NB, NV])
        gl = sb("glast", [128, NB, NV])
        hj = sb("ghj", [128, NB, NV])
        dl = sb("gdl", [128, NB, NV])
        r1 = sb("gr1", [128, NB, NV])
        parts = sb("parts", [128, NB, 2, 3, NV], bf16)
        rows = sb("rows", [3 * NV, 2, NB * C], bf16)
        pz = ctx.enter_context(nc.psum_tensor("pz", [128, 512], f32))
        pg = [ctx.enter_context(nc.psum_tensor(f"pg{i}", [128, 512], f32)) for i in range(4)]
        pt = [ctx.enter_context(nc.psum_tensor(f"pt{i}", [128, 1024], bf16)) for i in range(2)]

        consts_in, x_in = signal("g_consts_in", 16), signal("g_x_in", 16)
        made_ones, made_identb = signal("g_ones"), signal("g_identb")
        ba_mm, ba_out, x_ready, abs_ready, exp_a, exp_abs = (signal(f"g_{n}") for n in ("ba_mm", "ba_out", "x", "abs", "expa", "expabs"))
        graw_ready, cum_mm, cum_out, dl_ready, parts_ready = (signal(f"g_{n}") for n in ("graw", "cum_mm", "cum_out", "dl", "parts"))
        turn_mm, turn_out, rows_out, chain = signal("g_turn_mm"), signal("g_turn_out"), signal("g_rows_out", 16), signal("g_chain")
        NTURN = 2 * NB // 4
        block = ctx.enter_context(nc.Block())
        loads = [
            (wba[:, :, :], io["Wba"].rearrange("(k p) n -> p k n", p=128)),
            (dtb[:, :], io["dt_bias"].rearrange("(a n) -> a n", a=1).broadcast_to([128, NV])),
            (na[:, :], io["A_log"].rearrange("(a n) -> a n", a=1).broadcast_to([128, NV])),
            (nwt[:, :], io["norm_weight"].rearrange("(p a) -> p a", a=1)),
            (triu[:, :], io["triu"]),
            (ident[:, :], io["ident"]),
            (cw[:, :, :], io["convw"]),
            (wout[:, :, :], io["W_out"].rearrange("(h p) n -> p h n", p=128)),
            (yacc[:, 0:NB // 2, :], io["x_tok"].rearrange("(n p) h -> p n h", p=128)[:, 0:NB // 2, :]),
            (yacc[:, NB // 2:NB, :], io["x_tok"].rearrange("(n p) h -> p n h", p=128)[:, NB // 2:NB, :]),
        ]
        LOADED = 16 * len(loads)

        @block.sync
        def _(sp):
            for dst, src in loads:
                sp.dma_start(dst, src).then_inc(consts_in.sem, 16)
            sp.dma_start(xb[:, :, :], io["xT"][0].rearrange("k p n -> p k n")).then_inc(x_in.sem, 16)
            with sp.Fori(1, B) as b:
                ba_mm.wait(sp, b, 0)
                sp.dma_start(xb[:, :, :], io["xT"][ds(b, 1), :, :, :].rearrange("a k p n -> p (a k) n")).then_inc(x_in.sem, 16)
            sp.wait_ge(turn_out.sem, NTURN)
            dst = rows_dram.rearrange("(k b) w q h s -> w q k h b s", b=B)
            for w in range(2):
                for q in range(3):
                    for k in range(NK):
                        sp.dma_start(dst[w, q, k], rows[q * NV + k * R:q * NV + (k + 1) * R, w, :]
                                     .rearrange("h (b s) -> h b s", b=B)).then_inc(rows_out.sem, 16)
            sp.wait_ge(rows_out.sem, 6 * NK * 16)

        @block.tensor
        def _(pe):
            pe.wait_ge(consts_in.sem, LOADED)

            def project(b):
                x_in.wait(pe, b, 16)
                ba_out.wait(pe, b - 1, 1)
                for n in range(NC):
                    for k in range(KT):
                        last = nc.tensor.matmul(pz[:, n * 2 * NV:(n + 1) * 2 * NV], xb[:, k, n * C:(n + 1) * C],
                                                wba[:, k, :], start=(k == 0), stop=(k == KT - 1))
                last.then_inc(ba_mm.sem, 1)
            project(0)
            with pe.Fori(1, B) as b:
                project(b)
            pe.wait_ge(made_ones.sem, 1)
            pe.wait_ge(graw_ready.sem, 1)
            for h in range(2):
                rhs = graw[:, h * NB // 2:(h + 1) * NB // 2, :].rearrange("p b h -> p (b h)")
                nc.tensor.matmul(pg[h][:, :], triu[:, :], rhs, start=True, stop=True)
                nc.tensor.matmul(pg[2 + h][:, :], ones[:, :], rhs, start=True, stop=True).then_inc(cum_mm.sem, 1)
            pe.wait_ge(made_identb.sem, 1)
            for g in range(NTURN):
                w, n0 = g % 2, g // 2 * 4
                pe.wait_ge(parts_ready.sem, w + 1)
                if g >= 2:
                    pe.wait_ge(turn_out.sem, g - 1)
                for n in range(4):
                    last = nc.tensor.transpose(pt[g % 2][0:3 * NV, n * C:(n + 1) * C],
                                               parts[:, n0 + n, w, :, :].rearrange("p q h -> p (q h)"), identb[:, :])
                last.then_inc(turn_mm.sem, 1)

        @block.scalar
        def _(act):
            act.wait_ge(consts_in.sem, LOADED)
            nc.scalar.activation(na[:, :], na[:, :], ACT.Exp).then_inc(exp_a.sem, 1)
            act.wait_ge(x_ready.sem, 1)
            nc.scalar.activation(e[:, :, :, :], ba[:, :, :, :], ACT.Abs).then_inc(abs_ready.sem, 1)
            act.wait_ge(abs_ready.sem, 1)
            nc.scalar.activation(e[:, :, :, :], e[:, :, :, :], ACT.Exp, scale=-1.0).then_inc(exp_abs.sem, 1)
            act.wait_ge(cum_out.sem, 2)
            act.wait_ge(dl_ready.sem, 1)
            for kind, src in enumerate((gs, dl, gl)):
                for b in range(B):
                    for h in range(R):
                        o = vec[:, :, :].rearrange("p (k b) (n q h) -> p b q h n k", b=B, n=NC, q=KINDS)[:, b, kind, h]
                        i = src[:, :, :].rearrange("p (b n) (k h) -> p b h n k", b=B, h=R)[:, b, h]
                        nc.scalar.activation(o, i, ACT.Exp)
            for g in range(NTURN):
                w, n0 = g % 2, g // 2 * 4
                act.wait_ge(turn_mm.sem, g + 1)
                nc.scalar.activation(rows[:, w, n0 * C:(n0 + 4) * C], pt[g % 2][0:3 * NV, 0:4 * C],
                                     ACT.Copy).then_inc(turn_out.sem, 1)

        @block.vector
        def _(ve):
            links = [0]

            def link(ins):
                links[0] += 1
                ins.then_inc(chain.sem, 1)
                ve.wait_ge(chain.sem, links[0])
            nc.vector.memset(ones[:, :], 1.0).then_inc(made_ones.sem, 1)
            ve.wait_ge(consts_in.sem, LOADED)
            nc.vector.tensor_copy(identb[:, :], ident[:, :]).then_inc(made_identb.sem, 1)
            nc.vector.tensor_scalar(wout[:, :, :], wout[:, :, :], nwt[:, 0:1], None, ALU.mult)

            def take(b):
                ba_mm.wait(ve, b, 1)
                nc.vector.tensor_copy(ba[:, ds(b * NC, NC), :, :].rearrange("p n a h -> p (n a h)"),
                                      pz[:, 0:NC * 2 * NV]).then_inc(ba_out.sem, 1)
            take(0)
            with ve.Fori(1, B) as b:
                take(b)
            ve.wait_ge(ba_out.sem, B)
            bb, aa = ba[:, :, 0, :], ba[:, :, 1, :]
            nc.vector.tensor_scalar(bb, bb, -1.0, None, ALU.mult)
            nc.vector.tensor_tensor(aa, aa, dtb[:, None, :].broadcast_to([128, NB, NV]), ALU.add).then_inc(x_ready.sem, 1)
            ve.wait_ge(x_ready.sem, 1)
            ve.wait_ge(exp_abs.sem, 1)
            link(nc.vector.tensor_scalar(s[:, :, :, :], e[:, :, :, :], 2.0, None, ALU.add))
            link(nc.vector.reciprocal(s[:, :, :, :], s[:, :, :, :]))
            link(nc.vector.tensor_tensor(s[:, :, :, :], s[:, :, :, :], e[:, :, :, :], ALU.mult))
            link(nc.vector.tensor_tensor(s2[:, :, :, :], s[:, :, :, :], s[:, :, :, :], ALU.mult))
            link(nc.vector.tensor_scalar(p[:, :, :, :], s2[:, :, :, :], 1.0 / 15, None, ALU.mult))
            for k in (13, 11, 9, 7, 5, 3):
                link(nc.vector.scalar_tensor_tensor(out=p[:, :, :, :], in0=p[:, :, :, :], scalar=1.0 / k,
                                                    in1=s2[:, :, :, :], op0=ALU.add, op1=ALU.mult))
            link(nc.vector.scalar_tensor_tensor(out=p[:, :, :, :], in0=p[:, :, :, :], scalar=1.0,
                                                in1=s[:, :, :, :], op0=ALU.add, op1=ALU.mult))
            link(nc.vector.tensor_scalar(sp_[:, :, :, :], ba[:, :, :, :], 0.0, None, ALU.max))
            link(nc.vector.scalar_tensor_tensor(out=sp_[:, :, :, :], in0=p[:, :, :, :], scalar=2.0,
                                                in1=sp_[:, :, :, :], op0=ALU.mult, op1=ALU.add))
            ve.wait_ge(exp_a.sem, 1)
            nc.vector.scalar_tensor_tensor(out=graw[:, :, :], in0=sp_[:, :, 1, :], scalar=-1.0,
                                           in1=na[:, None, :].broadcast_to([128, NB, NV]),
                                           op0=ALU.mult, op1=ALU.mult).then_inc(graw_ready.sem, 1)
            for h in range(2):
                ve.wait_ge(cum_mm.sem, h + 1)
                n = slice(h * NB // 2, (h + 1) * NB // 2)
                nc.vector.tensor_copy(gs[:, n, :].rearrange("p b h -> p (b h)"), pg[h][:, :])
                nc.vector.tensor_copy(gl[:, n, :].rearrange("p b h -> p (b h)"), pg[2 + h][:, :]).then_inc(cum_out.sem, 1)
            ve.wait_ge(cum_out.sem, 2)
            link(nc.vector.scalar_tensor_tensor(out=hj[:, :, :], in0=sp_[:, :, 0, :], scalar=-1.0, in1=gs[:, :, :],
                                                op0=ALU.mult, op1=ALU.subtract))
            nc.vector.tensor_tensor(dl[:, :, :], hj[:, :, :], gl[:, :, :], ALU.add).then_inc(dl_ready.sem, 1)
            for w, src in enumerate((hj, gs)):
                link(nc.vector.tensor_copy(parts[:, :, w, 0, :], src[:, :, :]))
                link(nc.vector.tensor_tensor(r1[:, :, :], src[:, :, :], parts[:, :, w, 0, :], ALU.subtract))
                link(nc.vector.tensor_copy(parts[:, :, w, 1, :], r1[:, :, :]))
                link(nc.vector.tensor_tensor(r1[:, :, :], r1[:, :, :], parts[:, :, w, 1, :], ALU.subtract))
                nc.vector.tensor_copy(parts[:, :, w, 2, :], r1[:, :, :]).then_inc(parts_ready.sem, 1)
                if w == 0:
                    ve.wait_ge(parts_ready.sem, 1)


def delta_rule(nc, io, m):
    yacc, ident, wout, vec, cw, rows_dram = (m[k] for k in ("yacc", "ident", "wout", "vec", "cw", "rows_dram"))
    with ExitStack() as ctx:
        def sb(name, shape, dt=f32):
            return ctx.enter_context(nc.sbuf_tensor(name, shape, dt))

        def signal(name, per=1):
            return Signal(nc, ctx, name, per)
        ident16 = sb("ident16", [128, 128], f16)
        identb = sb("identb", [128, 128], bf16)
        ident_esc = sb("ident_esc", [128, 128])
        neg = sb("neg", [128, 4, 128], bf16)
        masks = sb("masks", [128, LEVELS, 128], u16)
        mask2 = sb("mask2", [128, 128], f16)
        expo_eps = sb("expo_eps", [128, 5, NC])
        wb = sb("wb", [128, KT, WCOL])
        xb = sb("xb", [128, KT, S])
        small = [sb(f"small{p}", [128, NC, KINDS, R]) for p in range(2)]
        cws = [sb(f"cws{p}", [128, 4 * TAPS]) for p in range(2)]
        lrow = [sb(f"lrow{p}", [6, R, NC, C], bf16) for p in range(2)]
        rrow = [sb(f"rrow{p}", [6, R, NC, C], bf16) for p in range(2)]
        conv = [sb(f"conv{c}", [128, S]) for c in range(4)]
        junk = sb("junk", [128, 4 * NC, C], bf16)
        ssq = sb("ssq", [128, 2, NC])
        ssqe = sb("ssqe", [128, 2, NC])
        rn = sb("rn", [128, 2, NC])
        tokn = [sb(f"tokn{c}", [128, NC, D]) for c in range(2)]
        kq = [sb(f"kq{p}", [128, NC, 2, C]) for p in range(2)]
        vt = [sb(f"vt{p}", [128, NC, R, D]) for p in range(2)]
        zs = [sb(f"zs{p}", [128, NC, R, D]) for p in range(2)]
        kw = [sb(f"kw{p}", [128, NC, R, D]) for p in range(2)]
        et = sb("et", [128, NU, C])
        a32 = sb("a32", [128, NU, C])
        a16 = sb("a16", [128, NU, C], f16)
        u16_ = sb("u16", [128, NU, C], f16)
        t16_ = sb("t16", [128, NU, C], f16)
        a_low = sb("a_low", [128, NU, C], bf16)
        pl = [sb(f"pl{l}", [128, NU, C], f16) for l in range(LEVELS)]
        e16 = sb("e16", [128, NU, C], f16)
        u32 = [sb(f"u32{p}", [128, NU, C]) for p in range(2)]
        attn = [sb(f"attn{p}", [128, NU, C]) for p in range(2)]
        st = sb("st", [128, R, D])
        res = sb("res", [128, R, D])
        yb = sb("yb", [128, R, D])
        qe = sb("qe", [128, R, D])
        xo = sb("xo", [128, NC, R, D])
        rs = sb("rs", [128, NU])
        rse = sb("rse", [128, NU])
        rr = sb("rr", [128, NU])
        xt = sb("xt", [128, NU, C])
        pa = [ctx.enter_context(nc.psum_tensor(f"pa{i}", [128, 512], f32)) for i in range(4)]
        pb = [ctx.enter_context(nc.psum_tensor(f"pb{i}", [128, 512], f32)) for i in range(4)]

        def unit(n, h):
            return n * R + h

        def convolved(c):
            return 6 * (c // 2) + 5 + c % 2

        def four(bank):
            return bank[:, :].rearrange("p (n c) -> p n c", n=4)

        def group(t, g):
            return t[:, 4 * g:4 * g + 4, :]

        def per_head(x):
            return x[:, :, None, :].broadcast_to([128, 2, R, C])

        consts_in, made, preset = signal("consts_in", 16), signal("made"), signal("preset")
        w_in, x_in, small_ready = signal("w_in", 16), signal("x_in", 16), signal("small_ready")
        rows_in = [signal(f"rows_in{p}", 32) for p in range(2)]
        proj_mm, tap_first, tapped, silued, z_ready = signal("proj_mm", 6), signal("tap_first", 4), signal("tapped", 12), signal("silued", 4), signal("z_ready", 2)
        turn_mm, squares, eps_in, rnorm, normed = signal("turn_mm", 4), signal("squares", 2), signal("eps_in", 2), signal("rnorm", 2), signal("normed", 2)
        back_mm, kq_ready, vt_ready, kw_ready = signal("back_mm", 2), signal("kq_ready", 2), signal("vt_ready", 2), signal("kw_ready", 2)
        gram_mm, decay_mm, decay_ready, attn_ready, sys_ready, sys_diag, sys_rounded = (
            signal(n, 2) for n in ("gram_mm", "decay_mm", "decay_ready", "attn_ready", "sys_ready", "sys_diag", "sys_rounded"))
        u_first, t_first_mm, p_mm, p_ready, t_mm, u_mm = signal("u_first", 2), signal("t_first_mm", 2), signal("p_mm", 12), signal("p_ready", 12), signal("t_mm", 12), signal("u_mm", 12)
        u_ready = [signal(f"u_ready{g}", LEVELS) for g in range(2)]
        t_ready = [signal(f"t_ready{g}", LEVELS + 1) for g in range(2)]
        low_ready, resid_mm, resid_ready, fix_mm, inv_ready = (signal(n, 2) for n in ("low_ready", "resid_mm", "resid_ready", "fix_mm", "inv_ready"))
        ks_mm, qs_mm, res_ready, y_mm, y_ready, upd_mm, intra_mm, qe_ready, st_ready, o_ready = (
            signal(*a) for a in (("ks_mm", 3), ("qs_mm", 3), ("res_ready", 4), ("y_mm", 4), ("y_ready", 4), ("upd_mm", 3),
                                 ("intra_mm", 4), ("qe_ready", 3), ("st_ready", 3), ("o_ready", 4)))
        gated, o_squares, o_eps, o_rnorm, o_normed, o_turn_mm, xt_ready, out_mm, added = (
            signal(n, 2) for n in ("gated", "o_squares", "o_eps", "o_rnorm", "o_normed", "o_turn_mm", "xt_ready", "out_mm", "added"))
        passed = [signal(f"passed{i}") for i in range(2)]
        block = ctx.enter_context(nc.Block())
        NCONST = 4
        MADE = 6

        @block.sync
        def _(sp):
            sp.dma_start(et[:, 0, :], io["neg"]).then_inc(consts_in.sem, 16)
            sp.dma_start(masks[:, :, :], io["masks"]).then_inc(consts_in.sem, 16)
            sp.dma_start(mask2[:, :], io["mask2"]).then_inc(consts_in.sem, 16)
            sp.dma_start(expo_eps[:, :, :], io["expo_eps"]).then_inc(consts_in.sem, 16)

            def load(a, p):
                proj_mm.wait(sp, a - 1, 6)
                sp.dma_start(wb[:, :, :], io["Wqkvz"].rearrange("(k p) (h n) -> h p k n", p=128, h=NK)[ds(a // B, 1)]
                             .rearrange("a p k n -> p (a k) n")).then_inc(w_in.sem, 16)
                sp.dma_start(xb[:, :, :], io["xT"][ds(a % B, 1)].rearrange("a k p n -> p (a k) n")).then_inc(x_in.sem, 16)
                decay_mm.wait(sp, a - 2, 2)
                sp.dma_start(lrow[p][3:6], rows_dram[ds(a, 1), 0].rearrange("a q h s -> (a q) h s")
                             .rearrange("q h (n c) -> q h n c", n=NC)).then_inc(rows_in[p].sem, 16)
                sp.dma_start(rrow[p][0:3], rows_dram[ds(a, 1), 1].rearrange("a q h s -> (a q) h s")
                             .rearrange("q h (n c) -> q h n c", n=NC)).then_inc(rows_in[p].sem, 16)
            made.wait(sp, 0, MADE)
            load(0, 0)
            load(1, 1)
            with sp.Fori(1, ITS // 2) as j:
                load(2 * j, 0)
                load(2 * j + 1, 1)

        def late(*names):
            return [("late", *name) for name in names]

        def early(*names):
            return [("early", *name) for name in names]

        def back(*names):
            return [("back", *name) for name in names]
        g0, g1 = 0, 1
        K, Q, V0, V1 = range(4)

        def level(l, *between):
            chain = l < NC
            return (late(("p_mm", l)) + (back(("qs_mm", l)) if l and chain else []) + (back(("y", l), ("y_copy", l)) if chain else [])
                    + (back(("q_part", l)) if l and chain else []) + late(("p", l), ("ut_mm", 2 * l)) + (back(("update_mm", l)) if l < NC - 1 else [])
                    + late(("ut_mm", 2 * l + 1)) + (back(("intra_mm", l)) if chain else []) + sum(between, []) + late(("ut", l))
                    + (back(("state", l), ("ks_mm", l + 1)) if l < NC - 1 else []) + (back(("out", l)) if chain else [])
                    + (back(("residual", l + 1)) if l < NC - 1 else []))
        ORDER = (
            late(("low", g0), ("low", g1)) + level(0, early(("decay_mm", g0))) + early(("decay", g0)) + level(1, early(("decay_mm", g1))) + back(("gate", g0))
            + early(("decay", g1)) + level(2) + back(("o_square", g0), ("o_rnorm", g0))
            + level(3) + back(("gate", g1), ("o_norm", g0)) + early(("small", 0)) + late(("p_mm", 4))
            + early(("project", K)) + late(("p", 4), ("ut_mm", 8), ("ut_mm", 9)) + early(("tap", K)) + late(("ut", 4))
            + back(("o_turn", g0), ("x_copy", g0)) + late(("p_mm", 5)) + early(("project", Q)) + late(("p", 5), ("ut_mm", 10), ("ut_mm", 11))
            + early(("tap", Q), ("conv", 0)) + late(("ut", 5)) + back(("o_square", g1), ("o_rnorm", g1)) + early(("conv", 1), ("project", V0))
            + late(("resid_mm", g0), ("resid_mm", g1), ("resid", g0), ("resid", g1)) + back(("out_mm", g0)) + early(("conv", 2), ("tap", V0)) + back(("o_norm", g1), ("added", g0))
            + early(("silu", K), ("silu", Q)) + late(("fix_mm", g0), ("fix_mm", g1), ("fix", g0), ("fix", g1)) + early(("project", V1))
            + early(("tap", V1), ("turn", K), ("turn", Q), ("squares", K), ("squares", Q), ("conv", 3), ("project_z", g0), ("project_z", g1))
            + early(("rnorm", K), ("rnorm", Q), ("conv", 4), ("normed", K), ("normed", Q), ("conv", 5)) + back(("o_turn", g1), ("x_copy", g1))
            + early(("z", g0), ("z", g1), ("back", K), ("kq", K), ("back", Q), ("kq", Q), ("kw", 0))
            + early(("gram", g0), ("gram", g1)) + early(("silu", V0), ("silu", V1), ("system", g0), ("diagonal", g0), ("system", g1), ("diagonal", g1))
            + early(("turn", V0), ("turn", V1), ("rounded", g0), ("vt", 0), ("rounded", g1), ("vt", 1), ("attn", g0), ("u_first", g0), ("u_first", g1), ("attn", g1))
            + back(("out_mm", g1)) + early(("t_first", g0), ("t_first", g1)) + back(("added", g1))
        )
        LAST = ITS - 1

        def steps(engine, **parts):
            def step(s, p, streams=("late", "early", "back")):
                at = {"late": (s, p), "early": (s + 1, 1 - p), "back": (s - 1, 1 - p)}
                for stream, stage, n in ORDER:
                    if stream in streams and stage in parts:
                        parts[stage](*at[stream], n)
            step(-1, 1, ("early",))
            step(0, 0, ("late", "early"))
            step(1, 1)
            with engine.Fori(1, ITS // 2 - 1) as j:
                step(2 * j, 0)
                step(2 * j + 1, 1)
            step(LAST - 1, 0)
            step(LAST, 1, ("late", "back"))
            step(LAST + 1, 0, ("back",))

        proj_bank = (pb[0], pb[1], pb[2], pa[0], pa[2], pa[1])
        turn_bank = (pb[0], pb[1], pa[3], pb[2])

        def more(b):
            return not (isinstance(b, int) and b == LAST)

        @block.tensor
        def _(pe):
            made.wait(pe, 0, MADE)

            def project(a, p, c):
                if c == K:
                    w_in.wait(pe, a, 16)
                    x_in.wait(pe, a, 16)
                    y_ready.wait(pe, a - 2, NC)
                if c == Q:
                    o_ready.wait(pe, a - 2, NC)
                if c == V0:
                    st_ready.wait(pe, a - 2, NC - 1)
                if c == V1:
                    resid_ready.wait(pe, a - 1, 1)
                for k in range(KT):
                    last = nc.tensor.matmul(proj_bank[c][:, :], wb[:, k, c * D:(c + 1) * D], xb[:, k, :],
                                            start=(k == 0), stop=(k == KT - 1))
                last.then_inc(proj_mm.sem, 1)

            def project_z(a, p, g):
                (resid_ready if g == 0 else inv_ready).wait(pe, a - 1, 2 if g == 0 else 1)
                for n in range(2):
                    for k in range(KT):
                        last = nc.tensor.matmul(proj_bank[4 + g][:, n * R * D:(n + 1) * R * D],
                                                xb[:, k, (2 * g + n) * C:(2 * g + n + 1) * C],
                                                wb[:, k, 4 * D:4 * D + R * D], start=(k == 0), stop=(k == KT - 1))
                last.then_inc(proj_mm.sem, 1)

            def turn(a, p, c):
                silued.wait(pe, a, c + 1)
                if c == V0:
                    inv_ready.wait(pe, a - 1, 2)
                for n in range(NC):
                    last = nc.tensor.transpose(turn_bank[c][:, n * C:(n + 1) * C], conv[c][:, n * C:(n + 1) * C], ident[:, :])
                last.then_inc(turn_mm.sem, 1)

            def back_turn(a, p, c):
                normed.wait(pe, a, c + 1)
                for n in range(NC):
                    last = nc.tensor.transpose(turn_bank[c][:, n * C:(n + 1) * C], tokn[c][:, n, :], ident[:, :])
                last.then_inc(back_mm.sem, 1)

            def gram(a, p, g):
                kq_ready.wait(pe, a, 2)
                if g == 0:
                    tapped.wait(pe, a, convolved(V1))
                else:
                    z_ready.wait(pe, a, 2)
                for n in range(2):
                    nn = 2 * g + n
                    last = nc.tensor.matmul(pa[g][:, n * 2 * C:(n + 1) * 2 * C], kq[p][:, nn, 0, :],
                                            kq[p][:, nn, :, :], start=True, stop=True)
                last.then_inc(gram_mm.sem, 1)

            def decay_product(a, p, g):
                if g == 0:
                    rows_in[p].wait(pe, a // 2, 32)
                    added.wait(pe, a - 3, 2)
                else:
                    decay_ready.wait(pe, a, 1)
                nc.tensor.matmul(pb[3][:, :], identb[:, :], neg[:, :, :].rearrange("p u c -> p (u c)"),
                                 start=True, stop=True)
                for n in range(2):
                    for h in range(R):
                        u = n * R + h
                        last = nc.tensor.matmul(pb[3][:, u * C:(u + 1) * C], lrow[p][:, h, 2 * g + n, :],
                                                rrow[p][:, h, 2 * g + n, :], start=False, stop=True,
                                                skip_group_check=True)
                last.then_inc(decay_mm.sem, 1)

            def t_first(a, p, g):
                u_first.wait(pe, a, g + 1)
                if g == 0:
                    attn_ready.wait(pe, a, 1)
                else:
                    z_ready.wait(pe, a, 1)
                for u in range(4):
                    last = nc.tensor.transpose(pa[2 * g][:, :].bitcast(f16)[:, u * C:(u + 1) * C],
                                               u16_[:, 4 * g + u, :], ident16[:, :])
                last.then_inc(t_first_mm.sem, 1)

            def p_product(a, p, l):
                for g in range(2):
                    t_ready[g].wait(pe, a, l + 1)
                    if l == 0 and g == 0:
                        attn_ready.wait(pe, a, 2)
                    if l == 0 and g == 1:
                        vt_ready.wait(pe, a, 1)
                    for u in range(4):
                        last = nc.tensor.matmul(pa[2 * g + 1][:, u * C:(u + 1) * C], a16[:, 4 * g + u, :],
                                                t16_[:, 4 * g + u, :], start=True, stop=True)
                    last.then_inc(p_mm.sem, 1)

            def ut_product(a, p, i):
                l, g = i // 2, i % 2
                p_ready.wait(pe, a, i + 1)
                if l:
                    u_ready[g].wait(pe, a, l)
                for u in range(4):
                    last = nc.tensor.matmul(pa[2 * g + 1][:, u * C:(u + 1) * C], u16_[:, 4 * g + u, :],
                                            pl[l][:, 4 * g + u, :], start=True, stop=True)
                last.then_inc(t_mm.sem, 1)
                for u in range(4):
                    last = nc.tensor.matmul(pa[2 * g][:, u * C:(u + 1) * C], pl[l][:, 4 * g + u, :], u16_[:, 4 * g + u, :],
                                            start=True, stop=True)
                last.then_inc(u_mm.sem, 1)

            def resid_product(a, p, g):
                t_ready[g].wait(pe, a, LEVELS + 1)
                u_ready[g].wait(pe, a, LEVELS)
                low_ready.wait(pe, a, g + 1)
                for u in range(4):
                    for part in range(2):
                        last = nc.tensor.matmul(pa[2 * g][:, u * C:(u + 1) * C], (a16, a_low)[part][:, 4 * g + u, :],
                                                t16_[:, 4 * g + u, :], start=(part == 0), stop=(part == 1))
                last.then_inc(resid_mm.sem, 1)

            def fix_product(a, p, g):
                resid_ready.wait(pe, a, g + 1)
                for u in range(4):
                    last = nc.tensor.matmul(pa[2 * g + 1][:, u * C:(u + 1) * C], e16[:, 4 * g + u, :],
                                            u16_[:, 4 * g + u, :], start=True, stop=True)
                last.then_inc(fix_mm.sem, 1)

            def keys_state(b, p, n):
                st_ready.wait(pe, b, n)
                y_ready.wait(pe, b, n)
                nc.tensor.matmul(pb[0][:, 0:R * D], kq[p][:, n, 0, :], st[:, :, :], start=True, stop=True)\
                    .then_inc(ks_mm.sem, 1)

            def queries_state(b, p, n):
                st_ready.wait(pe, b, n)
                o_ready.wait(pe, b, n)
                nc.tensor.matmul(pb[1][:, 0:R * D], kq[p][:, n, 1, :], st[:, :, :], start=True, stop=True)\
                    .then_inc(qs_mm.sem, 1)

            def y(b, p, n):
                res_ready.wait(pe, b, n + 1)
                if n == 0:
                    inv_ready.wait(pe, b, 2)
                    if more(b):
                        kq_ready.wait(pe, b + 1, 1)
                for h in range(R):
                    last = nc.tensor.matmul(pb[0][:, h * D:(h + 1) * D], u32[p][:, unit(n, h), :], res[:, h, :],
                                            start=True, stop=True)
                last.then_inc(y_mm.sem, 1)

            def update_product(b, p, n):
                y_ready.wait(pe, b, n + 1)
                if n == 0:
                    kw_ready.wait(pe, b, 2)
                    if more(b):
                        vt_ready.wait(pe, b + 1, 2)
                else:
                    st_ready.wait(pe, b, n)
                for h in range(R):
                    last = nc.tensor.matmul(pb[2][:, h * D:(h + 1) * D], kw[p][:, n, h, :], yb[:, h, :],
                                            start=True, stop=True)
                last.then_inc(upd_mm.sem, 1)

            def intra_product(b, p, n):
                y_ready.wait(pe, b, n + 1)
                if n == 0:
                    attn_ready.wait(pe, b, 2)
                    if more(b):
                        kq_ready.wait(pe, b + 1, 2)
                else:
                    qe_ready.wait(pe, b, n)
                for h in range(R):
                    last = nc.tensor.matmul(pb[1][:, h * D:(h + 1) * D], attn[p][:, unit(n, h), :], yb[:, h, :],
                                            start=True, stop=True)
                last.then_inc(intra_mm.sem, 1)

            def o_turn(b, p, g):
                o_normed.wait(pe, b, g + 1)
                if g:
                    added.wait(pe, b, 1)
                elif not isinstance(b, int) or b + 2 <= LAST:
                    decay_ready.wait(pe, b + 2, 2)
                else:
                    added.wait(pe, b - 1, 2)
                for u in range(4):
                    last = nc.tensor.transpose(pb[3][:, u * C:(u + 1) * C], xo[:, 2 * g + u // R, u % R, :], ident[:, :])
                last.then_inc(o_turn_mm.sem, 1)

            def out_product(b, p, g):
                xt_ready.wait(pe, b, g + 1)
                for i in range(2):
                    for h in range(R):
                        last = nc.tensor.matmul(pb[3][:, i * H:(i + 1) * H], xt[:, unit(2 * g + i, h), :],
                                                wout[:, ds((b // B) * R + h, 1), :].rearrange("p a n -> p (a n)"),
                                                start=(h == 0), stop=(h == R - 1))
                last.then_inc(out_mm.sem, 1)
            steps(pe, project=project, project_z=project_z, turn=turn, back=back_turn, gram=gram, decay_mm=decay_product,
                  t_first=t_first, p_mm=p_product, ut_mm=ut_product, resid_mm=resid_product, fix_mm=fix_product,
                  ks_mm=keys_state, qs_mm=queries_state, y=y, update_mm=update_product, intra_mm=intra_product, o_turn=o_turn,
                  out_mm=out_product)

        @block.scalar
        def _(act):
            made.wait(act, 0, MADE)

            def tap(a, p, c):
                if c == K:
                    small_ready.wait(act, a, 1)
                proj_mm.wait(act, a, c + 1)
                turn_mm.wait(act, a - 1, c + 1)
                nc.scalar.activation(conv[c][:, :], proj_bank[c][:, :], ACT.Copy,
                                     scale=cws[p][:, c * TAPS + 3:c * TAPS + 4]).then_inc(tap_first.sem, 1)

            def silu(a, p, c):
                tapped.wait(act, a, convolved(c))
                nc.scalar.activation(conv[c][:, :], conv[c][:, :], ACT.Silu).then_inc(silued.sem, 1)

            def z(a, p, g):
                proj_mm.wait(act, a, 5 + g)
                gated.wait(act, a - 2, 2)
                nc.scalar.activation(zs[p][:, 2 * g:2 * g + 2, :, :].rearrange("p n h c -> p (n h c)"),
                                     proj_bank[4 + g][:, :], ACT.Silu).then_inc(z_ready.sem, 1)

            def norm_squares(a, p, c):
                turn_mm.wait(act, a, c + 1)
                for n in range(NC):
                    last = nc.scalar.activation(junk[:, c * NC + n, :], turn_bank[c][:, n * C:(n + 1) * C], ACT.Square,
                                                scale=1.0 if c == K else float(D) ** 0.5, accum_out=ssq[:, c, n:n + 1])
                last.then_inc(squares.sem, 1)

            def values(a, p, h):
                turn_mm.wait(act, a, h + 3)
                res_ready.wait(act, a - 2, NC)
                nc.scalar.activation(vt[p][:, :, h, :], four(turn_bank[V0 + h]), ACT.Copy).then_inc(vt_ready.sem, 1)

            def keys_queries(a, p, c):
                back_mm.wait(act, a, c + 1)
                qs_mm.wait(act, a - 2, 3)
                nc.scalar.activation(kq[p][:, :, c, :], four(turn_bank[c]), ACT.Copy).then_inc(kq_ready.sem, 1)

            def decay(a, p, g):
                decay_mm.wait(act, a, g + 1)
                attn_ready.wait(act, a - 1, 2)
                nc.scalar.activation(group(et, g), four(pb[3]), ACT.Exp).then_inc(decay_ready.sem, 1)

            def rounded(a, p, g):
                sys_diag.wait(act, a, g + 1)
                nc.scalar.activation(group(a16, g), group(a32, g), ACT.Copy).then_inc(sys_rounded.sem, 1)

            def t_first(a, p, g):
                if g == 1:
                    t_first_mm.wait(act, a, 2)
                    nc.scalar.activation(group(t16_, 1), pa[2][:, :].bitcast(f16)[:, 0:512].rearrange("p (u c) -> p u c", u=4),
                                         ACT.Copy).then_inc(t_ready[1].sem, 1)

            def ut(a, p, l):
                for g in range(2):
                    if g == 1:
                        t_mm.wait(act, a, 2 * l + 2)
                        nc.scalar.activation(group(t16_, g), four(pa[2 * g + 1]), ACT.Copy)\
                            .then_inc(t_ready[g].sem, 1)
                    u_mm.wait(act, a, 2 * l + g + 1)
                    nc.scalar.activation(group(u16_, g), four(pa[2 * g]), ACT.Copy).then_inc(u_ready[g].sem, 1)

            def y_copy(b, p, n):
                y_mm.wait(act, b, n + 1)
                if n:
                    intra_mm.wait(act, b, n)
                else:
                    intra_mm.wait(act, b - 1, NC)
                nc.scalar.activation(yb[:, :, :], pb[0][:, 0:R * D].rearrange("p (h d) -> p h d", h=R), ACT.Copy)\
                    .then_inc(y_ready.sem, 1)

            def q_part(b, p, n):
                qs_mm.wait(act, b, n)
                o_ready.wait(act, b, n)
                for h in range(R):
                    last = nc.scalar.activation(qe[:, h, :], pb[1][:, h * D:(h + 1) * D], ACT.Copy,
                                                scale=small[p][:, n, 0, h:h + 1])
                last.then_inc(qe_ready.sem, 1)

            def o_square(b, p, g):
                gated.wait(act, b, g + 1)
                for u in range(4):
                    last = nc.scalar.activation(junk[:, 2 * NC + 4 * g + u, :], xo[:, 2 * g + u // R, u % R, :], ACT.Square,
                                                scale=float(D) ** -0.5, accum_out=rs[:, 4 * g + u:4 * g + u + 1])
                last.then_inc(o_squares.sem, 1)

            def x_copy(b, p, g):
                o_turn_mm.wait(act, b, g + 1)
                nc.scalar.activation(group(xt, g), four(pb[3]), ACT.Copy).then_inc(xt_ready.sem, 1)
            steps(act, tap=tap, silu=silu, z=z, squares=norm_squares, vt=values, kq=keys_queries, decay=decay,
                  rounded=rounded, t_first=t_first, ut=ut, y_copy=y_copy, q_part=q_part, o_square=o_square, x_copy=x_copy)

        @block.vector
        def _(ve):
            for q in range(2):
                nc.vector.memset(lrow[q][:, :, :, :], 1.0)
                nc.vector.memset(rrow[q][:, :, :, :], 1.0).then_inc(made.sem, 1)
            nc.vector.tensor_copy(ident16[:, :], ident[:, :]).then_inc(made.sem, 1)
            nc.vector.tensor_copy(identb[:, :], ident[:, :]).then_inc(made.sem, 1)
            nc.vector.tensor_scalar(ident_esc[:, :], ident[:, :], ESC, None, ALU.mult).then_inc(made.sem, 1)
            consts_in.wait(ve, 0, 16 * NCONST)
            nc.vector.tensor_copy(neg[:, :, :], et[:, 0:1, :].broadcast_to([128, 4, C])).then_inc(made.sem, 1)
            made.wait(ve, 0, MADE)
            preset.wait(ve, 0, LEVELS)

            def convolve(a, p, i):
                part, back = i // 3, i % 3 + 1
                for c in (2 * part, 2 * part + 1):
                    if back == 1:
                        tap_first.wait(ve, a, c + 1)
                    else:
                        tapped.wait(ve, a, 6 * part + 2 * (back - 2) + (c % 2) + 1)
                    nc.vector.scalar_tensor_tensor(
                        out=conv[c][:, back:S], in0=proj_bank[c][:, 0:S - back],
                        scalar=cws[p][:, c * TAPS + 3 - back:c * TAPS + 4 - back], in1=conv[c][:, back:S],
                        op0=ALU.mult, op1=ALU.add).then_inc(tapped.sem, 1)

            def norm(a, p, c):
                rnorm.wait(ve, a, c + 1)
                if c == K:
                    kw_ready.wait(ve, a - 1, 2)
                nc.vector.tensor_tensor(tokn[c][:, :, :], four(turn_bank[c]),
                                        rn[:, c, :, None].broadcast_to([128, NC, C]), ALU.mult).then_inc(normed.sem, 1)

            def by_decay(out, g, which):
                grams = pa[g][:, :].rearrange("p (n w c) -> p n w c", n=2, w=2)
                return nc.vector.tensor_tensor(group(out, g).rearrange("p (n h) c -> p n h c", h=R), per_head(grams[:, :, which, :]),
                                               group(et, g).rearrange("p (n h) c -> p n h c", h=R), ALU.mult)

            def system(a, p, g):
                decay_ready.wait(ve, a, g + 1)
                gram_mm.wait(ve, a, g + 1)
                by_decay(a32, g, 0).then_inc(sys_ready.sem, 1)

            def attention(a, p, g):
                intra_mm.wait(ve, a - 2, NC)
                by_decay(attn[p], g, 1).then_inc(attn_ready.sem, 1)

            def first(a, p, g):
                sys_rounded.wait(ve, a, g + 1)
                nc.vector.tensor_tensor(group(u16_, g), group(a16, g),
                                        mask2[:, None, :].broadcast_to([128, 4, C]), ALU.mult).then_inc(u_first.sem, 1)

            def t_first(a, p, g):
                if g == 0:
                    t_first_mm.wait(ve, a, 1)
                    nc.vector.tensor_copy(group(t16_, 0), pa[0][:, :].bitcast(f16)[:, 0:512].rearrange("p (u c) -> p u c", u=4))\
                        .then_inc(t_ready[0].sem, 1)

            def factor(a, p, l):
                for g in range(2):
                    p_mm.wait(ve, a, 2 * l + g + 1)
                    ve.sem_inc(passed[0].sem, 1)
                    nc.vector.copy_predicated(group(pl[l], g), masks[:, l:l + 1, :].broadcast_to([128, 4, C]),
                                              four(pa[2 * g + 1])).then_inc(p_ready.sem, 1)

            def ut(a, p, l):
                t_mm.wait(ve, a, 2 * l + 1)
                nc.vector.tensor_copy(group(t16_, 0), four(pa[1])).then_inc(t_ready[0].sem, 1)

            def resid(a, p, g):
                resid_mm.wait(ve, a, g + 1)
                nc.vector.scalar_tensor_tensor(out=group(e16, g), in0=four(pa[2 * g]), scalar=ESC,
                                               in1=ident_esc[:, None, :].broadcast_to([128, 4, C]),
                                               op0=ALU.mult, op1=ALU.add).then_inc(resid_ready.sem, 1)

            def fix(a, p, g):
                fix_mm.wait(ve, a, g + 1)
                y_mm.wait(ve, a - 2, NC)
                nc.vector.scalar_tensor_tensor(out=group(u32[p], g), in0=four(pa[2 * g + 1]), scalar=1.0 / ESC,
                                               in1=group(u16_, g), op0=ALU.mult, op1=ALU.add).then_inc(inv_ready.sem, 1)

            def residual(b, p, n):
                if n == 0:
                    vt_ready.wait(ve, b, 2)
                    y_mm.wait(ve, b - 1, NC)
                    nc.vector.tensor_scalar(res[:, :, :], vt[p][:, 0, :, :], -1.0, None, ALU.mult).then_inc(res_ready.sem, 1)
                    return
                ks_mm.wait(ve, b, n)
                for h in range(R):
                    last = nc.vector.scalar_tensor_tensor(out=res[:, h, :], in0=pb[0][:, h * D:(h + 1) * D],
                                                          scalar=small[p][:, n, 0, h:h + 1], in1=vt[p][:, n, h, :],
                                                          op0=ALU.mult, op1=ALU.subtract)
                last.then_inc(res_ready.sem, 1)

            def y(b, p, n):
                if n == 0:
                    residual(b, p, 0)

            def state(b, p, n):
                upd_mm.wait(ve, b, n + 1)
                if n == 0:
                    nc.vector.tensor_copy(st[:, :, :].rearrange("p h d -> p (h d)"), pb[2][:, 0:R * D]).then_inc(st_ready.sem, 1)
                else:
                    st_ready.wait(ve, b, n)
                    for h in range(R):
                        last = nc.vector.scalar_tensor_tensor(out=st[:, h, :], in0=st[:, h, :],
                                                              scalar=small[p][:, n, 2, h:h + 1],
                                                              in1=pb[2][:, h * D:(h + 1) * D],
                                                              op0=ALU.mult, op1=ALU.add)
                    last.then_inc(st_ready.sem, 1)

            def output(b, p, n):
                intra_mm.wait(ve, b, n + 1)
                if n == 0:
                    o_turn_mm.wait(ve, b - 1, 2)
                    nc.vector.tensor_copy(xo[:, 0, :, :].rearrange("p h d -> p (h d)"), pb[1][:, 0:R * D]).then_inc(o_ready.sem, 1)
                else:
                    qe_ready.wait(ve, b, n)
                    nc.vector.tensor_tensor(xo[:, n, :, :], qe[:, :, :], pb[1][:, 0:R * D].rearrange("p (h d) -> p h d", h=R),
                                            ALU.add).then_inc(o_ready.sem, 1)

            def o_norm(b, p, g):
                o_rnorm.wait(ve, b, g + 1)
                x = xo[:, 2 * g:2 * g + 2, :, :].rearrange("p n h d -> p (n h) d")
                nc.vector.tensor_tensor(x, x, rr[:, 4 * g:4 * g + 4, None].broadcast_to([128, 4, D]), ALU.mult)\
                    .then_inc(o_normed.sem, 1)

            def add(b, p, g):
                out_mm.wait(ve, b, g + 1)
                y = yacc[:, ds((b % B) * NC + 2 * g, 2), :]
                added.wait(ve, b - 1, 2)
                nc.vector.tensor_tensor(y, y, pb[3][:, :].rearrange("p (n h) -> p n h", n=2), ALU.add)\
                    .then_inc(added.sem, 1)
            steps(ve, conv=convolve, normed=norm, system=system, attn=attention, u_first=first, t_first=t_first, p=factor,
                  ut=ut, resid=resid, fix=fix, residual=residual, y=y, state=state, out=output, o_norm=o_norm, added=add)

        @block.gpsimd
        def _(pool):
            made.wait(pool, 0, 1)
            for q in range(LEVELS):
                nc.gpsimd.tensor_copy(pl[q][:, :, :], ident[:, None, :].broadcast_to([128, NU, C])).then_inc(preset.sem, 1)

            def factors(a, p, _):
                qe_ready.wait(pool, a - 2, 3)
                st_ready.wait(pool, a - 2, 3)
                res_ready.wait(pool, a - 2, NC)
                pool.sem_inc(passed[1].sem, 1)
                nc.gpsimd.tensor_copy(cws[p][:, :], cw[:, ds(a // B, 1), :].rearrange("p a n -> p (a n)"))
                nc.gpsimd.tensor_copy(small[p][:, :, :, :].rearrange("p n q h -> p (n q h)"),
                                      vec[:, ds(a, 1), :].rearrange("p a n -> p (a n)")).then_inc(small_ready.sem, 1)

            def rnorms(a, p, c):
                squares.wait(pool, a, c + 1)
                nc.gpsimd.tensor_tensor(ssqe[:, c, :], ssq[:, c, :], expo_eps[:, 1 + c, :], ALU.add)\
                    .then_inc(eps_in.sem, 1)
                eps_in.wait(pool, a, c + 1)
                nc.gpsimd.tensor_tensor(rn[:, c, :], ssqe[:, c, :], expo_eps[:, 0, :], ALU.pow).then_inc(rnorm.sem, 1)

            def weighted_keys(a, p, _):
                normed.wait(pool, a, 1)
                upd_mm.wait(pool, a - 2, 3)
                small_ready.wait(pool, a, 1)
                for h in range(R):
                    nc.gpsimd.tensor_tensor(kw[p][:, :, h, :], tokn[K][:, :, :],
                                            small[p][:, :, 1, h:h + 1].broadcast_to([128, NC, D]), ALU.mult)\
                        .then_inc(kw_ready.sem, 1)

            def diagonal(a, p, g):
                sys_ready.wait(pool, a, g + 1)
                pool.sem_inc(passed[1].sem, 1)
                nc.gpsimd.affine_select(out=group(a32, g), in_=group(a32, g), compare_op=ALU.not_equal, fill=1.0,
                                        base=0, pattern=[[0, 4], [-1, C]], channel_multiplier=1).then_inc(sys_diag.sem, 1)

            def low_part(a, p, g):
                sys_rounded.wait(pool, a, g + 1)
                resid_mm.wait(pool, a - 1, 2)
                nc.gpsimd.tensor_tensor(group(a_low, g), group(a32, g), group(a16, g), ALU.subtract).then_inc(low_ready.sem, 1)

            def gate(b, p, g):
                x = xo[:, 2 * g:2 * g + 2, :, :]
                z_ready.wait(pool, b, g + 1)
                o_ready.wait(pool, b, 2 * g + 2)
                nc.gpsimd.tensor_tensor(x, x, zs[p][:, 2 * g:2 * g + 2, :, :], ALU.mult).then_inc(gated.sem, 1)

            def o_rnorms(b, p, g):
                o_squares.wait(pool, b, g + 1)
                nc.gpsimd.tensor_tensor(rse[:, 4 * g:4 * g + 4], rs[:, 4 * g:4 * g + 4], expo_eps[:, 3, :], ALU.add)\
                    .then_inc(o_eps.sem, 1)
                o_eps.wait(pool, b, g + 1)
                nc.gpsimd.tensor_tensor(rr[:, 4 * g:4 * g + 4], rse[:, 4 * g:4 * g + 4], expo_eps[:, 0, :], ALU.pow)\
                    .then_inc(o_rnorm.sem, 1)
            steps(pool, small=factors, rnorm=rnorms, kw=weighted_keys, diagonal=diagonal, low=low_part, gate=gate, o_rnorm=o_rnorms)


def feed_forward(nc, io, m):
    yacc, ident = m["yacc"], m["ident"]
    with ExitStack() as ctx:
        def sb(name, shape, dt=f32):
            return ctx.enter_context(nc.sbuf_tensor(name, shape, dt))

        def signal(name, per=1):
            return Signal(nc, ctx, name, per)
        wug = sb("wug", [128, 2, KT, E])
        wdn = sb("wdn", [128, ET, H])
        low = sb("low", [128, 2, KT, E])
        ones = sb("fones", [128, 128])
        expo_eps = sb("fexpo_eps", [128, 5, NC])
        asum = sb("asum", [128, 3])
        scale = sb("scale", [128, 3])
        half = sb("half", [128, 3])
        mhalfs = sb("mhalfs", [128, 3])
        sgd = sb("sgd", [128, 1])
        mean = sb("fmean", [128, 2, NC])
        meanm = sb("fmeanm", [128, 2, NC])
        var = sb("fvar", [128, 2, NC])
        vare = sb("fvare", [128, 2, NC])
        rstd = sb("frstd", [128, 2, NC])
        junk = sb("fjunk", [128, 2 * NC, H], bf16)
        xn = sb("fxn", [128, NC, H])
        xnT = sb("fxnT", [128, KT, S])
        up = sb("fup", [128, ET, S])
        hid = sb("fhid", [128, ET, S])
        yo = sb("fyo", [128, NC, H])
        ob = [sb(f"fob{i}", [128, NC, H]) for i in range(2)]
        pw = ctx.enter_context(nc.psum_tensor("pw", [128, 512], f32))
        pt = ctx.enter_context(nc.psum_tensor("fpt", [128, 512], f32))
        pu = [ctx.enter_context(nc.psum_tensor(f"pu{i}", [128, 512], f32)) for i in range(2)]
        pv = [ctx.enter_context(nc.psum_tensor(f"pv{i}", [128, 512], f32)) for i in range(2)]
        pd = [ctx.enter_context(nc.psum_tensor(f"pd{i}", [128, 512], f32)) for i in range(2)]
        w_in, made, sums, total_mm, chain, tern = (signal(f"f_{n}") for n in ("w_in", "made", "sums", "total_mm", "chain", "tern"))
        meaned, centred, vars_ready, eps_in, rstd_ready, normed = (signal(f"f_{n}", 2) for n in ("meaned", "centred", "vars", "eps", "rstd", "normed"))
        means = signal("f_means", 2)
        turn_mm, turned, up_mm, gate_mm, silued, hid_ready, down_mm, y_ready = (
            signal(*a) for a in (("f_turn_mm", 2), ("f_turned", 2), ("f_up_mm", ET), ("f_gate_mm", ET), ("f_silued", ET),
                                 ("f_hid", ET), ("f_down_mm", 2), ("f_y", 2)))
        stored = [signal(f"f_stored{p}", 16) for p in range(2)]
        block = ctx.enter_context(nc.Block())
        NTERN = 3

        @block.sync
        def _(sp):
            sp.dma_start(wug[:, 0, :, :], io["WupT"].rearrange("(k p) n -> p k n", p=128)).then_inc(w_in.sem, 16)
            sp.dma_start(wug[:, 1, :, :], io["WgateT"].rearrange("(k p) n -> p k n", p=128)).then_inc(w_in.sem, 16)
            sp.dma_start(wdn[:, :, :], io["WdownT"].rearrange("(k p) n -> p k n", p=128)).then_inc(w_in.sem, 16)
            sp.dma_start(expo_eps[:, :, :], io["expo_eps"]).then_inc(w_in.sem, 16)

            def store(i, p):
                normed.wait(sp, i, 2)
                sp.dma_start(io["out"].rearrange("(i n p) h -> i p n h", n=NC, p=128)[ds(i, 1)]
                             .rearrange("i p n h -> p (i n) h"), ob[p][:, :, :]).then_inc(stored[p].sem, 16)
            store(0, 0)
            store(1, 1)
            with sp.Fori(1, B // 2) as j:
                store(2 * j, 0)
                store(2 * j + 1, 1)
            for p in range(2):
                stored[p].wait(sp, B // 2 - 1, 16)

        def loop(engine, body):
            body(0, 0)
            body(1, 1)
            with engine.Fori(1, B // 2) as j:
                body(2 * j, 0)
                body(2 * j + 1, 1)

        @block.tensor
        def _(pe):
            made.wait(pe, 0, 1)
            sums.wait(pe, 0, 3)
            nc.tensor.matmul(pw[:, 0:3], ones[:, :], asum[:, :], start=True, stop=True).then_inc(total_mm.sem, 1)
            tern.wait(pe, 0, NTERN)

            def body(i, p):
                normed.wait(pe, i, 1)
                for k in range(KT):
                    if k == 0:
                        turned.wait(pe, i - 1, 2)
                    else:
                        turned.wait(pe, i, 1)
                    for n in range(NC):
                        last = nc.tensor.transpose(pt[:, n * C:(n + 1) * C], xn[:, n, k * 128:(k + 1) * 128], ident[:, :])
                    last.then_inc(turn_mm.sem, 1)
                turned.wait(pe, i, 2)
                for t in range(ET):
                    if t >= 2:
                        silued.wait(pe, i, t - 1)
                    else:
                        silued.wait(pe, i - 1, ET)
                    for k in range(KT):
                        last = nc.tensor.matmul(pu[t % 2][:, :], wug[:, 0, k, t * 128:(t + 1) * 128], xnT[:, k, :],
                                                start=(k == 0), stop=(k == KT - 1))
                    last.then_inc(up_mm.sem, 1)
                    if t >= 2:
                        hid_ready.wait(pe, i, t - 1)
                    else:
                        hid_ready.wait(pe, i - 1, ET)
                    for k in range(KT):
                        last = nc.tensor.matmul(pv[t % 2][:, :], wug[:, 1, k, t * 128:(t + 1) * 128], xnT[:, k, :],
                                                start=(k == 0), stop=(k == KT - 1))
                    last.then_inc(gate_mm.sem, 1)
                hid_ready.wait(pe, i, ET)
                for g in range(2):
                    y_ready.wait(pe, i - 1, g + 1)
                    for n in range(2):
                        for t in range(ET):
                            last = nc.tensor.matmul(pd[g][:, n * H:(n + 1) * H],
                                                    hid[:, t, (2 * g + n) * C:(2 * g + n + 1) * C], wdn[:, t, :],
                                                    start=(t == 0), stop=(t == ET - 1))
                    last.then_inc(down_mm.sem, 1)
            loop(pe, body)

        @block.scalar
        def _(act):
            def squares(i, which, src):
                centred.wait(act, i, which + 1)
                for n in range(NC):
                    last = nc.scalar.activation(junk[:, which * NC + n, :], src[:, n, :], ACT.Square, scale=float(H) ** -0.5,
                                                accum_out=var[:, which, n:n + 1])
                last.then_inc(vars_ready.sem, 1)
            tern.wait(act, 0, NTERN)

            def body(i, p):
                squares(i, 0, xn)
                for k in range(KT):
                    turn_mm.wait(act, i, k + 1)
                    nc.scalar.activation(xnT[:, k, :], pt[:, :], ACT.Copy).then_inc(turned.sem, 1)
                for t in range(ET):
                    up_mm.wait(act, i, t + 1)
                    hid_ready.wait(act, i - 1, ET)
                    nc.scalar.activation(up[:, t, :], pu[t % 2][:, :], ACT.Silu, scale=scale[:, 0:1]).then_inc(silued.sem, 1)
                squares(i, 1, yo)
            loop(act, body)

        @block.gpsimd
        def _(pool):
            w_in.wait(pool, 0, 64)

            def body(i, p):
                for w in range(2):
                    vars_ready.wait(pool, i, w + 1)
                    nc.gpsimd.tensor_tensor(vare[:, w, :], var[:, w, :], expo_eps[:, 4, :], ALU.add).then_inc(eps_in.sem, 1)
                    eps_in.wait(pool, i, w + 1)
                    nc.gpsimd.tensor_tensor(rstd[:, w, :], vare[:, w, :], expo_eps[:, 0, :], ALU.pow).then_inc(rstd_ready.sem, 1)
            loop(pool, body)

        @block.vector
        def _(ve):
            links = [0]

            def link(ins):
                links[0] += 1
                ins.then_inc(chain.sem, 1)
                ve.wait_ge(chain.sem, links[0])
            nc.vector.memset(ones[:, :], 1.0).then_inc(made.sem, 1)
            w_in.wait(ve, 0, 64)
            for q, w in enumerate((wug[:, 0], wug[:, 1], wdn[:, :, :])):
                nc.vector.tensor_reduce(asum[:, q:q + 1], w, AX.XY, ALU.add, apply_absolute_value=True).then_inc(sums.sem, 1)
            total_mm.wait(ve, 0, 1)
            link(nc.vector.tensor_scalar(scale[:, :], pw[:, 0:3], 1.0 / (E * H), TERN_EPS, ALU.mult, ALU.add))
            link(nc.vector.tensor_scalar(half[:, :], scale[:, :], 0.5, None, ALU.mult))
            link(nc.vector.tensor_scalar(mhalfs[:, :], scale[:, :], -0.5, None, ALU.mult))
            link(nc.vector.tensor_tensor(sgd[:, :], scale[:, 1:2], scale[:, 2:3], ALU.mult))
            for q, w in enumerate((wug[:, 0], wug[:, 1], wdn[:, :, :])):
                lo = low[:, 0, :, :] if q < 2 else low[:, 0, :, :].rearrange("p k n -> p (k n)").rearrange("p (t h) -> p t h", t=ET)
                link(nc.vector.tensor_scalar(lo, w, mhalfs[:, q:q + 1], None, ALU.is_lt))
                nc.vector.scalar_tensor_tensor(out=w, in0=w, scalar=half[:, q:q + 1], in1=lo, op0=ALU.is_gt,
                                               op1=ALU.subtract).then_inc(tern.sem, 1)
                tern.wait(ve, 0, q + 1)

            def norm(i, w, src, centre, dst):
                nc.vector.tensor_reduce(mean[:, w, :], src, AX.X, ALU.add).then_inc(meaned.sem, 1)
                meaned.wait(ve, i, w + 1)
                nc.vector.tensor_scalar(meanm[:, w, :], mean[:, w, :], 1.0 / H, None, ALU.mult).then_inc(means.sem, 1)
                means.wait(ve, i, w + 1)
                nc.vector.tensor_tensor(centre, src, meanm[:, w, :, None].broadcast_to([128, NC, H]), ALU.subtract)\
                    .then_inc(centred.sem, 1)
                rstd_ready.wait(ve, i, w + 1)
                vars_ready.wait(ve, i, w + 1)
                nc.vector.tensor_tensor(dst, centre, rstd[:, w, :, None].broadcast_to([128, NC, H]), ALU.mult)\
                    .then_inc(normed.sem, 1)

            def body(i, p):
                turn_mm.wait(ve, i - 1, 2)
                y_ready.wait(ve, i - 1, 2)
                norm(i, 0, yacc[:, ds(i * NC, NC), :], xn[:, :, :], xn[:, :, :])
                for t in range(ET):
                    gate_mm.wait(ve, i, t + 1)
                    silued.wait(ve, i, t + 1)
                    down_mm.wait(ve, i - 1, 2)
                    nc.vector.tensor_tensor(hid[:, t, :], up[:, t, :], pv[t % 2][:, :], ALU.mult).then_inc(hid_ready.sem, 1)
                normed.wait(ve, i, 1)
                for g in range(2):
                    down_mm.wait(ve, i, g + 1)
                    nc.vector.scalar_tensor_tensor(out=yo[:, 2 * g:2 * g + 2, :],
                                                   in0=pd[g][:, :].rearrange("p (n h) -> p n h", n=2), scalar=sgd[:, 0:1],
                                                   in1=xn[:, 2 * g:2 * g + 2, :], op0=ALU.mult, op1=ALU.add)\
                        .then_inc(y_ready.sem, 1)
                y_ready.wait(ve, i, 2)
                stored[p].wait(ve, i // 2 - 1, 16)
                norm(i, 1, yo[:, :, :], yo[:, :, :], ob[p][:, :, :])
            loop(ve, body)


def constants():
    i = np.arange(128)
    masks = np.zeros((128, LEVELS, 128), np.uint16)
    for l in range(LEVELS):
        s = 2 << l
        same = (i[:, None] // (2 * s)) == (i[None, :] // (2 * s))
        masks[:, l, :] = same & (i[:, None] % (2 * s) >= s) & (i[None, :] % (2 * s) < s)
    mask2 = -np.eye(128) + ((i[:, None] // 2 == i[None, :] // 2) & (i[:, None] < i[None, :]))
    neg = np.where(i[None, :] < i[:, None], -1e30, 0.0)
    return {
        "ident": np.eye(128, dtype=np.float32),
        "triu": (i[:, None] <= i[None, :]).astype(np.float32),
        "neg": neg.astype(np.float32),
        "masks": masks,
        "mask2": mask2.astype(np.float16),
        "expo_eps": np.broadcast_to(np.array([-0.5, EPS, EPS * D, EPS, LN_EPS], np.float32)[None, :, None], (128, 5, NC)),
    }


def kernel(L0_attn_hidden_states, L0_attn_W_qkvz, L0_attn_W_ba, L0_attn_conv_weight, L0_attn_A_log, L0_attn_dt_bias,
           L0_attn_norm_weight, L0_attn_W_out, L0_ffn_W_up, L0_ffn_W_gate, L0_ffn_W_down):
    import concourse.bacc as bacc
    from concourse.bass_utils import run_bass_kernel_spmd
    x = np.asarray(L0_attn_hidden_states)
    w = np.asarray(L0_attn_W_qkvz).reshape(H, NK, WCOL)
    w = np.concatenate([w[..., D:2 * D], w[..., 0:D], w[..., 2 * D:]], -1).reshape(H, NK * WCOL)
    wba = np.asarray(L0_attn_W_ba).reshape(H, NK, 2, R).transpose(0, 2, 1, 3).reshape(H, 2 * NV)
    cwt = np.asarray(L0_attn_conv_weight)
    q, k, v = cwt[:NK * D].reshape(NK, 1, D, TAPS), cwt[NK * D:2 * NK * D].reshape(NK, 1, D, TAPS), cwt[2 * NK * D:].reshape(NK, R, D, TAPS)
    cwt = np.concatenate([k, q, v], 1).transpose(2, 0, 1, 3).reshape(D, NK, 4 * TAPS)
    arrays = {
        "xT": x.transpose(0, 2, 1).reshape(B, KT, 128, S),
        "x_tok": x.reshape(B * S, H),
        "Wqkvz": w, "Wba": wba, "convw": cwt,
        "A_log": L0_attn_A_log, "dt_bias": L0_attn_dt_bias, "norm_weight": L0_attn_norm_weight, "W_out": L0_attn_W_out,
        "WupT": np.asarray(L0_ffn_W_up).T, "WgateT": np.asarray(L0_ffn_W_gate).T, "WdownT": np.asarray(L0_ffn_W_down).T,
    }
    arrays.update(constants())
    arrays = {f"in_{n}": np.ascontiguousarray(a) for n, a in arrays.items()}
    nc = bacc.Bacc("TRN2", target_bir_lowering=False, num_devices=1)
    io = {n[3:]: nc.dram_tensor(n, a.shape, mybir.dt.from_np(a.dtype), kind="ExternalInput").ap() for n, a in arrays.items()}
    io["out"] = nc.dram_tensor("out", (B * S, H), f32, kind="ExternalOutput").ap()
    build(nc, io)
    r = run_bass_kernel_spmd(nc, [arrays], core_ids=[0])
    return r.results[0]["out"].reshape(B, S, H)
```

```python
import numpy as np
import concourse.bass as bass
from concourse import mybir
from contextlib import ExitStack

B, S, H = 8, 512, 256
NK, R, D = 16, 2, 128
NV = NK * R
KT = H // 128
C = 128
NC = S // C
NB = B * NC
NU = NC * R
TAPS = 4
WCOL = 2 * D + 2 * R * D
ITS = NK * B
LEVELS = 6
E = 1024
ET = E // 128
ESC = 256.0
KINDS = 3
SMALL = NC * KINDS * R
EPS, LN_EPS, TERN_EPS = 1e-6, 1e-5, 1e-8

f32, f32r, f16, bf16, u16 = mybir.dt.float32, mybir.dt.float32r, mybir.dt.float16, mybir.dt.bfloat16, mybir.dt.uint16
ALU, ACT, AX = mybir.AluOpType, mybir.ActivationFunctionType, mybir.AxisListType
ds = bass.ds


class Signal:

    def __init__(self, nc, ctx, name, per=1):
        self.sem, self.per = ctx.enter_context(nc.semaphore(name)), per

    def at(self, it, n):
        return it * self.per + n

    def wait(self, engine, it, n):
        if isinstance(it, int) and it < 0:
            return
        engine.wait_ge(self.sem, self.at(it, n))


def build(nc, io):
    with ExitStack() as ctx:
        def sb(name, shape, dt=f32):
            return ctx.enter_context(nc.sbuf_tensor(name, shape, dt))
        m = {
            "yacc": sb("yacc", [128, NB, H]),
            "ident": sb("ident", [128, 128]),
        }
        with ExitStack() as attention:
            def sa(name, shape, dt=f32):
                return attention.enter_context(nc.sbuf_tensor(name, shape, dt))
            m["wout"] = sa("wout", [128, NV, H])
            m["vec"] = sa("vec", [128, ITS, SMALL])
            m["cw"] = sa("cw", [128, NK, 4 * TAPS])
            m["rows_dram"] = nc.dram_tensor("rows_scratch", (ITS, 2, 3, R, S), bf16, kind="Internal").ap()
            gates(nc, io, m)
            delta_rule(nc, io, m)
        feed_forward(nc, io, m)


def gates(nc, io, m):
    yacc, ident, wout, vec, cw, rows_dram = (m[k] for k in ("yacc", "ident", "wout", "vec", "cw", "rows_dram"))
    with ExitStack() as ctx:
        def sb(name, shape, dt=f32):
            return ctx.enter_context(nc.sbuf_tensor(name, shape, dt))

        def signal(name, per=1):
            return Signal(nc, ctx, name, per)
        wba = sb("wba", [128, KT, 2 * NV])
        xb = [sb(f"gxb{p}", [128, KT, S]) for p in range(2)]
        nwt = sb("nwt", [128, 1])
        na = sb("na", [128, NV])
        dtb = sb("dtb", [128, NV])
        triu = sb("triu", [128, 128])
        ones = sb("ones", [128, 128])
        identb = sb("gidentb", [128, 128], bf16)
        ba = sb("ba", [128, NB, 2, NV])
        e = sb("ge", [128, NB, 2, NV])
        s = sb("gs", [128, NB, 2, NV])
        s2 = sb("gs2", [128, NB, 2, NV])
        p = sb("gp", [128, NB, 2, NV])
        sp_ = sb("gsoft", [128, NB, 2, NV])
        graw = sb("graw", [128, NB, NV])
        gs = sb("gcum", [128, NB, NV])
        gl = sb("glast", [128, NB, NV])
        hj = sb("ghj", [128, NB, NV])
        dl = sb("gdl", [128, NB, NV])
        r1 = sb("gr1", [128, NB, NV])
        parts = sb("parts", [128, NB, 2, 3, NV], bf16)
        rows = sb("rows", [3 * NV, 2, NB * C], bf16)
        pz = ctx.enter_context(nc.psum_tensor("pz", [128, 512], f32))
        pg = [ctx.enter_context(nc.psum_tensor(f"pg{i}", [128, 512], f32)) for i in range(4)]
        pt = [ctx.enter_context(nc.psum_tensor(f"pt{i}", [128, 1024], bf16)) for i in range(2)]

        consts_in, more_in = signal("g_consts_in", 16), signal("g_more_in", 16)
        x_in = [signal(f"g_x_in{p}", 16) for p in range(2)]
        made_ones, made_identb = signal("g_ones"), signal("g_identb")
        ba_mm, ba_out, x_ready, abs_ready, exp_a, exp_abs = (signal(f"g_{n}") for n in ("ba_mm", "ba_out", "x", "abs", "expa", "expabs"))
        graw_ready, cum_mm, cum_out, dl_ready, parts_ready = (signal(f"g_{n}") for n in ("graw", "cum_mm", "cum_out", "dl", "parts"))
        turn_mm, turn_out, chain = signal("g_turn_mm"), signal("g_turn_out"), signal("g_chain")
        rows_out = [signal(f"g_rows_out{w}", 16) for w in range(2)]
        NTURN = 2 * NB // 4
        block = ctx.enter_context(nc.Block())
        loads = [
            (wba[:, :, :], io["Wba"].rearrange("(k p) n -> p k n", p=128)),
            (dtb[:, :], io["dt_bias"].rearrange("(a n) -> a n", a=1).broadcast_to([128, NV])),
            (na[:, :], io["A_log"].rearrange("(a n) -> a n", a=1).broadcast_to([128, NV])),
            (nwt[:, :], io["norm_weight"].rearrange("(p a) -> p a", a=1)),
            (triu[:, :], io["triu"]),
            (ident[:, :], io["ident"]),
            (cw[:, :, :], io["convw"]),
            (wout[:, :, :], io["W_out"].rearrange("(h p) n -> p h n", p=128)),
            (yacc[:, 0:NB // 2, :], io["x_tok"].rearrange("(n p) h -> p n h", p=128)[:, 0:NB // 2, :]),
            (yacc[:, NB // 2:NB, :], io["x_tok"].rearrange("(n p) h -> p n h", p=128)[:, NB // 2:NB, :]),
        ]
        FIRST = 6
        LOADED = 16 * FIRST

        def rows_to_dram(engine, w):
            engine.wait_ge(turn_out.sem, (w + 1) * NTURN // 2)
            dst = rows_dram.rearrange("(k b) w q h s -> w q k h b s", b=B)
            for q in range(3):
                for b in range(B):
                    engine.dma_start(dst[w, q, :, :, b, :], rows[q * NV:(q + 1) * NV, w, b * S:(b + 1) * S])\
                        .then_inc(rows_out[w].sem, 16)

        @block.sync
        def _(sp):
            for dst, src in loads[:FIRST]:
                sp.dma_start(dst, src).then_inc(consts_in.sem, 16)

            def load(b, p):
                ba_mm.wait(sp, b - 1, 0)
                sp.dma_start(xb[p][:, :, :], io["xT"][ds(b, 1), :, :, :].rearrange("a k p n -> p (a k) n")).then_inc(x_in[p].sem, 16)
            load(0, 0)
            load(1, 1)
            with sp.Fori(1, B // 2) as j:
                load(2 * j, 0)
                load(2 * j + 1, 1)
            for dst, src in loads[FIRST:]:
                sp.dma_start(dst, src).then_inc(more_in.sem, 16)
            rows_to_dram(sp, 0)
            for w in range(2):
                sp.wait_ge(rows_out[w].sem, 3 * B * 16)
            sp.wait_ge(more_in.sem, 16 * (len(loads) - FIRST))

        @block.tensor
        def _(pe):
            pe.wait_ge(consts_in.sem, LOADED)

            def project(b, p):
                pe.wait_ge(x_in[p].sem, x_in[p].at(b // 2, 16))
                ba_out.wait(pe, b - 1, 1)
                for n in range(NC):
                    for k in range(KT):
                        last = nc.tensor.matmul(pz[:, n * 2 * NV:(n + 1) * 2 * NV], xb[p][:, k, n * C:(n + 1) * C],
                                                wba[:, k, :], start=(k == 0), stop=(k == KT - 1))
                last.then_inc(ba_mm.sem, 1)
            project(0, 0)
            project(1, 1)
            with pe.Fori(1, B // 2) as j:
                project(2 * j, 0)
                project(2 * j + 1, 1)
            pe.wait_ge(made_ones.sem, 1)
            pe.wait_ge(graw_ready.sem, 1)
            for h in range(2):
                rhs = graw[:, h * NB // 2:(h + 1) * NB // 2, :].rearrange("p b h -> p (b h)")
                nc.tensor.matmul(pg[h][:, :], triu[:, :], rhs, start=True, stop=True)
                nc.tensor.matmul(pg[2 + h][:, :], ones[:, :], rhs, start=True, stop=True).then_inc(cum_mm.sem, 1)
            pe.wait_ge(made_identb.sem, 1)
            for g in range(NTURN):
                w, n0 = g // (NTURN // 2), g % (NTURN // 2) * 4
                pe.wait_ge(parts_ready.sem, w + 1)
                if g >= 2:
                    pe.wait_ge(turn_out.sem, g - 1)
                for n in range(4):
                    last = nc.tensor.transpose(pt[g % 2][0:3 * NV, n * C:(n + 1) * C],
                                               parts[:, n0 + n, w, :, :].rearrange("p q h -> p (q h)"), identb[:, :])
                last.then_inc(turn_mm.sem, 1)

        @block.scalar
        def _(act):
            act.wait_ge(consts_in.sem, LOADED)
            nc.scalar.activation(na[:, :], na[:, :], ACT.Exp).then_inc(exp_a.sem, 1)
            act.wait_ge(x_ready.sem, 1)
            nc.scalar.activation(e[:, :, :, :], ba[:, :, :, :], ACT.Abs).then_inc(abs_ready.sem, 1)
            act.wait_ge(abs_ready.sem, 1)
            nc.scalar.activation(e[:, :, :, :], e[:, :, :, :], ACT.Exp, scale=-1.0).then_inc(exp_abs.sem, 1)
            for g in range(NTURN):
                w, n0 = g // (NTURN // 2), g % (NTURN // 2) * 4
                act.wait_ge(turn_mm.sem, g + 1)
                nc.scalar.activation(rows[:, w, n0 * C:(n0 + 4) * C], pt[g % 2][0:3 * NV, 0:4 * C],
                                     ACT.Copy).then_inc(turn_out.sem, 1)
            rows_to_dram(act, 1)
            act.wait_ge(cum_out.sem, 2)
            act.wait_ge(dl_ready.sem, 1)
            for kind, src in enumerate((gs, dl, gl)):
                for b in range(B):
                    for h in range(R):
                        o = vec[:, :, :].rearrange("p (k b) (n q h) -> p b q h n k", b=B, n=NC, q=KINDS)[:, b, kind, h]
                        i = src[:, :, :].rearrange("p (b n) (k h) -> p b h n k", b=B, h=R)[:, b, h]
                        nc.scalar.activation(o, i, ACT.Exp)

        @block.vector
        def _(ve):
            links = [0]

            def link(ins):
                links[0] += 1
                ins.then_inc(chain.sem, 1)
                ve.wait_ge(chain.sem, links[0])
            nc.vector.memset(ones[:, :], 1.0).then_inc(made_ones.sem, 1)
            ve.wait_ge(consts_in.sem, LOADED)
            nc.vector.tensor_copy(identb[:, :], ident[:, :]).then_inc(made_identb.sem, 1)

            def take(b):
                ve.wait_ge(ba_mm.sem, ba_mm.at(b, 1))
                nc.vector.tensor_copy(ba[:, ds(b * NC, NC), :, :].rearrange("p n a h -> p (n a h)"),
                                      pz[:, 0:NC * 2 * NV]).then_inc(ba_out.sem, 1)
            take(0)
            with ve.Fori(1, B) as b:
                take(b)
            ve.wait_ge(ba_out.sem, B)
            bb, aa = ba[:, :, 0, :], ba[:, :, 1, :]
            nc.vector.tensor_scalar(bb, bb, -1.0, None, ALU.mult)
            nc.vector.tensor_tensor(aa, aa, dtb[:, None, :].broadcast_to([128, NB, NV]), ALU.add).then_inc(x_ready.sem, 1)
            ve.wait_ge(x_ready.sem, 1)
            ve.wait_ge(exp_abs.sem, 1)
            link(nc.vector.tensor_scalar(s[:, :, :, :], e[:, :, :, :], 2.0, None, ALU.add))
            link(nc.vector.reciprocal(s[:, :, :, :], s[:, :, :, :]))
            link(nc.vector.tensor_tensor(s[:, :, :, :], s[:, :, :, :], e[:, :, :, :], ALU.mult))
            link(nc.vector.tensor_tensor(s2[:, :, :, :], s[:, :, :, :], s[:, :, :, :], ALU.mult))
            link(nc.vector.tensor_scalar(p[:, :, :, :], s2[:, :, :, :], 1.0 / 15, None, ALU.mult))
            for k in (13, 11, 9, 7, 5, 3):
                link(nc.vector.scalar_tensor_tensor(out=p[:, :, :, :], in0=p[:, :, :, :], scalar=1.0 / k,
                                                    in1=s2[:, :, :, :], op0=ALU.add, op1=ALU.mult))
            link(nc.vector.scalar_tensor_tensor(out=p[:, :, :, :], in0=p[:, :, :, :], scalar=1.0,
                                                in1=s[:, :, :, :], op0=ALU.add, op1=ALU.mult))
            link(nc.vector.tensor_scalar(sp_[:, :, :, :], ba[:, :, :, :], 0.0, None, ALU.max))
            link(nc.vector.scalar_tensor_tensor(out=sp_[:, :, :, :], in0=p[:, :, :, :], scalar=2.0,
                                                in1=sp_[:, :, :, :], op0=ALU.mult, op1=ALU.add))
            ve.wait_ge(exp_a.sem, 1)
            nc.vector.scalar_tensor_tensor(out=graw[:, :, :], in0=sp_[:, :, 1, :], scalar=-1.0,
                                           in1=na[:, None, :].broadcast_to([128, NB, NV]),
                                           op0=ALU.mult, op1=ALU.mult).then_inc(graw_ready.sem, 1)
            for h in range(2):
                ve.wait_ge(cum_mm.sem, h + 1)
                n = slice(h * NB // 2, (h + 1) * NB // 2)
                nc.vector.tensor_copy(gs[:, n, :].rearrange("p b h -> p (b h)"), pg[h][:, :])
                nc.vector.tensor_copy(gl[:, n, :].rearrange("p b h -> p (b h)"), pg[2 + h][:, :]).then_inc(cum_out.sem, 1)
            ve.wait_ge(cum_out.sem, 2)
            link(nc.vector.scalar_tensor_tensor(out=hj[:, :, :], in0=sp_[:, :, 0, :], scalar=-1.0, in1=gs[:, :, :],
                                                op0=ALU.mult, op1=ALU.subtract))
            nc.vector.tensor_tensor(dl[:, :, :], hj[:, :, :], gl[:, :, :], ALU.add).then_inc(dl_ready.sem, 1)
            for w, src in enumerate((hj, gs)):
                link(nc.vector.tensor_copy(parts[:, :, w, 0, :], src[:, :, :]))
                link(nc.vector.tensor_tensor(r1[:, :, :], src[:, :, :], parts[:, :, w, 0, :], ALU.subtract))
                link(nc.vector.tensor_copy(parts[:, :, w, 1, :], r1[:, :, :]))
                link(nc.vector.tensor_tensor(r1[:, :, :], r1[:, :, :], parts[:, :, w, 1, :], ALU.subtract))
                nc.vector.tensor_copy(parts[:, :, w, 2, :], r1[:, :, :]).then_inc(parts_ready.sem, 1)
                if w == 0:
                    ve.wait_ge(parts_ready.sem, 1)
            ve.wait_ge(more_in.sem, 16 * (len(loads) - FIRST))
            nc.vector.tensor_scalar(wout[:, :, :], wout[:, :, :], nwt[:, 0:1], None, ALU.mult)


def delta_rule(nc, io, m):
    yacc, ident, wout, vec, cw, rows_dram = (m[k] for k in ("yacc", "ident", "wout", "vec", "cw", "rows_dram"))
    with ExitStack() as ctx:
        def sb(name, shape, dt=f32):
            return ctx.enter_context(nc.sbuf_tensor(name, shape, dt))

        def signal(name, per=1):
            return Signal(nc, ctx, name, per)
        ident16 = sb("ident16", [128, 128], f16)
        identb = sb("identb", [128, 128], bf16)
        ident_esc = sb("ident_esc", [128, 128])
        neg = sb("neg", [128, 4, 128], bf16)
        masks = sb("masks", [128, LEVELS, 128], u16)
        mask2 = sb("mask2", [128, 128], f16)
        expo_eps = sb("expo_eps", [128, 5, NC])
        wb = sb("wb", [128, 2, KT * WCOL], f32r)
        xb = sb("xb", [128, 2, KT * S], f32r)
        small = [sb(f"small{p}", [128, NC, KINDS, R]) for p in range(2)]
        cws = [sb(f"cws{p}", [128, 4 * TAPS]) for p in range(2)]
        lrow = sb("lrow", [6, R, NC, C], bf16)
        rrow = sb("rrow", [6, R, NC, C], bf16)
        conv = [sb(f"conv{c}", [128, S]) for c in range(4)]
        ssq = sb("ssq", [128, 2, NC])
        ssqe = sb("ssqe", [128, 2, NC])
        rn = sb("rn", [128, 2, NC])
        tokn = [sb(f"tokn{c}", [128, NC, D]) for c in range(2)]
        kq = [sb(f"kq{p}", [128, NC, 2, C]) for p in range(2)]
        vt = [sb(f"vt{p}", [128, NC, R, D]) for p in range(2)]
        zs = [sb(f"zs{p}", [128, NC, R, D]) for p in range(2)]
        kw = [sb(f"kw{p}", [128, NC, R, D]) for p in range(2)]
        et = sb("et", [128, NU, C])
        a32 = sb("a32", [128, NU, C])
        a16 = sb("a16", [128, NU, C], f16)
        u16_ = sb("u16", [128, NU, C], f16)
        t16_ = sb("t16", [128, NU, C], f16)
        a_low = sb("a_low", [128, NU, C], bf16)
        pl = [sb(f"pl{l}", [128, NU, C], f16) for l in range(LEVELS)]
        e16 = sb("e16", [128, NU, C], f16)
        u32 = [sb(f"u32{p}", [128, NU, C]) for p in range(2)]
        attn = [sb(f"attn{p}", [128, NU, C]) for p in range(2)]
        st = sb("st", [128, R, D])
        res = sb("res", [128, R, D])
        yb = sb("yb", [128, R, D])
        qe = sb("qe", [128, R, D])
        xo = sb("xo", [128, NC, R, D])
        rs = sb("rs", [128, NU])
        rse = sb("rse", [128, NU])
        rr = sb("rr", [128, NU])
        xt = sb("xt", [128, NU, C])
        pa = [ctx.enter_context(nc.psum_tensor(f"pa{i}", [128, 512], f32)) for i in range(4)]
        pb = [ctx.enter_context(nc.psum_tensor(f"pb{i}", [128, 512], f32)) for i in range(4)]

        w_parts = [wb[:, q, :].rearrange("p (k n) -> p k n", k=KT) for q in range(2)]
        pieces = ([(tokn[k][:, :, :].rearrange("p n c -> p (n c)"), [w[:, k, 0:S] for w in w_parts]) for k in range(KT)]
                  + [(conv[k][:, :], [xb[:, q, k * S:(k + 1) * S] for q in range(2)]) for k in range(KT)]
                  + [(conv[3][:, :].rearrange("p (k n) -> p k n", k=KT), [w[:, :, S:WCOL] for w in w_parts])])

        def unit(n, h):
            return n * R + h

        def convolved(c):
            return 6 * (c // 2) + 5 + c % 2

        def four(bank):
            return bank[:, :].rearrange("p (n c) -> p n c", n=4)

        def group(t, g):
            return t[:, 4 * g:4 * g + 4, :]

        def per_head(x):
            return x[:, :, None, :].broadcast_to([128, 2, R, C])

        consts_in, made, preset = signal("consts_in", 16), signal("made"), signal("preset")
        w_in, x_in, small_ready = signal("w_in", 16 * KT), signal("x_in", 16 * KT), signal("small_ready")
        wz_in = signal("wz_in", 16)
        rows_in, split_high, split_low = signal("rows_in", 32), signal("split_high", 5), signal("split_low", 5)
        proj_mm, tap_first, tapped, silued, z_ready = signal("proj_mm", 6), signal("tap_first", 4), signal("tapped", 12), signal("silued", 4), signal("z_ready", 2)
        turn_mm, squares, eps_in, rnorm, normed = signal("turn_mm", 4), signal("squares", 2), signal("eps_in", 2), signal("rnorm", 2), signal("normed", 2)
        back_mm, kq_ready, vt_ready, kw_ready = signal("back_mm", 2), signal("kq_ready", 2), signal("vt_ready", 2), signal("kw_ready", 2)
        gram_mm, decay_mm, decay_ready, attn_ready, sys_ready, sys_diag, sys_rounded = (
            signal(n, 2) for n in ("gram_mm", "decay_mm", "decay_ready", "attn_ready", "sys_ready", "sys_diag", "sys_rounded"))
        u_first, t_first_mm, p_mm, p_ready, t_mm, u_mm = signal("u_first", 2), signal("t_first_mm", 2), signal("p_mm", 12), signal("p_ready", 12), signal("t_mm", 12), signal("u_mm", 12)
        u_ready = [signal(f"u_ready{g}", LEVELS) for g in range(2)]
        t_ready = [signal(f"t_ready{g}", LEVELS + 1) for g in range(2)]
        low_ready, resid_mm, resid_ready, fix_mm, inv_ready = (signal(n, 2) for n in ("low_ready", "resid_mm", "resid_ready", "fix_mm", "inv_ready"))
        ks_mm, qs_mm, res_ready, y_mm, y_ready, upd_mm, intra_mm, qe_ready, st_ready, o_ready = (
            signal(*a) for a in (("ks_mm", 3), ("qs_mm", 3), ("res_ready", 4), ("y_mm", 4), ("y_ready", 4), ("upd_mm", 3),
                                 ("intra_mm", 4), ("qe_ready", 3), ("st_ready", 3), ("o_ready", 4)))
        gated, o_squares, o_eps, o_rnorm, o_normed, o_turn_mm, xt_ready, out_mm, added = (
            signal(n, 2) for n in ("gated", "o_squares", "o_eps", "o_rnorm", "o_normed", "o_turn_mm", "xt_ready", "out_mm", "added"))
        passed = [signal(f"passed{i}") for i in range(2)]
        block = ctx.enter_context(nc.Block())
        NCONST = 4
        MADE = 5

        @block.sync
        def _(sp):
            sp.dma_start(et[:, 0, :], io["neg"]).then_inc(consts_in.sem, 16)
            sp.dma_start(masks[:, :, :], io["masks"]).then_inc(consts_in.sem, 16)
            sp.dma_start(mask2[:, :], io["mask2"]).then_inc(consts_in.sem, 16)
            sp.dma_start(expo_eps[:, :, :], io["expo_eps"]).then_inc(consts_in.sem, 16)

            def load(a, p):
                w = io["Wqkvz"].rearrange("(k p) (h n) -> h p k n", p=128, h=NK)[ds(a // B, 1)]
                back_mm.wait(sp, a - 1, 2)
                kw_ready.wait(sp, a - 1, 2)
                for k in range(KT):
                    sp.dma_start(tokn[k][:, :, :].rearrange("p n c -> p (n c)"),
                                 w[:, :, k, 0:S].rearrange("a p n -> p (a n)")).then_inc(w_in.sem, 16)
                turn_mm.wait(sp, a - 1, 4)
                sp.dma_start(conv[3][:, :].rearrange("p (k n) -> p k n", k=KT),
                             w[:, :, :, S:WCOL].rearrange("a p k n -> p (a k) n")).then_inc(wz_in.sem, 16)
                for k in range(KT):
                    sp.dma_start(conv[k][:, :], io["xT"][ds(a % B, 1), k].rearrange("a p n -> p (a n)")).then_inc(x_in.sem, 16)
                decay_mm.wait(sp, a - 1, 2)
                sp.dma_start(lrow[3:6], rows_dram[ds(a, 1), 0].rearrange("a q h s -> (a q) h s")
                             .rearrange("q h (n c) -> q h n c", n=NC)).then_inc(rows_in.sem, 16)
                sp.dma_start(rrow[0:3], rows_dram[ds(a, 1), 1].rearrange("a q h s -> (a q) h s")
                             .rearrange("q h (n c) -> q h n c", n=NC)).then_inc(rows_in.sem, 16)
            sp.wait_ge(made.sem, made.at(0, MADE))
            load(0, 0)
            load(1, 1)
            with sp.Fori(1, ITS // 2) as j:
                load(2 * j, 0)
                load(2 * j + 1, 1)

        def late(*names):
            return [("late", *name) for name in names]

        def early(*names):
            return [("early", *name) for name in names]

        def back(*names):
            return [("back", *name) for name in names]
        g0, g1 = 0, 1
        K, Q, V0, V1 = range(4)

        def level(l, *between):
            chain = l < NC
            return (late(("p_mm", l)) + (back(("qs_mm", l)) if l and chain else []) + (back(("y", l), ("y_copy", l)) if chain else [])
                    + (back(("q_part", l)) if l and chain else []) + late(("p", l), ("ut_mm", 2 * l)) + (back(("update_mm", l)) if l < NC - 1 else [])
                    + late(("ut_mm", 2 * l + 1)) + (back(("intra_mm", l)) if chain else []) + sum(between, []) + late(("ut", l))
                    + (back(("state", l), ("ks_mm", l + 1)) if l < NC - 1 else []) + (back(("out", l)) if chain else [])
                    + (back(("residual", l + 1)) if l < NC - 1 else []))
        ORDER = (
            late(("low", g0), ("low", g1)) + early(("split", 0), ("split", 1)) + level(0, early(("decay_mm", g0)))
            + early(("decay", g0)) + level(1, early(("decay_mm", g1))) + back(("gate", g0)) + early(("split", 2), ("split", 3))
            + early(("decay", g1)) + level(2) + early(("small", 0)) + back(("o_square", g0), ("o_rnorm", g0))
            + level(3) + back(("gate", g1)) + early(("split", 4)) + late(("p_mm", 4))
            + early(("project", K)) + late(("p", 4), ("ut_mm", 8), ("ut_mm", 9)) + back(("o_norm", g0)) + early(("tap", K)) + late(("ut", 4))
            + back(("o_turn", g0), ("x_copy", g0)) + late(("p_mm", 5)) + early(("project", Q)) + late(("p", 5), ("ut_mm", 10), ("ut_mm", 11))
            + early(("tap", Q), ("conv", 0)) + late(("ut", 5)) + back(("o_square", g1), ("o_rnorm", g1)) + early(("conv", 1), ("project", V0))
            + late(("resid_mm", g0), ("resid_mm", g1), ("resid", g0), ("resid", g1)) + back(("out_mm", g0)) + early(("conv", 2), ("tap", V0)) + back(("o_norm", g1), ("added", g0))
            + early(("silu", K), ("silu", Q)) + late(("fix_mm", g0), ("fix_mm", g1), ("fix", g0), ("fix", g1)) + early(("project", V1))
            + early(("tap", V1), ("turn", K), ("turn", Q), ("squares", K), ("squares", Q), ("conv", 3), ("project_z", g0), ("project_z", g1))
            + early(("rnorm", K), ("rnorm", Q), ("conv", 4), ("normed", K), ("normed", Q), ("conv", 5)) + back(("o_turn", g1))
            + early(("z", g0), ("z", g1), ("back", K), ("kq", K), ("back", Q), ("kq", Q), ("kw", 0)) + back(("x_copy", g1))
            + early(("gram", g0), ("gram", g1)) + early(("silu", V0), ("silu", V1), ("system", g0), ("diagonal", g0), ("system", g1), ("diagonal", g1))
            + early(("turn", V0), ("turn", V1), ("rounded", g0), ("rounded", g1), ("vt", 0), ("vt", 1), ("attn", g0), ("u_first", g0), ("u_first", g1), ("attn", g1))
            + back(("out_mm", g1)) + early(("t_first", g0), ("t_first", g1)) + back(("added", g1))
        )
        LAST = ITS - 1

        def steps(engine, **parts):
            def step(s, p, streams=("late", "early", "back")):
                at = {"late": (s, p), "early": (s + 1, 1 - p), "back": (s - 1, 1 - p)}
                for stream, stage, n in ORDER:
                    if stream in streams and stage in parts:
                        parts[stage](*at[stream], n)
            step(-1, 1, ("early",))
            step(0, 0, ("late", "early"))
            step(1, 1)
            with engine.Fori(1, ITS // 2 - 1) as j:
                step(2 * j, 0)
                step(2 * j + 1, 1)
            step(LAST - 1, 0)
            step(LAST, 1, ("late", "back"))
            step(LAST + 1, 0, ("back",))

        proj_bank = (pb[0], pb[1], pb[2], pa[0], pa[2], pa[1])
        turn_bank = (pb[0], pb[1], pa[3], pb[2])

        def more(b):
            return not (isinstance(b, int) and b == LAST)

        @block.tensor
        def _(pe):
            pe.wait_ge(made.sem, made.at(0, MADE))

            PASSES = [(k, pw, px) for k in range(KT) for pw, px in ((0, 0), (0, 1), (1, 0))]

            def project(a, p, c):
                if c == K:
                    pe.wait_ge(split_low.sem, split_low.at(a, 4))
                    y_ready.wait(pe, a - 2, NC)
                if c == Q:
                    o_ready.wait(pe, a - 2, NC)
                if c == V0:
                    st_ready.wait(pe, a - 2, NC - 1)
                if c == V1:
                    resid_ready.wait(pe, a - 1, 1)
                for i, (k, pw, px) in enumerate(PASSES):
                    last = nc.tensor.matmul(proj_bank[c][:, :], wb[:, pw, k * WCOL + c * D:k * WCOL + (c + 1) * D],
                                            xb[:, px, k * S:(k + 1) * S], start=(i == 0), stop=(i == len(PASSES) - 1))
                last.then_inc(proj_mm.sem, 1)

            def project_z(a, p, g):
                pe.wait_ge(split_low.sem, split_low.at(a, 5))
                (resid_ready if g == 0 else inv_ready).wait(pe, a - 1, 2 if g == 0 else 1)
                for n in range(2):
                    for i, (k, pw, px) in enumerate(PASSES):
                        at = k * S + (2 * g + n) * C
                        last = nc.tensor.matmul(proj_bank[4 + g][:, n * R * D:(n + 1) * R * D], xb[:, px, at:at + C],
                                                wb[:, pw, k * WCOL + 4 * D:(k + 1) * WCOL],
                                                start=(i == 0), stop=(i == len(PASSES) - 1))
                last.then_inc(proj_mm.sem, 1)

            def turn(a, p, c):
                pe.wait_ge(silued.sem, silued.at(a, c + 1))
                if c == V0:
                    inv_ready.wait(pe, a - 1, 2)
                for n in range(NC):
                    last = nc.tensor.transpose(turn_bank[c][:, n * C:(n + 1) * C], conv[c][:, n * C:(n + 1) * C], ident[:, :])
                last.then_inc(turn_mm.sem, 1)

            def back_turn(a, p, c):
                pe.wait_ge(normed.sem, normed.at(a, c + 1))
                for n in range(NC):
                    last = nc.tensor.transpose(turn_bank[c][:, n * C:(n + 1) * C], tokn[c][:, n, :], ident[:, :])
                last.then_inc(back_mm.sem, 1)

            def gram(a, p, g):
                pe.wait_ge(kq_ready.sem, kq_ready.at(a, 2))
                if g == 0:
                    pe.wait_ge(tapped.sem, tapped.at(a, convolved(V1)))
                else:
                    pe.wait_ge(z_ready.sem, z_ready.at(a, 2))
                for n in range(2):
                    nn = 2 * g + n
                    last = nc.tensor.matmul(pa[g][:, n * 2 * C:(n + 1) * 2 * C], kq[p][:, nn, 0, :],
                                            kq[p][:, nn, :, :], start=True, stop=True)
                last.then_inc(gram_mm.sem, 1)

            def decay_product(a, p, g):
                if g == 0:
                    pe.wait_ge(rows_in.sem, rows_in.at(a, 32))
                    added.wait(pe, a - 3, 2)
                else:
                    pe.wait_ge(decay_ready.sem, decay_ready.at(a, 1))
                nc.tensor.matmul(pb[3][:, :], identb[:, :], neg[:, :, :].rearrange("p u c -> p (u c)"),
                                 start=True, stop=True)
                for n in range(2):
                    for h in range(R):
                        u = n * R + h
                        last = nc.tensor.matmul(pb[3][:, u * C:(u + 1) * C], lrow[:, h, 2 * g + n, :],
                                                rrow[:, h, 2 * g + n, :], start=False, stop=True,
                                                skip_group_check=True)
                last.then_inc(decay_mm.sem, 1)

            def t_first(a, p, g):
                pe.wait_ge(u_first.sem, u_first.at(a, g + 1))
                if g == 0:
                    pe.wait_ge(attn_ready.sem, attn_ready.at(a, 1))
                else:
                    pe.wait_ge(z_ready.sem, z_ready.at(a, 1))
                for u in range(4):
                    last = nc.tensor.transpose(pa[2 * g][:, :].bitcast(f16)[:, u * C:(u + 1) * C],
                                               u16_[:, 4 * g + u, :], ident16[:, :])
                last.then_inc(t_first_mm.sem, 1)

            def p_product(a, p, l):
                for g in range(2):
                    pe.wait_ge(t_ready[g].sem, t_ready[g].at(a, l + 1))
                    if l == 0 and g == 0:
                        pe.wait_ge(attn_ready.sem, attn_ready.at(a, 2))
                    if l == 0 and g == 1:
                        pe.wait_ge(vt_ready.sem, vt_ready.at(a, 1))
                    for u in range(4):
                        last = nc.tensor.matmul(pa[2 * g + 1][:, u * C:(u + 1) * C], a16[:, 4 * g + u, :],
                                                t16_[:, 4 * g + u, :], start=True, stop=True)
                    last.then_inc(p_mm.sem, 1)

            def ut_product(a, p, i):
                l, g = i // 2, i % 2
                pe.wait_ge(p_ready.sem, p_ready.at(a, i + 1))
                if l:
                    pe.wait_ge(u_ready[g].sem, u_ready[g].at(a, l))
                for u in range(4):
                    last = nc.tensor.matmul(pa[2 * g + 1][:, u * C:(u + 1) * C], u16_[:, 4 * g + u, :],
                                            pl[l][:, 4 * g + u, :], start=True, stop=True)
                last.then_inc(t_mm.sem, 1)
                for u in range(4):
                    last = nc.tensor.matmul(pa[2 * g][:, u * C:(u + 1) * C], pl[l][:, 4 * g + u, :], u16_[:, 4 * g + u, :],
                                            start=True, stop=True)
                last.then_inc(u_mm.sem, 1)

            def resid_product(a, p, g):
                pe.wait_ge(t_ready[g].sem, t_ready[g].at(a, LEVELS + 1))
                pe.wait_ge(u_ready[g].sem, u_ready[g].at(a, LEVELS))
                pe.wait_ge(low_ready.sem, low_ready.at(a, g + 1))
                for u in range(4):
                    for part in range(2):
                        last = nc.tensor.matmul(pa[2 * g][:, u * C:(u + 1) * C], (a16, a_low)[part][:, 4 * g + u, :],
                                                t16_[:, 4 * g + u, :], start=(part == 0), stop=(part == 1))
                last.then_inc(resid_mm.sem, 1)

            def fix_product(a, p, g):
                pe.wait_ge(resid_ready.sem, resid_ready.at(a, g + 1))
                for u in range(4):
                    last = nc.tensor.matmul(pa[2 * g + 1][:, u * C:(u + 1) * C], e16[:, 4 * g + u, :],
                                            u16_[:, 4 * g + u, :], start=True, stop=True)
                last.then_inc(fix_mm.sem, 1)

            def keys_state(b, p, n):
                pe.wait_ge(st_ready.sem, st_ready.at(b, n))
                pe.wait_ge(y_ready.sem, y_ready.at(b, n))
                nc.tensor.matmul(pb[0][:, 0:R * D], kq[p][:, n, 0, :], st[:, :, :], start=True, stop=True)\
                    .then_inc(ks_mm.sem, 1)

            def queries_state(b, p, n):
                pe.wait_ge(st_ready.sem, st_ready.at(b, n))
                pe.wait_ge(o_ready.sem, o_ready.at(b, n))
                nc.tensor.matmul(pb[1][:, 0:R * D], kq[p][:, n, 1, :], st[:, :, :], start=True, stop=True)\
                    .then_inc(qs_mm.sem, 1)

            def y(b, p, n):
                pe.wait_ge(res_ready.sem, res_ready.at(b, n + 1))
                if n == 0:
                    pe.wait_ge(inv_ready.sem, inv_ready.at(b, 2))
                    if more(b):
                        kq_ready.wait(pe, b + 1, 1)
                for h in range(R):
                    last = nc.tensor.matmul(pb[0][:, h * D:(h + 1) * D], u32[p][:, unit(n, h), :], res[:, h, :],
                                            start=True, stop=True)
                last.then_inc(y_mm.sem, 1)

            def update_product(b, p, n):
                pe.wait_ge(y_ready.sem, y_ready.at(b, n + 1))
                if n == 0:
                    pe.wait_ge(kw_ready.sem, kw_ready.at(b, 2))
                    if more(b):
                        vt_ready.wait(pe, b + 1, 2)
                else:
                    pe.wait_ge(st_ready.sem, st_ready.at(b, n))
                for h in range(R):
                    last = nc.tensor.matmul(pb[2][:, h * D:(h + 1) * D], kw[p][:, n, h, :], yb[:, h, :],
                                            start=True, stop=True)
                last.then_inc(upd_mm.sem, 1)

            def intra_product(b, p, n):
                pe.wait_ge(y_ready.sem, y_ready.at(b, n + 1))
                if n == 0:
                    pe.wait_ge(attn_ready.sem, attn_ready.at(b, 2))
                    if more(b):
                        kq_ready.wait(pe, b + 1, 2)
                else:
                    pe.wait_ge(qe_ready.sem, qe_ready.at(b, n))
                for h in range(R):
                    last = nc.tensor.matmul(pb[1][:, h * D:(h + 1) * D], attn[p][:, unit(n, h), :], yb[:, h, :],
                                            start=True, stop=True)
                last.then_inc(intra_mm.sem, 1)

            def o_turn(b, p, g):
                pe.wait_ge(o_normed.sem, o_normed.at(b, g + 1))
                if g:
                    pe.wait_ge(added.sem, added.at(b, 1))
                elif not isinstance(b, int) or b + 2 <= LAST:
                    decay_ready.wait(pe, b + 2, 2)
                else:
                    added.wait(pe, b - 1, 2)
                for u in range(4):
                    last = nc.tensor.transpose(pb[3][:, u * C:(u + 1) * C], xo[:, 2 * g + u // R, u % R, :], ident[:, :])
                last.then_inc(o_turn_mm.sem, 1)

            def out_product(b, p, g):
                pe.wait_ge(xt_ready.sem, xt_ready.at(b, g + 1))
                for i in range(2):
                    for h in range(R):
                        last = nc.tensor.matmul(pb[3][:, i * H:(i + 1) * H], xt[:, unit(2 * g + i, h), :],
                                                wout[:, ds((b // B) * R + h, 1), :].rearrange("p a n -> p (a n)"),
                                                start=(h == 0), stop=(h == R - 1))
                last.then_inc(out_mm.sem, 1)
            steps(pe, project=project, project_z=project_z, turn=turn, back=back_turn, gram=gram, decay_mm=decay_product,
                  t_first=t_first, p_mm=p_product, ut_mm=ut_product, resid_mm=resid_product, fix_mm=fix_product,
                  ks_mm=keys_state, qs_mm=queries_state, y=y, update_mm=update_product, intra_mm=intra_product, o_turn=o_turn,
                  out_mm=out_product)

        @block.scalar
        def _(act):
            act.wait_ge(made.sem, made.at(0, MADE))

            def tap(a, p, c):
                if c == K:
                    act.wait_ge(small_ready.sem, small_ready.at(a, 1))
                if c == V1:
                    act.wait_ge(split_low.sem, split_low.at(a, 5))
                act.wait_ge(proj_mm.sem, proj_mm.at(a, c + 1))
                turn_mm.wait(act, a - 1, c + 1)
                nc.scalar.activation(conv[c][:, :], proj_bank[c][:, :], ACT.Copy,
                                     scale=cws[p][:, c * TAPS + 3:c * TAPS + 4]).then_inc(tap_first.sem, 1)

            def silu(a, p, c):
                act.wait_ge(tapped.sem, tapped.at(a, convolved(c)))
                nc.scalar.activation(conv[c][:, :], conv[c][:, :], ACT.Silu).then_inc(silued.sem, 1)

            def z(a, p, g):
                act.wait_ge(proj_mm.sem, proj_mm.at(a, 5 + g))
                gated.wait(act, a - 2, 2)
                nc.scalar.activation(zs[p][:, 2 * g:2 * g + 2, :, :].rearrange("p n h c -> p (n h c)"),
                                     proj_bank[4 + g][:, :], ACT.Silu).then_inc(z_ready.sem, 1)

            def norm_squares(a, p, c):
                if c == K:
                    kw_ready.wait(act, a - 1, 2)
                back_mm.wait(act, a - 1, c + 1)
                act.wait_ge(turn_mm.sem, turn_mm.at(a, c + 1))
                for n in range(NC):
                    last = nc.scalar.activation(tokn[c][:, n, :], turn_bank[c][:, n * C:(n + 1) * C], ACT.Square,
                                                scale=1.0 if c == K else float(D) ** 0.5, accum_out=ssq[:, c, n:n + 1])
                last.then_inc(squares.sem, 1)

            def values(a, p, h):
                act.wait_ge(turn_mm.sem, turn_mm.at(a, h + 3))
                res_ready.wait(act, a - 2, NC)
                nc.scalar.activation(vt[p][:, :, h, :], four(turn_bank[V0 + h]), ACT.Copy).then_inc(vt_ready.sem, 1)

            def keys_queries(a, p, c):
                act.wait_ge(back_mm.sem, back_mm.at(a, c + 1))
                qs_mm.wait(act, a - 2, 3)
                nc.scalar.activation(kq[p][:, :, c, :], four(turn_bank[c]), ACT.Copy).then_inc(kq_ready.sem, 1)

            def decay(a, p, g):
                act.wait_ge(decay_mm.sem, decay_mm.at(a, g + 1))
                attn_ready.wait(act, a - 1, 2)
                nc.scalar.activation(group(et, g), four(pb[3]), ACT.Exp).then_inc(decay_ready.sem, 1)

            def rounded(a, p, g):
                act.wait_ge(sys_diag.sem, sys_diag.at(a, g + 1))
                nc.scalar.activation(group(a16, g), group(a32, g), ACT.Copy).then_inc(sys_rounded.sem, 1)

            def t_first(a, p, g):
                if g == 1:
                    act.wait_ge(t_first_mm.sem, t_first_mm.at(a, 2))
                    nc.scalar.activation(group(t16_, 1), pa[2][:, :].bitcast(f16)[:, 0:512].rearrange("p (u c) -> p u c", u=4),
                                         ACT.Copy).then_inc(t_ready[1].sem, 1)

            def ut(a, p, l):
                for g in range(2):
                    if g == 1:
                        act.wait_ge(t_mm.sem, t_mm.at(a, 2 * l + 2))
                        nc.scalar.activation(group(t16_, g), four(pa[2 * g + 1]), ACT.Copy)\
                            .then_inc(t_ready[g].sem, 1)
                    act.wait_ge(u_mm.sem, u_mm.at(a, 2 * l + g + 1))
                    nc.scalar.activation(group(u16_, g), four(pa[2 * g]), ACT.Copy).then_inc(u_ready[g].sem, 1)

            def y_copy(b, p, n):
                act.wait_ge(y_mm.sem, y_mm.at(b, n + 1))
                if n:
                    act.wait_ge(intra_mm.sem, intra_mm.at(b, n))
                else:
                    intra_mm.wait(act, b - 1, NC)
                nc.scalar.activation(yb[:, :, :], pb[0][:, 0:R * D].rearrange("p (h d) -> p h d", h=R), ACT.Copy)\
                    .then_inc(y_ready.sem, 1)

            def q_part(b, p, n):
                act.wait_ge(qs_mm.sem, qs_mm.at(b, n))
                act.wait_ge(o_ready.sem, o_ready.at(b, n))
                for h in range(R):
                    last = nc.scalar.activation(qe[:, h, :], pb[1][:, h * D:(h + 1) * D], ACT.Copy,
                                                scale=small[p][:, n, 0, h:h + 1])
                last.then_inc(qe_ready.sem, 1)

            def o_square(b, p, g):
                out_mm.wait(act, b - 1, g + 1)
                act.wait_ge(gated.sem, gated.at(b, g + 1))
                for u in range(4):
                    last = nc.scalar.activation(xt[:, 4 * g + u, :], xo[:, 2 * g + u // R, u % R, :], ACT.Square,
                                                scale=float(D) ** -0.5, accum_out=rs[:, 4 * g + u:4 * g + u + 1])
                last.then_inc(o_squares.sem, 1)

            def x_copy(b, p, g):
                act.wait_ge(o_turn_mm.sem, o_turn_mm.at(b, g + 1))
                nc.scalar.activation(group(xt, g), four(pb[3]), ACT.Copy).then_inc(xt_ready.sem, 1)
            steps(act, tap=tap, silu=silu, z=z, squares=norm_squares, vt=values, kq=keys_queries, decay=decay,
                  rounded=rounded, t_first=t_first, ut=ut, y_copy=y_copy, q_part=q_part, o_square=o_square, x_copy=x_copy)

        @block.vector
        def _(ve):
            nc.vector.memset(lrow[:, :, :, :], 1.0)
            nc.vector.memset(rrow[:, :, :, :], 1.0).then_inc(made.sem, 1)
            nc.vector.tensor_copy(ident16[:, :], ident[:, :]).then_inc(made.sem, 1)
            nc.vector.tensor_copy(identb[:, :], ident[:, :]).then_inc(made.sem, 1)
            nc.vector.tensor_scalar(ident_esc[:, :], ident[:, :], ESC, None, ALU.mult).then_inc(made.sem, 1)
            ve.wait_ge(consts_in.sem, consts_in.at(0, 16 * NCONST))
            nc.vector.tensor_copy(neg[:, :, :], et[:, 0:1, :].broadcast_to([128, 4, C])).then_inc(made.sem, 1)
            ve.wait_ge(made.sem, made.at(0, MADE))
            ve.wait_ge(preset.sem, preset.at(0, LEVELS))

            def convolve(a, p, i):
                part, back = i // 3, i % 3 + 1
                for c in (2 * part, 2 * part + 1):
                    if back == 1:
                        ve.wait_ge(tap_first.sem, tap_first.at(a, c + 1))
                    else:
                        ve.wait_ge(tapped.sem, tapped.at(a, 6 * part + 2 * (back - 2) + (c % 2) + 1))
                    nc.vector.scalar_tensor_tensor(
                        out=conv[c][:, back:S], in0=proj_bank[c][:, 0:S - back],
                        scalar=cws[p][:, c * TAPS + 3 - back:c * TAPS + 4 - back], in1=conv[c][:, back:S],
                        op0=ALU.mult, op1=ALU.add).then_inc(tapped.sem, 1)

            def norm(a, p, c):
                ve.wait_ge(rnorm.sem, rnorm.at(a, c + 1))
                if c == K:
                    kw_ready.wait(ve, a - 1, 2)
                nc.vector.tensor_tensor(tokn[c][:, :, :], four(turn_bank[c]),
                                        rn[:, c, :, None].broadcast_to([128, NC, C]), ALU.mult).then_inc(normed.sem, 1)

            def by_decay(out, g, which):
                grams = pa[g][:, :].rearrange("p (n w c) -> p n w c", n=2, w=2)
                return nc.vector.tensor_tensor(group(out, g).rearrange("p (n h) c -> p n h c", h=R), per_head(grams[:, :, which, :]),
                                               group(et, g).rearrange("p (n h) c -> p n h c", h=R), ALU.mult)

            def system(a, p, g):
                ve.wait_ge(decay_ready.sem, decay_ready.at(a, g + 1))
                ve.wait_ge(gram_mm.sem, gram_mm.at(a, g + 1))
                by_decay(a32, g, 0).then_inc(sys_ready.sem, 1)

            def attention(a, p, g):
                intra_mm.wait(ve, a - 2, NC)
                by_decay(attn[p], g, 1).then_inc(attn_ready.sem, 1)

            def first(a, p, g):
                ve.wait_ge(sys_rounded.sem, sys_rounded.at(a, g + 1))
                nc.vector.tensor_tensor(group(u16_, g), group(a16, g),
                                        mask2[:, None, :].broadcast_to([128, 4, C]), ALU.mult).then_inc(u_first.sem, 1)

            def t_first(a, p, g):
                if g == 0:
                    ve.wait_ge(t_first_mm.sem, t_first_mm.at(a, 1))
                    nc.vector.tensor_copy(group(t16_, 0), pa[0][:, :].bitcast(f16)[:, 0:512].rearrange("p (u c) -> p u c", u=4))\
                        .then_inc(t_ready[0].sem, 1)

            def factor(a, p, l):
                for g in range(2):
                    ve.wait_ge(p_mm.sem, p_mm.at(a, 2 * l + g + 1))
                    ve.sem_inc(passed[0].sem, 1)
                    nc.vector.copy_predicated(group(pl[l], g), masks[:, l:l + 1, :].broadcast_to([128, 4, C]),
                                              four(pa[2 * g + 1])).then_inc(p_ready.sem, 1)

            def ut(a, p, l):
                ve.wait_ge(t_mm.sem, t_mm.at(a, 2 * l + 1))
                nc.vector.tensor_copy(group(t16_, 0), four(pa[1])).then_inc(t_ready[0].sem, 1)

            def resid(a, p, g):
                ve.wait_ge(resid_mm.sem, resid_mm.at(a, g + 1))
                nc.vector.scalar_tensor_tensor(out=group(e16, g), in0=four(pa[2 * g]), scalar=ESC,
                                               in1=ident_esc[:, None, :].broadcast_to([128, 4, C]),
                                               op0=ALU.mult, op1=ALU.add).then_inc(resid_ready.sem, 1)

            def fix(a, p, g):
                ve.wait_ge(fix_mm.sem, fix_mm.at(a, g + 1))
                y_mm.wait(ve, a - 2, NC)
                nc.vector.scalar_tensor_tensor(out=group(u32[p], g), in0=four(pa[2 * g + 1]), scalar=1.0 / ESC,
                                               in1=group(u16_, g), op0=ALU.mult, op1=ALU.add).then_inc(inv_ready.sem, 1)

            def residual(b, p, n):
                if n == 0:
                    ve.wait_ge(vt_ready.sem, vt_ready.at(b, 2))
                    y_mm.wait(ve, b - 1, NC)
                    nc.vector.tensor_scalar(res[:, :, :], vt[p][:, 0, :, :], -1.0, None, ALU.mult).then_inc(res_ready.sem, 1)
                    return
                ve.wait_ge(ks_mm.sem, ks_mm.at(b, n))
                for h in range(R):
                    last = nc.vector.scalar_tensor_tensor(out=res[:, h, :], in0=pb[0][:, h * D:(h + 1) * D],
                                                          scalar=small[p][:, n, 0, h:h + 1], in1=vt[p][:, n, h, :],
                                                          op0=ALU.mult, op1=ALU.subtract)
                last.then_inc(res_ready.sem, 1)

            def y(b, p, n):
                if n == 0:
                    residual(b, p, 0)

            def state(b, p, n):
                ve.wait_ge(upd_mm.sem, upd_mm.at(b, n + 1))
                if n == 0:
                    nc.vector.tensor_copy(st[:, :, :].rearrange("p h d -> p (h d)"), pb[2][:, 0:R * D]).then_inc(st_ready.sem, 1)
                else:
                    ve.wait_ge(st_ready.sem, st_ready.at(b, n))
                    for h in range(R):
                        last = nc.vector.scalar_tensor_tensor(out=st[:, h, :], in0=st[:, h, :],
                                                              scalar=small[p][:, n, 2, h:h + 1],
                                                              in1=pb[2][:, h * D:(h + 1) * D],
                                                              op0=ALU.mult, op1=ALU.add)
                    last.then_inc(st_ready.sem, 1)

            def output(b, p, n):
                ve.wait_ge(intra_mm.sem, intra_mm.at(b, n + 1))
                if n == 0:
                    o_turn_mm.wait(ve, b - 1, 2)
                    nc.vector.tensor_copy(xo[:, 0, :, :].rearrange("p h d -> p (h d)"), pb[1][:, 0:R * D]).then_inc(o_ready.sem, 1)
                else:
                    ve.wait_ge(qe_ready.sem, qe_ready.at(b, n))
                    nc.vector.tensor_tensor(xo[:, n, :, :], qe[:, :, :], pb[1][:, 0:R * D].rearrange("p (h d) -> p h d", h=R),
                                            ALU.add).then_inc(o_ready.sem, 1)

            def o_norm(b, p, g):
                ve.wait_ge(o_rnorm.sem, o_rnorm.at(b, g + 1))
                x = xo[:, 2 * g:2 * g + 2, :, :].rearrange("p n h d -> p (n h) d")
                nc.vector.tensor_tensor(x, x, rr[:, 4 * g:4 * g + 4, None].broadcast_to([128, 4, D]), ALU.mult)\
                    .then_inc(o_normed.sem, 1)

            def add(b, p, g):
                ve.wait_ge(out_mm.sem, out_mm.at(b, g + 1))
                y = yacc[:, ds((b % B) * NC + 2 * g, 2), :]
                added.wait(ve, b - 1, 2)
                nc.vector.tensor_tensor(y, y, pb[3][:, :].rearrange("p (n h) -> p n h", n=2), ALU.add)\
                    .then_inc(added.sem, 1)
            steps(ve, conv=convolve, normed=norm, system=system, attn=attention, u_first=first, t_first=t_first, p=factor,
                  ut=ut, resid=resid, fix=fix, residual=residual, y=y, state=state, out=output, o_norm=o_norm, added=add)

        @block.gpsimd
        def _(pool):
            pool.wait_ge(made.sem, made.at(0, 1))
            for q in range(LEVELS):
                nc.gpsimd.tensor_copy(pl[q][:, :, :], ident[:, None, :].broadcast_to([128, NU, C])).then_inc(preset.sem, 1)

            def factors(a, p, _):
                qe_ready.wait(pool, a - 2, 3)
                st_ready.wait(pool, a - 2, 3)
                res_ready.wait(pool, a - 2, NC)
                pool.sem_inc(passed[1].sem, 1)
                nc.gpsimd.tensor_copy(cws[p][:, :], cw[:, ds(a // B, 1), :].rearrange("p a n -> p (a n)"))
                nc.gpsimd.tensor_copy(small[p][:, :, :, :].rearrange("p n q h -> p (n q h)"),
                                      vec[:, ds(a, 1), :].rearrange("p a n -> p (a n)")).then_inc(small_ready.sem, 1)

            def rnorms(a, p, c):
                pool.wait_ge(squares.sem, squares.at(a, c + 1))
                nc.gpsimd.tensor_tensor(ssqe[:, c, :], ssq[:, c, :], expo_eps[:, 1 + c, :], ALU.add)\
                    .then_inc(eps_in.sem, 1)
                pool.wait_ge(eps_in.sem, eps_in.at(a, c + 1))
                nc.gpsimd.tensor_tensor(rn[:, c, :], ssqe[:, c, :], expo_eps[:, 0, :], ALU.pow).then_inc(rnorm.sem, 1)

            def weighted_keys(a, p, _):
                pool.wait_ge(normed.sem, normed.at(a, 1))
                upd_mm.wait(pool, a - 2, 3)
                pool.wait_ge(small_ready.sem, small_ready.at(a, 1))
                for h in range(R):
                    nc.gpsimd.tensor_tensor(kw[p][:, :, h, :], tokn[K][:, :, :],
                                            small[p][:, :, 1, h:h + 1].broadcast_to([128, NC, D]), ALU.mult)\
                        .then_inc(kw_ready.sem, 1)

            def diagonal(a, p, g):
                pool.wait_ge(sys_ready.sem, sys_ready.at(a, g + 1))
                pool.sem_inc(passed[1].sem, 1)
                nc.gpsimd.affine_select(out=group(a32, g), in_=group(a32, g), compare_op=ALU.not_equal, fill=1.0,
                                        base=0, pattern=[[0, 4], [-1, C]], channel_multiplier=1).then_inc(sys_diag.sem, 1)

            def low_part(a, p, g):
                pool.wait_ge(sys_rounded.sem, sys_rounded.at(a, g + 1))
                resid_mm.wait(pool, a - 1, 2)
                nc.gpsimd.tensor_tensor(group(a_low, g), group(a32, g), group(a16, g), ALU.subtract).then_inc(low_ready.sem, 1)

            def split(a, p, n):
                proj_mm.wait(pool, a - 1, 6)
                arrived = (w_in, w_in, x_in, x_in, wz_in)[n]
                pool.wait_ge(arrived.sem, arrived.at(a, arrived.per))
                pool.sem_inc(passed[1].sem, 1)
                raw, parts = pieces[n]
                nc.gpsimd.tensor_copy(parts[0], raw).then_inc(split_high.sem, 1)
                pool.wait_ge(split_high.sem, split_high.at(a, n + 1))
                nc.gpsimd.tensor_tensor(parts[1], raw, parts[0], ALU.subtract).then_inc(split_low.sem, 1)

            def gate(b, p, g):
                x = xo[:, 2 * g:2 * g + 2, :, :]
                pool.wait_ge(z_ready.sem, z_ready.at(b, g + 1))
                pool.wait_ge(o_ready.sem, o_ready.at(b, 2 * g + 2))
                nc.gpsimd.tensor_tensor(x, x, zs[p][:, 2 * g:2 * g + 2, :, :], ALU.mult).then_inc(gated.sem, 1)

            def o_rnorms(b, p, g):
                pool.wait_ge(o_squares.sem, o_squares.at(b, g + 1))
                nc.gpsimd.tensor_tensor(rse[:, 4 * g:4 * g + 4], rs[:, 4 * g:4 * g + 4], expo_eps[:, 3, :], ALU.add)\
                    .then_inc(o_eps.sem, 1)
                pool.wait_ge(o_eps.sem, o_eps.at(b, g + 1))
                nc.gpsimd.tensor_tensor(rr[:, 4 * g:4 * g + 4], rse[:, 4 * g:4 * g + 4], expo_eps[:, 0, :], ALU.pow)\
                    .then_inc(o_rnorm.sem, 1)
            steps(pool, split=split, small=factors, rnorm=rnorms, kw=weighted_keys, diagonal=diagonal, low=low_part, gate=gate, o_rnorm=o_rnorms)


def feed_forward(nc, io, m):
    yacc, ident = m["yacc"], m["ident"]
    with ExitStack() as ctx:
        def sb(name, shape, dt=f32):
            return ctx.enter_context(nc.sbuf_tensor(name, shape, dt))

        def signal(name, per=1):
            return Signal(nc, ctx, "f_" + name, per)

        def pair(name, per=1):
            return [signal(f"{name}{w}", per) for w in range(2)]
        wraw = sb("wraw", [128, 3, KT * E])
        wug = sb("wug", [128, 2, KT, E], f32r)
        wdn = sb("wdn", [128, ET, H], f32r)
        low = sb("low", [128, KT * E], bf16)
        ones = sb("fones", [128, 128])
        expo_eps = sb("fexpo_eps", [128, 5, NC])
        asum = sb("asum", [128, 3])
        scale = sb("scale", [128, 3])
        half = sb("half", [128, 3])
        mhalfs = sb("mhalfs", [128, 3])
        sgd = sb("sgd", [128, 1])
        mean = sb("fmean", [128, 2, NC])
        meanm = sb("fmeanm", [128, 2, NC])
        var = sb("fvar", [128, 2, NC])
        vare = sb("fvare", [128, 2, NC])
        rstd = sb("frstd", [128, 2, NC])
        junk = sb("fjunk", [128, 2 * NC, H], bf16)
        centre = [sb(f"fcentre{w}", [128, NC, H]) for w in range(2)]
        xn = [sb(f"fxn{p}", [128, NC, H]) for p in range(2)]
        xnT = [sb(f"fxnT{p}", [128, 2, KT, S], f32r) for p in range(2)]
        hid = [sb(f"fhid{p}", [128, 2, ET, NC, C], f32r) for p in range(2)]
        up = [sb(f"fup{i}", [128, S]) for i in range(2)]
        prod = [sb(f"fprod{i}", [128, S]) for i in range(2)]
        ob = [sb(f"fob{p}", [128, NC, H]) for p in range(2)]
        yo = sb("fyo", [128, NC, H])
        pw = ctx.enter_context(nc.psum_tensor("pw", [128, 512], f32))
        pt = ctx.enter_context(nc.psum_tensor("fpt", [128, 512], f32))
        pu = [ctx.enter_context(nc.psum_tensor(f"pu{i}", [128, 512], f32)) for i in range(2)]
        pv = [ctx.enter_context(nc.psum_tensor(f"pv{i}", [128, 512], f32)) for i in range(2)]
        pd = [ctx.enter_context(nc.psum_tensor(f"pd{i}", [128, 512], f32)) for i in range(2)]
        w_in, made, sums, total_mm, chain, tern = (signal(n) for n in ("w_in", "made", "sums", "total_mm", "chain", "tern"))
        meaned, means, centred, vars_ready, eps_in, rstd_ready, normed = (
            pair(n) for n in ("meaned", "means", "centred", "vars", "eps", "rstd", "normed"))
        turn_mm, turned, turned_low, up_mm, gate_mm, silued, prod_ready, hid_high, hid_low, down_mm, y_ready = (
            signal(*a) for a in (("turn_mm", 2), ("turned", 2), ("turned_low", 2), ("up_mm", ET), ("gate_mm", ET), ("silued", ET),
                                 ("prod", ET), ("hid_high", ET), ("hid_low", ET), ("down_mm", NC), ("y", 2)))
        stored = pair("stored", 16)
        block = ctx.enter_context(nc.Block())
        NTERN = 3
        LAST = B - 1

        def pre(*names):
            return [("pre", *name) for name in names]

        def mid(*names):
            return [("mid", *name) for name in names]

        def post(*names):
            return [("post", *name) for name in names]
        beside = (
            pre(("mean", 0), ("squares", 0)) + post(("down", 0)),
            post(("down", 1), ("y", 0)) + pre(("rstd", 0)),
            post(("down", 2)),
            post(("down", 3), ("y", 1)) + pre(("norm", 0)) + post(("mean", 1)),
            post(("squares", 1), ("rstd", 1)),
            pre(("turn", 0), ("turned", 0), ("turned_low", 0)) + post(("norm", 1), ("store", 0)),
            pre(("turn", 1), ("turned", 1), ("turned_low", 1)),
            [],
        )
        ORDER = []
        for t in range(ET):
            ORDER += mid(("up", t), ("gate", t), ("silu", t), ("prod", t)) + (mid(("high", t - 1), ("low", t - 1)) if t else []) + list(beside[t])
        ORDER += mid(("high", ET - 1), ("low", ET - 1))

        def steps(engine, **parts):
            def step(s, p, streams=("pre", "mid", "post")):
                at = {"mid": (s, p), "pre": (s + 1, 1 - p), "post": (s - 1, 1 - p)}
                for stream, stage, n in ORDER:
                    if stream in streams and stage in parts:
                        parts[stage](*at[stream], n)
            step(-1, 1, ("pre",))
            step(0, 0, ("pre", "mid"))
            step(1, 1)
            step(2, 0)
            with engine.Fori(2, B // 2) as j:
                step(2 * j - 1, 1)
                step(2 * j, 0)
            step(LAST, 1, ("mid", "post"))
            step(LAST + 1, 0, ("post",))

        def two_tiles_ago(sig, engine, i, t):
            if t >= 2:
                engine.wait_ge(sig.sem, sig.at(i, t - 1))
            else:
                sig.wait(engine, i - 1, ET + t - 1)

        @block.sync
        def _(sp):
            sp.dma_start(wraw[:, 0, :].rearrange("p (k n) -> p k n", k=KT), io["WupT"].rearrange("(k p) n -> p k n", p=128)).then_inc(w_in.sem, 16)
            sp.dma_start(wraw[:, 1, :].rearrange("p (k n) -> p k n", k=KT), io["WgateT"].rearrange("(k p) n -> p k n", p=128)).then_inc(w_in.sem, 16)
            sp.dma_start(wraw[:, 2, :].rearrange("p (k n) -> p k n", k=ET), io["WdownT"].rearrange("(k p) n -> p k n", p=128)).then_inc(w_in.sem, 16)
            sp.dma_start(expo_eps[:, :, :], io["expo_eps"]).then_inc(w_in.sem, 16)

            def store(i, p, _):
                sp.wait_ge(normed[1].sem, normed[1].at(i, 1))
                sp.dma_start(io["out"].rearrange("(i n p) h -> i p n h", n=NC, p=128)[ds(i, 1)]
                             .rearrange("i p n h -> p (i n) h"), ob[p][:, :, :]).then_inc(stored[p].sem, 16)
            steps(sp, store=store)
            for p in range(2):
                stored[p].wait(sp, B // 2 - 1, 16)

        @block.tensor
        def _(pe):
            pe.wait_ge(made.sem, made.at(0, 1))
            pe.wait_ge(sums.sem, sums.at(0, 3))
            nc.tensor.matmul(pw[:, 0:3], ones[:, :], asum[:, :], start=True, stop=True).then_inc(total_mm.sem, 1)

            def turn(i, p, k):
                if k == 0:
                    pe.wait_ge(normed[0].sem, normed[0].at(i, 1))
                    turned_low.wait(pe, i - 1, KT)
                else:
                    pe.wait_ge(turned_low.sem, turned_low.at(i, k))
                for n in range(NC):
                    last = nc.tensor.transpose(pt[:, n * C:(n + 1) * C], xn[p][:, n, k * 128:(k + 1) * 128], ident[:, :])
                last.then_inc(turn_mm.sem, 1)

            def project(bank, which, t, p):
                for k in range(KT):
                    for part in range(2):
                        last = nc.tensor.matmul(bank[:, :], wug[:, which, k, t * 128:(t + 1) * 128], xnT[p][:, part, k, :],
                                                start=(k == 0 and part == 0), stop=(k == KT - 1 and part == 1))
                return last

            def up_product(i, p, t):
                if t == 0:
                    pe.wait_ge(tern.sem, tern.at(0, NTERN))
                    pe.wait_ge(turned_low.sem, turned_low.at(i, KT))
                two_tiles_ago(silued, pe, i, t)
                project(pu[t % 2], 0, t, p).then_inc(up_mm.sem, 1)

            def gate_product(i, p, t):
                two_tiles_ago(prod_ready, pe, i, t)
                project(pv[t % 2], 1, t, p).then_inc(gate_mm.sem, 1)

            def down_product(i, p, n):
                if n == 0:
                    pe.wait_ge(hid_low.sem, hid_low.at(i, ET))
                if n % 2 == 0:
                    y_ready.wait(pe, i - 1, n // 2 + 1)
                for t in range(ET):
                    for part in range(2):
                        last = nc.tensor.matmul(pd[n // 2][:, n % 2 * H:(n % 2 + 1) * H], hid[p][:, part, t, n, :], wdn[:, t, :],
                                                start=(t == 0 and part == 0), stop=(t == ET - 1 and part == 1))
                last.then_inc(down_mm.sem, 1)
            steps(pe, turn=turn, up=up_product, gate=gate_product, down=down_product)

        @block.scalar
        def _(act):
            def squares(i, p, w):
                act.wait_ge(centred[w].sem, centred[w].at(i, 1))
                for n in range(NC):
                    last = nc.scalar.activation(junk[:, w * NC + n, :], centre[w][:, n, :], ACT.Square, scale=float(H) ** -0.5,
                                                accum_out=var[:, w, n:n + 1])
                last.then_inc(vars_ready[w].sem, 1)

            def turned_high(i, p, k):
                act.wait_ge(turn_mm.sem, turn_mm.at(i, k + 1))
                up_mm.wait(act, i - 2, ET)
                gate_mm.wait(act, i - 2, ET)
                nc.scalar.activation(xnT[p][:, 0, k, :], pt[:, :], ACT.Copy).then_inc(turned.sem, 1)

            def silu(i, p, t):
                if t == 0:
                    act.wait_ge(tern.sem, tern.at(0, 1))
                act.wait_ge(up_mm.sem, up_mm.at(i, t + 1))
                two_tiles_ago(prod_ready, act, i, t)
                nc.scalar.activation(up[t % 2][:, :], pu[t % 2][:, :], ACT.Silu, scale=scale[:, 0:1]).then_inc(silued.sem, 1)

            def high(i, p, t):
                act.wait_ge(prod_ready.sem, prod_ready.at(i, t + 1))
                down_mm.wait(act, i - 2, NC)
                nc.scalar.activation(hid[p][:, 0, t, :, :].rearrange("p n c -> p (n c)"), prod[t % 2][:, :], ACT.Copy)\
                    .then_inc(hid_high.sem, 1)
            steps(act, squares=squares, turned=turned_high, silu=silu, high=high)

        @block.gpsimd
        def _(pool):
            pool.wait_ge(w_in.sem, w_in.at(0, 64))

            def deviation(i, p, w):
                pool.wait_ge(vars_ready[w].sem, vars_ready[w].at(i, 1))
                nc.gpsimd.tensor_tensor(vare[:, w, :], var[:, w, :], expo_eps[:, 4, :], ALU.add).then_inc(eps_in[w].sem, 1)
                pool.wait_ge(eps_in[w].sem, eps_in[w].at(i, 1))
                nc.gpsimd.tensor_tensor(rstd[:, w, :], vare[:, w, :], expo_eps[:, 0, :], ALU.pow).then_inc(rstd_ready[w].sem, 1)

            def low_part(i, p, t):
                pool.wait_ge(hid_high.sem, hid_high.at(i, t + 1))
                down_mm.wait(pool, i - 2, NC)
                nc.gpsimd.tensor_tensor(hid[p][:, 1, t, :, :].rearrange("p n c -> p (n c)"), prod[t % 2][:, :],
                                        hid[p][:, 0, t, :, :].rearrange("p n c -> p (n c)"), ALU.subtract).then_inc(hid_low.sem, 1)
            steps(pool, rstd=deviation, low=low_part)

        @block.vector
        def _(ve):
            links = [0]

            def link(ins):
                links[0] += 1
                ins.then_inc(chain.sem, 1)
                ve.wait_ge(chain.sem, links[0])
            nc.vector.memset(ones[:, :], 1.0).then_inc(made.sem, 1)

            def mean_out(i, p, w):
                src = yacc[:, ds(i * NC, NC), :] if w == 0 else yo[:, :, :]
                if w == 1:
                    ve.wait_ge(y_ready.sem, y_ready.at(i, 2))
                nc.vector.tensor_reduce(mean[:, w, :], src, AX.X, ALU.add).then_inc(meaned[w].sem, 1)
                ve.wait_ge(meaned[w].sem, meaned[w].at(i, 1))
                nc.vector.tensor_scalar(meanm[:, w, :], mean[:, w, :], 1.0 / H, None, ALU.mult).then_inc(means[w].sem, 1)
                ve.wait_ge(means[w].sem, means[w].at(i, 1))
                normed[w].wait(ve, i - 1, 1)
                nc.vector.tensor_tensor(centre[w][:, :, :], src, meanm[:, w, :, None].broadcast_to([128, NC, H]), ALU.subtract)\
                    .then_inc(centred[w].sem, 1)

            def norm(i, p, w):
                ve.wait_ge(rstd_ready[w].sem, rstd_ready[w].at(i, 1))
                if w == 0:
                    turn_mm.wait(ve, i - 2, KT)
                    y_ready.wait(ve, i - 2, 2)
                else:
                    stored[p].wait(ve, i // 2 - 1, 16)
                nc.vector.tensor_tensor((xn if w == 0 else ob)[p][:, :, :], centre[w][:, :, :],
                                        rstd[:, w, :, None].broadcast_to([128, NC, H]), ALU.mult).then_inc(normed[w].sem, 1)

            def turned_low_part(i, p, k):
                ve.wait_ge(turned.sem, turned.at(i, k + 1))
                nc.vector.tensor_tensor(xnT[p][:, 1, k, :], pt[:, :], xnT[p][:, 0, k, :], ALU.subtract).then_inc(turned_low.sem, 1)

            def product(i, p, t):
                ve.wait_ge(gate_mm.sem, gate_mm.at(i, t + 1))
                ve.wait_ge(silued.sem, silued.at(i, t + 1))
                two_tiles_ago(hid_low, ve, i, t)
                nc.vector.tensor_tensor(prod[t % 2][:, :], up[t % 2][:, :], pv[t % 2][:, :], ALU.mult).then_inc(prod_ready.sem, 1)

            def y(i, p, g):
                ve.wait_ge(down_mm.sem, down_mm.at(i, 2 * g + 2))
                centred[1].wait(ve, i - 1, 1)
                ve.wait_ge(normed[0].sem, normed[0].at(i, 1))
                nc.vector.scalar_tensor_tensor(out=yo[:, 2 * g:2 * g + 2, :], in0=pd[g][:, :].rearrange("p (n h) -> p n h", n=2),
                                               scalar=sgd[:, 0:1], in1=xn[p][:, 2 * g:2 * g + 2, :], op0=ALU.mult, op1=ALU.add)\
                    .then_inc(y_ready.sem, 1)
            ve.wait_ge(w_in.sem, w_in.at(0, 64))
            for q in range(3):
                nc.vector.tensor_reduce(asum[:, q:q + 1], wraw[:, q, :], AX.X, ALU.add, apply_absolute_value=True)\
                    .then_inc(sums.sem, 1)
            ve.wait_ge(total_mm.sem, total_mm.at(0, 1))
            link(nc.vector.tensor_scalar(scale[:, :], pw[:, 0:3], 1.0 / (E * H), TERN_EPS, ALU.mult, ALU.add))
            link(nc.vector.tensor_scalar(half[:, :], scale[:, :], 0.5, None, ALU.mult))
            link(nc.vector.tensor_scalar(mhalfs[:, :], scale[:, :], -0.5, None, ALU.mult))
            link(nc.vector.tensor_tensor(sgd[:, :], scale[:, 1:2], scale[:, 2:3], ALU.mult))
            for q in range(3):
                out = wug[:, q, :, :].rearrange("p k n -> p (k n)") if q < 2 else wdn[:, :, :].rearrange("p t h -> p (t h)")
                link(nc.vector.tensor_scalar(low[:, :], wraw[:, q, :], mhalfs[:, q:q + 1], None, ALU.is_lt))
                nc.vector.scalar_tensor_tensor(out=out, in0=wraw[:, q, :], scalar=half[:, q:q + 1], in1=low[:, :], op0=ALU.is_gt,
                                               op1=ALU.subtract).then_inc(tern.sem, 1)
                ve.wait_ge(tern.sem, tern.at(0, q + 1))
            steps(ve, mean=mean_out, norm=norm, turned_low=turned_low_part, prod=product, y=y)


def constants():
    i = np.arange(128)
    masks = np.zeros((128, LEVELS, 128), np.uint16)
    for l in range(LEVELS):
        s = 2 << l
        same = (i[:, None] // (2 * s)) == (i[None, :] // (2 * s))
        masks[:, l, :] = same & (i[:, None] % (2 * s) >= s) & (i[None, :] % (2 * s) < s)
    mask2 = -np.eye(128) + ((i[:, None] // 2 == i[None, :] // 2) & (i[:, None] < i[None, :]))
    neg = np.where(i[None, :] < i[:, None], -1e30, 0.0)
    return {
        "ident": np.eye(128, dtype=np.float32),
        "triu": (i[:, None] <= i[None, :]).astype(np.float32),
        "neg": neg.astype(np.float32),
        "masks": masks,
        "mask2": mask2.astype(np.float16),
        "expo_eps": np.broadcast_to(np.array([-0.5, EPS, EPS * D, EPS, LN_EPS], np.float32)[None, :, None], (128, 5, NC)),
    }


def kernel(L0_attn_hidden_states, L0_attn_W_qkvz, L0_attn_W_ba, L0_attn_conv_weight, L0_attn_A_log, L0_attn_dt_bias,
           L0_attn_norm_weight, L0_attn_W_out, L0_ffn_W_up, L0_ffn_W_gate, L0_ffn_W_down):
    import concourse.bacc as bacc
    from concourse.bass_utils import run_bass_kernel_spmd
    x = np.asarray(L0_attn_hidden_states)
    w = np.asarray(L0_attn_W_qkvz).reshape(H, NK, WCOL)
    w = np.concatenate([w[..., D:2 * D], w[..., 0:D], w[..., 2 * D:]], -1).reshape(H, NK * WCOL)
    wba = np.asarray(L0_attn_W_ba).reshape(H, NK, 2, R).transpose(0, 2, 1, 3).reshape(H, 2 * NV)
    cwt = np.asarray(L0_attn_conv_weight)
    q, k, v = cwt[:NK * D].reshape(NK, 1, D, TAPS), cwt[NK * D:2 * NK * D].reshape(NK, 1, D, TAPS), cwt[2 * NK * D:].reshape(NK, R, D, TAPS)
    cwt = np.concatenate([k, q, v], 1).transpose(2, 0, 1, 3).reshape(D, NK, 4 * TAPS)
    arrays = {
        "xT": x.transpose(0, 2, 1).reshape(B, KT, 128, S),
        "x_tok": x.reshape(B * S, H),
        "Wqkvz": w, "Wba": wba, "convw": cwt,
        "A_log": L0_attn_A_log, "dt_bias": L0_attn_dt_bias, "norm_weight": L0_attn_norm_weight, "W_out": L0_attn_W_out,
        "WupT": np.asarray(L0_ffn_W_up).T, "WgateT": np.asarray(L0_ffn_W_gate).T, "WdownT": np.asarray(L0_ffn_W_down).T,
    }
    arrays.update(constants())
    arrays = {f"in_{n}": np.ascontiguousarray(a) for n, a in arrays.items()}
    nc = bacc.Bacc("TRN2", target_bir_lowering=False, num_devices=1)
    io = {n[3:]: nc.dram_tensor(n, a.shape, mybir.dt.from_np(a.dtype), kind="ExternalInput").ap() for n, a in arrays.items()}
    io["out"] = nc.dram_tensor("out", (B * S, H), f32, kind="ExternalOutput").ap()
    build(nc, io)
    r = run_bass_kernel_spmd(nc, [arrays], core_ids=[0])
    return r.results[0]["out"].reshape(B, S, H)
```
